# Optimizing a Trainium2 kernel written in Bass

```python
import numpy as np
import jax
import jax.numpy as jnp

def _softmax(x, axis=-1):
    return jax.nn.softmax(x, axis=axis)

def _gelu(x):
    return jax.nn.gelu(x, approximate=True)

def _silu(x):
    return jax.nn.silu(x)

def _sigmoid(x):
    return jax.nn.sigmoid(x)

def _layernorm(x, axis=-1, eps=1e-05):
    m = jnp.mean(x, axis=axis, keepdims=True)
    v = jnp.var(x, axis=axis, keepdims=True)
    return (x - m) / jnp.sqrt(v + eps)

def _scatter_add(tgt, idx, src, axis=0):
    return tgt.at[idx].add(src)

def _segment_sum(src, seg, n):
    return jax.ops.segment_sum(src, seg, n)
kernel_name = 'mk_prb_d2_jaxref_r8_6bb920'

def setup_inputs(seed: int=0):
    np.random.seed(seed)
    _w = jnp.asarray

    def _L0_attn_setup():
        import jax, jax.numpy as jnp
        import numpy as np
        D = 128
        H = 16
        KVH = 4
        HD = D // H
        LAT = 32
        WIN = 32
        B, S = (1, 256)
        BASE_G, BASE_L = (1000000.0, 10000.0)
        EPS = 1e-06

        def rmsnorm(x, w):
            return x * jax.lax.rsqrt(jnp.mean(x * x, axis=-1, keepdims=True) + EPS) * w

        def qk_norm(x):
            return x * jax.lax.rsqrt(jnp.mean(x * x, axis=-1, keepdims=True) + EPS)

        def rope(x, base):
            s, hd = (x.shape[-2], x.shape[-1])
            inv_freq = 1.0 / base ** (jnp.arange(0, hd, 2, dtype=jnp.float32) / hd)
            freqs = jnp.arange(s, dtype=jnp.float32)[:, None] * inv_freq[None, :]
            cos, sin = (jnp.cos(freqs), jnp.sin(freqs))
            xe, xo = (x[..., ::2], x[..., 1::2])
            out = jnp.stack([xe * cos - xo * sin, xe * sin + xo * cos], axis=-1)
            return out.reshape(x.shape)

        def split_heads(x, n_heads):
            b, s, _ = x.shape
            return x.reshape(b, s, n_heads, HD).transpose(0, 2, 1, 3)

        def repeat_kv(x):
            return jnp.repeat(x, H // KVH, axis=1)

        def sdpa(q, k, v, mask):
            scores = jnp.einsum('bhqd,bhkd->bhqk', q, k) / np.sqrt(HD).astype(np.float32)
            scores = jnp.where(mask, scores, jnp.float32(-1e+30))
            probs = jax.nn.softmax(scores, axis=-1)
            return jnp.einsum('bhqk,bhkd->bhqd', probs, v)

        def merge_heads(x):
            b, h, s, hd = x.shape
            return x.transpose(0, 2, 1, 3).reshape(b, s, h * hd)

        def global_latent_attn(x, wq, w_kv_down, w_k_up, w_v_up, wo):
            q = split_heads(x @ wq, H)
            latent = x @ w_kv_down
            k = split_heads(latent @ w_k_up, KVH)
            v = split_heads(latent @ w_v_up, KVH)
            q, k = (rope(q, BASE_G), rope(k, BASE_G))
            q, k = (qk_norm(q), qk_norm(k))
            k, v = (repeat_kv(k), repeat_kv(v))
            i = jnp.arange(x.shape[1])
            causal = i[:, None] >= i[None, :]
            return merge_heads(sdpa(q, k, v, causal)) @ wo

        def local_gqa_attn(x, wq, wk, wv, wo):
            q = split_heads(x @ wq, H)
            k = split_heads(x @ wk, KVH)
            v = split_heads(x @ wv, KVH)
            q, k = (rope(q, BASE_L), rope(k, BASE_L))
            q, k = (qk_norm(q), qk_norm(k))
            k, v = (repeat_kv(k), repeat_kv(v))
            i = jnp.arange(x.shape[1])
            diff = i[:, None] - i[None, :]
            mask = (diff >= 0) & (diff < WIN)
            return merge_heads(sdpa(q, k, v, mask)) @ wo
        key = jax.random.key(seed)
        ks = jax.random.split(key, 12)
        std = 0.02
        return {'hidden': jax.random.normal(ks[0], (B, S, D), dtype=jnp.float32), 'norm1_w': jnp.ones((D,), jnp.float32), 'norm2_w': jnp.ones((D,), jnp.float32), 'g_wq': jax.random.normal(ks[1], (D, H * HD), jnp.float32) * std, 'g_kv_down': jax.random.normal(ks[2], (D, LAT), jnp.float32) * std, 'g_k_up': jax.random.normal(ks[3], (LAT, KVH * HD), jnp.float32) * std, 'g_v_up': jax.random.normal(ks[4], (LAT, KVH * HD), jnp.float32) * std, 'g_wo': jax.random.normal(ks[5], (D, D), jnp.float32) * std, 'l_wq': jax.random.normal(ks[6], (D, H * HD), jnp.float32) * std, 'l_wk': jax.random.normal(ks[7], (D, KVH * HD), jnp.float32) * std, 'l_wv': jax.random.normal(ks[8], (D, KVH * HD), jnp.float32) * std, 'l_wo': jax.random.normal(ks[9], (D, D), jnp.float32) * std}
    _L0_attn_in = _L0_attn_setup()

    def _L0_ffn_setup():
        import jax, jax.numpy as jnp
        import numpy as np
        B, S, DIM = (4, 256, 128)
        E, K, HID = (8, 2, 512)
        key = jax.random.key(seed)
        ks = jax.random.split(key, 8)
        init = lambda k, sh: jax.random.normal(k, sh, jnp.float32) * 0.02
        return {'x': jax.random.normal(ks[0], (B, S, DIM), jnp.float32), 'gate_w': init(ks[1], (DIM, E)), 'gate_b': jnp.zeros((E,), jnp.float32), 'w1': init(ks[2], (E, DIM, HID)), 'b1': jnp.zeros((E, HID), jnp.float32), 'w2': init(ks[3], (E, HID, DIM)), 'b2': jnp.zeros((E, DIM), jnp.float32), 'ws1': init(ks[4], (DIM, HID)), 'bs1': jnp.zeros((HID,), jnp.float32), 'ws2': init(ks[5], (HID, DIM)), 'bs2': jnp.zeros((DIM,), jnp.float32)}
    _L0_ffn_in = _L0_ffn_setup()

    def _L1_attn_setup():
        import jax, jax.numpy as jnp
        import numpy as np

        def _rope_cos_sin(m, d, dtype=jnp.float32):
            i = jnp.arange(d // 2, dtype=dtype)
            theta = jnp.power(jnp.asarray(10000.0, dtype), -2.0 * (i - 1.0) / d)
            pos = jnp.arange(m, dtype=dtype)
            ang = pos[:, None] * theta[None, :]
            return (jnp.cos(ang), jnp.sin(ang))

        def _rotate(t, cos, sin):
            te = t[..., 0::2]
            to = t[..., 1::2]
            re = te * cos + to * sin
            ro = -te * sin + to * cos
            return jnp.stack((re, ro), axis=-1).reshape(t.shape)
        key = jax.random.key(seed)
        k1, k2, k3, k4 = jax.random.split(key, 4)
        b, m, d = (4, 256, 128)
        scale = 1.0 / np.sqrt(d)
        return {'x': jax.random.normal(k1, (b, m, d), dtype=jnp.float32), 'w_q': jax.random.normal(k2, (d, d), dtype=jnp.float32) * scale, 'w_k': jax.random.normal(k3, (d, d), dtype=jnp.float32) * scale, 'w_v': jax.random.normal(k4, (d, d), dtype=jnp.float32) * scale}
    _L1_attn_in = _L1_attn_setup()

    def _L1_ffn_setup():
        import jax, jax.numpy as jnp
        import numpy as np
        B, T = (2, 256)
        D_MODEL, D_HIDDEN = (128, 256)
        N_EXPERTS, TOP_K = (8, 2)
        N_TOKENS = B * T
        CAPACITY = 2 * N_TOKENS * TOP_K // N_EXPERTS
        key = jax.random.key(seed)
        k_x, k_rw, k_w, k_v, k_o = jax.random.split(key, 5)
        x = jax.random.normal(k_x, (B, T, D_MODEL), jnp.float32)
        router_w = jax.random.normal(k_rw, (N_EXPERTS, D_MODEL), jnp.float32) * D_MODEL ** (-0.5)
        router_b = jnp.zeros((N_EXPERTS,), jnp.float32)
        W = jax.random.normal(k_w, (N_EXPERTS, D_MODEL, D_HIDDEN), jnp.float32) * D_MODEL ** (-0.5)
        V = jax.random.normal(k_v, (N_EXPERTS, D_MODEL, D_HIDDEN), jnp.float32) * D_MODEL ** (-0.5)
        W_out = jax.random.normal(k_o, (N_EXPERTS, D_HIDDEN, D_MODEL), jnp.float32) * D_HIDDEN ** (-0.5)
        return {'x': x, 'router_w': router_w, 'router_b': router_b, 'W': W, 'V': V, 'W_out': W_out}
    _L1_ffn_in = _L1_ffn_setup()
    _d = {'L0_attn_hidden': _L0_attn_in['hidden'], 'L0_attn_norm1_w': _L0_attn_in['norm1_w'], 'L0_attn_norm2_w': _L0_attn_in['norm2_w'], 'L0_attn_g_wq': _L0_attn_in['g_wq'], 'L0_attn_g_kv_down': _L0_attn_in['g_kv_down'], 'L0_attn_g_k_up': _L0_attn_in['g_k_up'], 'L0_attn_g_v_up': _L0_attn_in['g_v_up'], 'L0_attn_g_wo': _L0_attn_in['g_wo'], 'L0_attn_l_wq': _L0_attn_in['l_wq'], 'L0_attn_l_wk': _L0_attn_in['l_wk'], 'L0_attn_l_wv': _L0_attn_in['l_wv'], 'L0_attn_l_wo': _L0_attn_in['l_wo'], 'L0_ffn_gate_w': _L0_ffn_in['gate_w'], 'L0_ffn_gate_b': _L0_ffn_in['gate_b'], 'L0_ffn_w1': _L0_ffn_in['w1'], 'L0_ffn_b1': _L0_ffn_in['b1'], 'L0_ffn_w2': _L0_ffn_in['w2'], 'L0_ffn_b2': _L0_ffn_in['b2'], 'L0_ffn_ws1': _L0_ffn_in['ws1'], 'L0_ffn_bs1': _L0_ffn_in['bs1'], 'L0_ffn_ws2': _L0_ffn_in['ws2'], 'L0_ffn_bs2': _L0_ffn_in['bs2'], 'L1_attn_w_q': _L1_attn_in['w_q'], 'L1_attn_w_k': _L1_attn_in['w_k'], 'L1_attn_w_v': _L1_attn_in['w_v'], 'L1_ffn_router_w': _L1_ffn_in['router_w'], 'L1_ffn_router_b': _L1_ffn_in['router_b'], 'L1_ffn_W': _L1_ffn_in['W'], 'L1_ffn_V': _L1_ffn_in['V'], 'L1_ffn_W_out': _L1_ffn_in['W_out']}
    _x0 = _d['L0_attn_hidden']
    _d['L0_attn_hidden'] = jax.random.normal(jax.random.fold_in(jax.random.key(seed), 1), (16, 512, 128), dtype=_x0.dtype)
    del _x0
    return _d

def reference(L0_attn_hidden, L0_attn_norm1_w, L0_attn_norm2_w, L0_attn_g_wq, L0_attn_g_kv_down, L0_attn_g_k_up, L0_attn_g_v_up, L0_attn_g_wo, L0_attn_l_wq, L0_attn_l_wk, L0_attn_l_wv, L0_attn_l_wo, L0_ffn_gate_w, L0_ffn_gate_b, L0_ffn_w1, L0_ffn_b1, L0_ffn_w2, L0_ffn_b2, L0_ffn_ws1, L0_ffn_bs1, L0_ffn_ws2, L0_ffn_bs2, L1_attn_w_q, L1_attn_w_k, L1_attn_w_v, L1_ffn_router_w, L1_ffn_router_b, L1_ffn_W, L1_ffn_V, L1_ffn_W_out):

    def _L0_attn_ref(hidden, norm1_w, norm2_w, g_wq, g_kv_down, g_k_up, g_v_up, g_wo, l_wq, l_wk, l_wv, l_wo):
        import jax, jax.numpy as jnp
        import numpy as np
        D = 128
        H = 16
        KVH = 4
        HD = D // H
        LAT = 32
        WIN = 32
        B, S = (1, 256)
        BASE_G, BASE_L = (1000000.0, 10000.0)
        EPS = 1e-06

        def rmsnorm(x, w):
            return x * jax.lax.rsqrt(jnp.mean(x * x, axis=-1, keepdims=True) + EPS) * w

        def qk_norm(x):
            return x * jax.lax.rsqrt(jnp.mean(x * x, axis=-1, keepdims=True) + EPS)

        def rope(x, base):
            s, hd = (x.shape[-2], x.shape[-1])
            inv_freq = 1.0 / base ** (jnp.arange(0, hd, 2, dtype=jnp.float32) / hd)
            freqs = jnp.arange(s, dtype=jnp.float32)[:, None] * inv_freq[None, :]
            cos, sin = (jnp.cos(freqs), jnp.sin(freqs))
            xe, xo = (x[..., ::2], x[..., 1::2])
            out = jnp.stack([xe * cos - xo * sin, xe * sin + xo * cos], axis=-1)
            return out.reshape(x.shape)

        def split_heads(x, n_heads):
            b, s, _ = x.shape
            return x.reshape(b, s, n_heads, HD).transpose(0, 2, 1, 3)

        def repeat_kv(x):
            return jnp.repeat(x, H // KVH, axis=1)

        def sdpa(q, k, v, mask):
            scores = jnp.einsum('bhqd,bhkd->bhqk', q, k) / np.sqrt(HD).astype(np.float32)
            scores = jnp.where(mask, scores, jnp.float32(-1e+30))
            probs = jax.nn.softmax(scores, axis=-1)
            return jnp.einsum('bhqk,bhkd->bhqd', probs, v)

        def merge_heads(x):
            b, h, s, hd = x.shape
            return x.transpose(0, 2, 1, 3).reshape(b, s, h * hd)

        def global_latent_attn(x, wq, w_kv_down, w_k_up, w_v_up, wo):
            q = split_heads(x @ wq, H)
            latent = x @ w_kv_down
            k = split_heads(latent @ w_k_up, KVH)
            v = split_heads(latent @ w_v_up, KVH)
            q, k = (rope(q, BASE_G), rope(k, BASE_G))
            q, k = (qk_norm(q), qk_norm(k))
            k, v = (repeat_kv(k), repeat_kv(v))
            i = jnp.arange(x.shape[1])
            causal = i[:, None] >= i[None, :]
            return merge_heads(sdpa(q, k, v, causal)) @ wo

        def local_gqa_attn(x, wq, wk, wv, wo):
            q = split_heads(x @ wq, H)
            k = split_heads(x @ wk, KVH)
            v = split_heads(x @ wv, KVH)
            q, k = (rope(q, BASE_L), rope(k, BASE_L))
            q, k = (qk_norm(q), qk_norm(k))
            k, v = (repeat_kv(k), repeat_kv(v))
            i = jnp.arange(x.shape[1])
            diff = i[:, None] - i[None, :]
            mask = (diff >= 0) & (diff < WIN)
            return merge_heads(sdpa(q, k, v, mask)) @ wo
        x = hidden
        x = x + global_latent_attn(rmsnorm(x, norm1_w), g_wq, g_kv_down, g_k_up, g_v_up, g_wo)
        x = x + local_gqa_attn(rmsnorm(x, norm2_w), l_wq, l_wk, l_wv, l_wo)
        return x

    def _L0_ffn_ref(x, gate_w, gate_b, w1, b1, w2, b2, ws1, bs1, ws2, bs2):
        import jax, jax.numpy as jnp
        import numpy as np
        B, S, DIM = (4, 256, 128)
        E, K, HID = (8, 2, 512)
        orig_shape = x.shape
        xf = x.reshape(-1, DIM)
        logits = xf @ gate_w + gate_b
        top_w, top_i = jax.lax.top_k(logits, K)
        gw = jax.nn.softmax(top_w, axis=-1).astype(xf.dtype)
        combine = (gw[:, :, None] * jax.nn.one_hot(top_i, E, dtype=xf.dtype)).sum(axis=1)
        out = jnp.zeros_like(xf)
        for e in range(E):
            h = jax.nn.gelu(xf @ w1[e] + b1[e], approximate=False)
            out = out + combine[:, e:e + 1] * (h @ w2[e] + b2[e])
        shared = jax.nn.gelu(xf @ ws1 + bs1, approximate=False) @ ws2 + bs2
        return (out + shared).reshape(orig_shape)

    def _L1_attn_ref(x, w_q, w_k, w_v):
        import jax, jax.numpy as jnp
        import numpy as np

        def _rope_cos_sin(m, d, dtype=jnp.float32):
            i = jnp.arange(d // 2, dtype=dtype)
            theta = jnp.power(jnp.asarray(10000.0, dtype), -2.0 * (i - 1.0) / d)
            pos = jnp.arange(m, dtype=dtype)
            ang = pos[:, None] * theta[None, :]
            return (jnp.cos(ang), jnp.sin(ang))

        def _rotate(t, cos, sin):
            te = t[..., 0::2]
            to = t[..., 1::2]
            re = te * cos + to * sin
            ro = -te * sin + to * cos
            return jnp.stack((re, ro), axis=-1).reshape(t.shape)
        b, m, d = x.shape
        q = jnp.einsum('bmd,ed->bme', x, w_q)
        k = jnp.einsum('bmd,ed->bme', x, w_k)
        v = jnp.einsum('bmd,ed->bme', x, w_v)
        cos, sin = _rope_cos_sin(m, d, x.dtype)
        q_rot = _rotate(q, cos, sin)
        k_rot = _rotate(k, cos, sin)
        scores = jnp.einsum('bqd,bkd->bqk', q_rot, k_rot) / jnp.sqrt(jnp.asarray(d, x.dtype))
        causal = jnp.tril(jnp.ones((m, m), dtype=bool))
        scores = jnp.where(causal[None], scores, jnp.asarray(-jnp.inf, scores.dtype))
        attn = jax.nn.softmax(scores, axis=-1)
        return jnp.einsum('bqk,bkd->bqd', attn, v)

    def _L1_ffn_ref(x, router_w, router_b, W, V, W_out):
        import jax, jax.numpy as jnp
        import numpy as np
        B, T = (2, 256)
        D_MODEL, D_HIDDEN = (128, 256)
        N_EXPERTS, TOP_K = (8, 2)
        N_TOKENS = B * T
        CAPACITY = 2 * N_TOKENS * TOP_K // N_EXPERTS
        Bq, Tq, D = x.shape
        N = Bq * Tq
        x_flat = x.reshape(N, D)
        router_logits = x_flat @ router_w.T + router_b
        top_vals, top_ids = jax.lax.top_k(router_logits, TOP_K)
        top_probs = jax.nn.softmax(top_vals, axis=-1)
        x_pad = jnp.concatenate([x_flat, jnp.zeros((1, D), x_flat.dtype)], axis=0)
        probs_pad = jnp.concatenate([top_probs, jnp.zeros((1, TOP_K), top_probs.dtype)], axis=0)
        out = jnp.zeros((N + 1, D), x_flat.dtype)
        for e in range(N_EXPERTS):
            tok, slot = jnp.nonzero(top_ids == e, size=CAPACITY, fill_value=(N, 0))
            w = probs_pad[tok, slot][:, None]
            xin = x_pad[tok]
            a = xin @ W[e]
            b = xin @ V[e]
            y = a * (b * jax.nn.sigmoid(b)) @ W_out[e]
            out = out.at[tok].add(y * w)
        return out[:N].reshape(Bq, Tq, D)
    x = L0_attn_hidden
    xn = _layernorm(x, axis=-1)
    x = x + _L0_attn_ref(xn, L0_attn_norm1_w, L0_attn_norm2_w, L0_attn_g_wq, L0_attn_g_kv_down, L0_attn_g_k_up, L0_attn_g_v_up, L0_attn_g_wo, L0_attn_l_wq, L0_attn_l_wk, L0_attn_l_wv, L0_attn_l_wo) + _L0_ffn_ref(xn, L0_ffn_gate_w, L0_ffn_gate_b, L0_ffn_w1, L0_ffn_b1, L0_ffn_w2, L0_ffn_b2, L0_ffn_ws1, L0_ffn_bs1, L0_ffn_ws2, L0_ffn_bs2)
    xn = _layernorm(x, axis=-1)
    x = x + _L1_attn_ref(xn, L1_attn_w_q, L1_attn_w_k, L1_attn_w_v) + _L1_ffn_ref(xn, L1_ffn_router_w, L1_ffn_router_b, L1_ffn_W, L1_ffn_V, L1_ffn_W_out)
    return x

_drawn_inputs = setup_inputs


def setup_inputs(seed=0):
    import zlib

    import numpy as np

    out = dict(_drawn_inputs(seed))
    spreads = {'L0_attn_norm1_w': (1.0, 0.6),
     'L0_attn_norm2_w': (1.0, 0.6),
     'L0_ffn_gate_b': (0.0, 0.1),
     'L0_ffn_b1': (0.0, 0.685),
     'L0_ffn_b2': (0.0, 0.1),
     'L0_ffn_bs1': (0.0, 0.546),
     'L0_ffn_bs2': (0.0, 0.1),
     'L1_ffn_router_b': (0.0, 0.268)}
    factors = {'L0_attn_g_wq': 8.0,
     'L0_attn_g_kv_down': 8.0,
     'L0_attn_g_k_up': 8.0,
     'L0_attn_g_v_up': 8.0,
     'L0_attn_g_wo': 8.0,
     'L0_attn_l_wq': 6.846,
     'L0_attn_l_wk': 7.218,
     'L0_attn_l_wv': 6.083,
     'L0_attn_l_wo': 5.469}
    for name, (base, spread) in spreads.items():
        noise = np.random.default_rng([zlib.crc32(name.encode()), seed]).standard_normal(out[name].shape)
        drawn = base * np.exp(spread * noise) if base else spread * noise
        out[name] = jnp.asarray(drawn.astype(out[name].dtype))
    for name, factor in factors.items():
        out[name] = (out[name] * factor).astype(out[name].dtype)
    return out
```

```python
import numpy as np
import concourse.bass as bass
from concourse import mybir
from contextlib import ExitStack

F32 = mybir.dt.float32
F16 = mybir.dt.float16
I32 = mybir.dt.int32
ALU = mybir.AluOpType
ACT = mybir.ActivationFunctionType
AX = mybir.AxisListType

P = 128
SEQS, LEN, D = 16, 512, 128
T = LEN // P
TOKENS = SEQS * LEN
H, KVH = 16, 4
HD = D // H
J = H // KVH
QK = (H + KVH) * HD
LAT, WIN = 32, 32
E, HID = 8, 512
HC = HID // P
TOPK = 2
CAP = 2 * (2 * 256) * TOPK // 8
HID1 = 256
HC1 = HID1 // P
CC = CAP // P
SLOTS = E * CAP
VD = HD + 1
ATT_SCALE = 1.0 / float(np.sqrt(np.float32(HD)))
L1_SCALE = 1.0 / float(np.sqrt(np.float32(D)))
BIG = 1.0e30

LOCAL = [(0, 96, 0), (96, 96, 64), (192, 96, 160), (288, 96, 256), (384, 96, 352), (480, 32, 384)]
GLOBAL_UNITS = [(qt, g, kt) for qt in range(T) for g in range(KVH) for kt in range(qt + 1)]
LOCAL_UNITS = [(b, g) for b in range(len(LOCAL)) for g in range(KVH)]
EXPERTS = [[E, 0, 1], [2, 3, 4], [5, 6, 7]]

CONST = {}
_at = 0
for _n, _w in [("ident", P), ("causal", P), ("band", P), ("negmask", P), ("before", P), ("ones", P),
               ("cos_g", T * HD), ("sin_g", T * HD // 2), ("nsin_g", T * HD // 2),
               ("cos_l", T * HD), ("sin_l", T * HD // 2), ("nsin_l", T * HD // 2),
               ("cos1", LEN), ("sin1", LEN), ("iota", E), ("base", E), ("tok", T), ("len", T), ("half", 80), ("dump", SLOTS // P * 2)]:
    CONST[_n] = (_at, _at + _w)
    _at += _w
NCONST = _at
WEIGHT_LOADS = 33


def shape_constants():
    f = np.float32
    c = np.zeros((P, NCONST), f)

    def put(name, x):
        a, b = CONST[name]
        c[:, a:b] = np.broadcast_to(np.asarray(x, f).reshape(-1, b - a), (P, b - a))

    i = np.arange(P)
    put("ident", np.eye(P))
    put("causal", i[:, None] <= i[None, :])
    put("band", (i[None, :] - i[:, None] >= 0) & (i[None, :] - i[:, None] < WIN))
    put("negmask", np.where(i[None, :] <= i[:, None], 0.0, -BIG))
    put("before", i[:, None] < i[None, :])
    put("ones", np.ones((P, P)))
    for n, base in (("g", 1000000.0), ("l", 10000.0)):
        inv = (f(1.0) / (f(base) ** (np.arange(0, HD, 2, dtype=f) / f(HD)))).astype(f)
        ang = (np.arange(LEN, dtype=f)[:, None] * inv[None, :]).astype(f).astype(np.float64)
        cos, sin = np.cos(ang), np.sin(ang)
        tiles = lambda x: x.reshape(T, P, -1).transpose(1, 0, 2).reshape(P, -1)
        put("cos_" + n, tiles(np.repeat(cos, 2, axis=1)))
        put("sin_" + n, tiles(sin))
        put("nsin_" + n, tiles(-sin))
    theta = np.power(f(10000.0), (f(-2.0) * (np.arange(D // 2, dtype=f) - f(1.0)) / f(D)).astype(f)).astype(f)
    ang = (np.arange(LEN, dtype=f)[:, None] * theta[None, :]).astype(f).astype(np.float64)
    put("cos1", np.repeat(np.cos(ang), 2, axis=1).T)
    put("sin1", (np.repeat(np.sin(ang), 2, axis=1) * np.tile([1.0, -1.0], D // 2)).T)
    put("iota", np.arange(E))
    put("base", np.arange(E) * CAP)
    put("tok", i[:, None] + P * np.arange(T)[None, :])
    put("len", np.full(T, LEN))
    put("half", np.full(80, -0.5))
    d = np.zeros((P, SLOTS // P, 2))
    d[:, :, 0] = TOKENS + i[:, None] + P * np.arange(SLOTS // P)[None, :]
    put("dump", d.reshape(P, -1))
    return c


def program(nc, a, out, seqs=SEQS, dbg=None):
    ctx = ExitStack()
    with ctx, nc.allow_non_contiguous_dma("weights are laid out once"):
        def sb(name, shape, dt=F32):
            return ctx.enter_context(nc.sbuf_tensor(name, shape, dt))

        def sem(name):
            return ctx.enter_context(nc.semaphore(name))

        def scratch(name, shape):
            return nc.dram_tensor(name, shape, F32, kind="Internal").ap()

        tokens = seqs * LEN
        xnew_d = scratch("xnew_d", [tokens, D])
        xn1_d = scratch("xn1_d", [tokens, D])
        slot_d = scratch("slot_d", [SLOTS, 2])

        consts = sb("consts", [P, NCONST])

        def const(name):
            return consts[:, CONST[name][0]:CONST[name][1]]
        ident = const("ident")
        ident16 = sb("ident16", [P, P], F16)
        w1 = sb("w1", [P, E + 1, HID])
        w2 = sb("w2", [P, E + 1, HC, D])
        b1 = sb("b1", [P, E + 1, HC])
        b2 = sb("b2", [E + 1, D])
        gate_b = sb("gate_b", [P, E])
        wg_raw = sb("wg_raw", [P, D])
        wl_raw = sb("wl_raw", [P, D + 64])
        norm1 = sb("norm1", [P, 1])
        norm2 = sb("norm2", [P, 1])
        kv_down = sb("kv_down", [P, LAT])
        kv_downT = sb("kv_downT", [LAT, P])
        kv_up = sb("kv_up", [LAT, 64])
        wg = sb("wg", [P, QK + 32 + E])
        wl = sb("wl", [P, QK + 32])
        wo_g = sb("wo_g", [P, D])
        wo_l = sb("wo_l", [P, D])
        l1_raw = sb("l1_raw", [P, 3, D])
        wqk1 = sb("wqk1", [P, 4, D])
        wv1 = sb("wv1", [P, D])
        router = sb("router", [P, E])
        router_b = sb("router_b", [P, E])
        w_a = sb("w_a", [P, E, HID1])
        w_b = sb("w_b", [P, E, HID1])
        w_o = sb("w_o", [P, E, HC1, D])

        x = sb("x", [P, T, D])
        xn = sb("xn", [P, T, D])
        x1 = sb("x1", [P, T, D])
        y2 = sb("y2", [P, T, D])
        acc = sb("acc", [P, T, D])
        xnT = sb("xnT", [P, LEN])
        y2T = sb("y2T", [P, LEN])
        stats = sb("stats", [P, T, 6])
        mv = sb("mv", [P, T, 2])
        small = sb("small", [P, 12, T])
        VE, RSTD, E1, R1, EPS1, MS2, R2, SQ = range(8)
        sq = sb("sq", [P, T, QK])
        msum = sb("msum", [P, T * (H + KVH)])
        rq = sb("rq", [P, T * (H + KVH)])
        t1 = sb("t1", [P, T, QK])
        t2 = sb("t2", [P, T, QK])
        qn = sb("qn", [P, T, QK])
        stack = sb("stack", [P, T, H + KVH, 4, HD], F16)
        QKT = sb("QKT", [P, J + 1, LEN], F16)
        Vg = sb("Vg", [P, T, KVH, VD])
        Vl = sb("Vl", [P, len(LOCAL), KVH, VD])
        probs = sb("probs", [P, 4, LEN])
        hidT = sb("hidT", [P, 2, HC, LEN])
        rden = sb("rden", [P, 2, H])
        otok = sb("otok", [P, 2, H, HD])
        oT = sb("oT", [P, LEN])
        lg = sb("lg", [P, T, E])
        gk = sb("gk", [P, T, E])
        l2 = sb("l2", [P, T, E])
        oh = sb("oh", [P, 2, T, E])
        km = sb("km", [P, 2, T])
        gm = sb("gm", [P, 2, T])
        gd = sb("gd", [P, 2, T])
        gw = sb("gw", [P, 2, T])
        cw = sb("cw", [P, T, E + 1])
        cwT = sb("cwT", [E + 1, LEN])

        qk_turned = sb("qk_turned", [P, 2, LEN])
        rot = sb("rot", [P, 2, 2, LEN])
        v1 = sb("v1", [P, T, D])
        pr1 = sb("pr1", [P, 2, LEN])
        prT = sb("prT", [P, 2, T, P])
        top = sb("top", [P, 2, T])
        psums = sb("psums", [P, 2, T])
        chosen = sb("chosen", [P, T, E])
        before_t = sb("before_t", [P, T + 1, E])
        rank = sb("rank", [P, T, E])
        rsel = sb("rsel", [P, 2, 2, T, E])
        rk = sb("rk", [P, 2, 2, T])
        tok = sb("tok", [P, T])
        entry = sb("entry", [P, 2, T, 2])
        slot = sb("slot", [P, 2, T], I32)
        table = sb("table", [P, E * CC, 2])
        gather_at = sb("gather_at", [P, E * CC], I32)
        add_at = sb("add_at", [P, E * CC], I32)
        tclip = sb("tclip", [P, E * CC])
        xg = sb("xg", [P, E * CC, D])
        xgT = sb("xgT", [P, 2, CAP])
        sig = sb("sig", [P, 2, HC1, CAP])
        gT = sb("gT", [P, 2, HC1, CAP])
        yo = sb("yo", [P, E * CC, D])

        bank = [ctx.enter_context(nc.psum_tensor(f"bank{i}", [P, 512], F32)) for i in range(8)]
        qkv_t = None
        ring = [bank[2], bank[3], bank[4]]
        obank = [bank[5], bank[6]]
        misc = bank[7]

        def qkv(t, lo, hi):
            return bank[t // 2][:, (t % 2) * 256 + lo:(t % 2) * 256 + hi]

        def qkv2(half, lo, hi):
            return bank[half][:, :].rearrange("p (t n) -> p t n", t=2)[:, :, lo:hi]

        def as16(b):
            return b[:, 0:(J + 1) * P // 2].bitcast(F16).rearrange("p (b n) -> p b n", b=J + 1)

        S = {}

        class Signal:
            def __init__(self, name, per):
                self.sem, self.per, self.name, self.n, self.base = sem(name), per, name, 0, 0
                S[name] = self

            def inc(self, ins, by=1):
                self.n += by
                ins.then_inc(self.sem, by)

            def at(self, s, n):
                return s * self.per + (n + self.base)

        weights_in = sem("weights_in")
        setup_dve = sem("setup_dve")
        setup_pe = sem("setup_pe")

        x_loaded = Signal("x_loaded", 16)
        x_free = Signal("x_free", 1)
        xnew_stored = Signal("xnew_stored", 16)
        vec = Signal("vec", 0)
        pow_in = Signal("pow_in", 5)
        pow_out = Signal("pow_out", 5)
        normed = Signal("normed", 2 * T)
        turned = Signal("turned", 2)
        turned_sb = Signal("turned_sb", 2)
        projected = Signal("projected", 2)
        roped = Signal("roped", 2)
        squared = Signal("squared", 2)
        stacked = Signal("stacked", 2)
        stackT = Signal("stackT", 2 * T)
        heads = Signal("heads", 2 * T)
        values = Signal("values", 2)
        filled = Signal("filled", 36 + 64)
        evac = Signal("evac", 36 + 64)
        masked = Signal("masked", 4 * T + 24)
        pv = Signal("pv", 64)
        otoks = Signal("otoks", T + 6)
        oturn = Signal("oturn", T + 6)
        oT_sb = Signal("oT_sb", T + 6)
        attn = Signal("attn", 2)
        attn_used = Signal("attn_used", 2)
        ypsum = Signal("ypsum", 9)
        yused = Signal("yused", 9)
        gate_in = Signal("gate_in", 1)
        gate_exp = Signal("gate_exp", 1)
        cw_ready = Signal("cw_ready", 1)
        cw_turn = Signal("cw_turn", 1)
        cwT_sb = Signal("cwT_sb", 1)
        bias2 = Signal("bias2", 1)
        xnew = Signal("xnew", 1)

        VEC_PER = 75
        vec.per = VEC_PER

        l_loaded = Signal("l_loaded", 16)
        l_free = Signal("l_free", 1)
        l_vec = Signal("l_vec", 59)
        l_pow_in = Signal("l_pow_in", 1)
        l_pow_out = Signal("l_pow_out", 1)
        l_normed = Signal("l_normed", T)
        l_turned = Signal("l_turned", 1)
        l_turned_sb = Signal("l_turned_sb", 1)
        l_proj = Signal("l_proj", 4)
        l_v1 = Signal("l_v1", 1)
        l_rotated = Signal("l_rotated", 2)
        l_gate_in = Signal("l_gate_in", 1)
        l_gate_exp = Signal("l_gate_exp", 1)
        l_chosen = Signal("l_chosen", 1)
        l_rank = Signal("l_rank", 1)
        l_entries = Signal("l_entries", 1)
        l_scattered = Signal("l_scattered", 16 * 2 * T)
        tok_next = Signal("tok_next", 1)
        l_scores = Signal("l_scores", T)
        l_max = Signal("l_max", T)
        l_exp = Signal("l_exp", T)
        l_prT = Signal("l_prT", T)
        l_prT_sb = Signal("l_prT_sb", T)
        l_pv = Signal("l_pv", T)
        l_out = Signal("l_out", T)
        xn1_stored = Signal("xn1_stored", 16)
        out_stored = Signal("out_stored", 16)
        table_in = sem("table_in")
        e_vec = sem("e_vec")
        e_index = sem("e_index")
        e_gathered = [sem(f"e_gathered{e}") for e in range(E)]
        e_turned = sem("e_turned")
        e_turned_sb = sem("e_turned_sb")
        e_hidden = sem("e_hidden")
        e_sig = sem("e_sig")
        e_gated = sem("e_gated")
        e_y = sem("e_y")
        e_yo = sem("e_yo")
        e_added = sem("e_added")

        block = ctx.enter_context(nc.Block())


        @block.sync
        def _(sp):
            n = [0]

            def load(dst, src):
                sp.dma_start(dst, src).then_inc(weights_in, 16)
                n[0] += 1
            load(consts[:, :], a["shape_constants"])
            load(norm1[:, 0:1], a["L0_attn_norm1_w"].rearrange("(p o) -> p o", o=1))
            load(norm2[:, 0:1], a["L0_attn_norm2_w"].rearrange("(p o) -> p o", o=1))
            load(wg_raw[:, :], a["L0_attn_g_wq"])
            load(kv_down[:, :], a["L0_attn_g_kv_down"])
            load(kv_up[:, 0:32], a["L0_attn_g_k_up"])
            load(kv_up[:, 32:64], a["L0_attn_g_v_up"])
            load(wl_raw[:, 0:D], a["L0_attn_l_wq"])
            load(wl_raw[:, D:D + 32], a["L0_attn_l_wk"])
            load(wl_raw[:, D + 32:D + 64], a["L0_attn_l_wv"])
            load(wo_g[:, :], a["L0_attn_g_wo"])
            load(wo_l[:, :], a["L0_attn_l_wo"])
            load(wg[:, QK + 32:QK + 32 + E], a["L0_ffn_gate_w"])
            load(gate_b[:, :], a["L0_ffn_gate_b"].partition_broadcast(P))
            load(w1[:, 0:E, :], a["L0_ffn_w1"].rearrange("e d h -> d e h"))
            load(w1[:, E, :], a["L0_ffn_ws1"])
            load(w2[:, E, :, :], a["L0_ffn_ws2"].rearrange("(c p) d -> p c d", p=P))
            for e in range(0, E, 4):
                load(w2[:, e:e + 4, :, :].rearrange("p e c d -> p (e c) d"),
                     a["L0_ffn_w2"][e:e + 4].rearrange("e (c p) d -> p (e c) d", p=P))
            load(b1[:, 0:E, :].rearrange("p e c -> p (e c)"), a["L0_ffn_b1"].rearrange("e (c p) -> p (e c)", p=P))
            load(b1[:, E, :], a["L0_ffn_bs1"].rearrange("(c p) -> p c", p=P))
            load(b2[0:E, :], a["L0_ffn_b2"])
            load(b2[E:E + 1, :], a["L0_ffn_bs2"].rearrange("(o d) -> o d", o=1))
            load(slot_d.rearrange("(c p) w -> p c w", p=P), a["shape_constants"][:, CONST["dump"][0]:CONST["dump"][1]].rearrange("p (c w) -> p c w", w=2))
            load(l1_raw[:, 0, :], a["L1_attn_w_q"])
            load(l1_raw[:, 1, :], a["L1_attn_w_k"])
            load(l1_raw[:, 2, :], a["L1_attn_w_v"])
            load(router[:, :], a["L1_ffn_router_w"].rearrange("e d -> d e"))
            load(router_b[:, :], a["L1_ffn_router_b"].partition_broadcast(P))
            load(w_a[:, :, :], a["L1_ffn_W"].rearrange("e d h -> d e h"))
            load(w_b[:, :, :], a["L1_ffn_V"].rearrange("e d h -> d e h"))
            load(w_o[:, :, :, :].rearrange("p e c d -> p (e c) d"), a["L1_ffn_W_out"].rearrange("e (c p) d -> p (e c) d", p=P))
            load(out[TOKENS:TOKENS + SLOTS, :].rearrange("(r p) d -> p r d", p=P), a["zero_rows"].rearrange("(r p) d -> p r d", p=P))
            assert n[0] == WEIGHT_LOADS, n[0]
            x_by_seq = a["x"].rearrange("s (t p) d -> s p t d", p=P)
            xnew_by_seq = xnew_d.rearrange("(s t p) d -> s p t d", p=P, t=T)
            sp.dma_start(x[:, :, :], x_by_seq[0]).then_inc(x_loaded.sem, 16)

            def store(s_before, nth):
                sp.wait_ge(xnew.sem, nth)
                sp.dma_start(xnew_by_seq[s_before], acc[:, :, :]).then_inc(xnew_stored.sem, 16)
            if seqs > 1:
                with sp.Fori(1, seqs) as s:
                    sp.wait_ge(x_free.sem, s)
                    sp.dma_start(x[:, :, :], x_by_seq[s]).then_inc(x_loaded.sem, 16)
                    store(s - 1, s)
            store(seqs - 1, seqs)
            sp.wait_ge(xnew_stored.sem, 16 * (seqs + 1))
            if dbg is not None:
                sp.dma_start(dbg, xnew_d[:, :]).then_inc(xnew_stored.sem, 16)
                sp.wait_ge(xnew_stored.sem, 16 * (seqs + 2))

            xn1_by_seq = xn1_d.rearrange("(s t p) d -> s p t d", p=P, t=T)
            out_by_seq = out[0:tokens, :].rearrange("(s t p) d -> s p t d", p=P, t=T)
            sp.dma_start(x[:, :, :], xnew_by_seq[0]).then_inc(l_loaded.sem, 16)

            def store1(s_before, nth):
                sp.wait_ge(l_normed.sem, l_normed.per * nth)
                sp.dma_start(xn1_by_seq[s_before], xn[:, :, :]).then_inc(xn1_stored.sem, 16)
                sp.wait_ge(l_out.sem, l_out.per * nth)
                sp.dma_start(out_by_seq[s_before], acc[:, :, :]).then_inc(out_stored.sem, 16)
            if seqs > 1:
                with sp.Fori(1, seqs) as s:
                    sp.wait_ge(l_free.sem, s)
                    sp.dma_start(x[:, :, :], xnew_by_seq[s]).then_inc(l_loaded.sem, 16)
                    store1(s - 1, s)
            store1(seqs - 1, seqs)
            sp.wait_ge(l_scattered.sem, l_scattered.per * seqs)
            sp.dma_start(table[:, :, :], slot_d.rearrange("(c p) w -> p c w", p=P)).then_inc(table_in, 16)
            sp.wait_ge(xn1_stored.sem, 16 * (seqs + 1))
            sp.wait_ge(out_stored.sem, 16 * (seqs + 1))
            sp.wait_ge(e_added, 16 * E * CC)

        @block.gpsimd
        def _(pool):
            pool.wait_ge(weights_in, WEIGHT_LOADS * 16)
            with pool.Fori(0, seqs) as s:
                def power(dst, src, n):
                    pool.wait_ge(pow_in.sem, pow_in.at(s, pow_out.n + 1))
                    pow_out.inc(nc.gpsimd.tensor_tensor(dst, src, const("half")[:, 0:n], ALU.pow))

                power(small[:, RSTD, :], small[:, VE, :], T)
                power(small[:, R1, :], small[:, E1, :], T)
                power(rq[:, :], msum[:, :], 80)
                power(small[:, R2, :], small[:, MS2, :], T)
                power(rq[:, :], msum[:, :], 80)

            with pool.Fori(0, seqs) as s:
                pool.wait_ge(l_pow_in.sem, l_pow_in.at(s, 1))
                l_pow_out.inc(nc.gpsimd.tensor_tensor(small[:, RSTD, :], small[:, VE, :], const("half")[:, 0:T], ALU.pow))
                pool.wait_ge(l_entries.sem, l_entries.at(s, 1))
                nc.gpsimd.tensor_tensor(tok[:, :], tok[:, :], const("len"), ALU.add).then_inc(tok_next.sem, 1)
                for k in range(2):
                    for t in range(T):
                        l_scattered.inc(nc.gpsimd.indirect_dma_start(
                            slot_d, bass.IndirectOffsetOnAxis(ap=slot[:, k, t:t + 1], axis=0), entry[:, k, t, :], None,
                            bounds_check=SLOTS - 1, oob_is_err=False), 16)
                pool.wait_ge(l_scattered.sem, l_scattered.at(s, l_scattered.per))

            pool.wait_ge(e_index, 1)
            pool.wait_ge(xn1_stored.sem, 16 * (seqs + 1))
            for c in range(E * CC):
                nc.gpsimd.indirect_dma_start(xg[:, c, :], None, xn1_d, bass.IndirectOffsetOnAxis(ap=gather_at[:, c:c + 1], axis=0),
                                             bounds_check=tokens - 1, oob_is_err=True).then_inc(e_gathered[c // CC], 16)
            pool.wait_ge(out_stored.sem, 16 * (seqs + 1))
            for e in range(E):
                pool.wait_ge(e_yo, e + 1)
                if e:
                    pool.wait_ge(e_added, 16 * CC * e)
                for c in range(CC * e, CC * e + CC):
                    nc.gpsimd.indirect_dma_start(out, bass.IndirectOffsetOnAxis(ap=add_at[:, c:c + 1], axis=0), yo[:, c, :], None,
                                                 bounds_check=TOKENS + SLOTS - 1, oob_is_err=True, compute_op=ALU.add).then_inc(e_added, 16)

        @block.scalar
        def _(act):
            act.wait_ge(weights_in, WEIGHT_LOADS * 16)
            with act.Fori(0, seqs) as s:
                def turned_copy(i, dst):
                    act.wait_ge(turned.sem, turned.at(s, i + 1))
                    turned_sb.inc(nc.scalar.activation(dst, misc[:, :], ACT.Copy))

                def square(i):
                    act.wait_ge(roped.sem, roped.at(s, i + 1))
                    squared.inc(nc.scalar.activation(sq[:, :, :], t1[:, :, :], ACT.Square))

                def gelus(group):
                    for k, e in enumerate(EXPERTS[group]):
                        n = 3 * group + k
                        if n >= 2:
                            act.wait_ge(ypsum.sem, ypsum.at(s, n - 1))
                        for c in range(HC):
                            act.wait_ge(filled.sem, filled.at(s, evac.n + 1))
                            evac.inc(nc.scalar.activation(hidT[:, n % 2, c, :], ring[evac.n % 3][:, :], ACT.Gelu, bias=b1[:, e, c:c + 1]))

                def exps(units, first, width):
                    for i in range(len(units)):
                        if i >= 4:
                            act.wait_ge(pv.sem, pv.at(s, first + i - 3))
                        n = width(i)
                        act.wait_ge(filled.sem, filled.at(s, evac.n + 1))
                        evac.inc(nc.scalar.activation(probs[:, i % 4, 0:n], ring[evac.n % 3][:, 0:n], ACT.Exp, scale=ATT_SCALE))

                turned_copy(0, xnT[:, :])
                square(0)
                act.wait_ge(gate_in.sem, gate_in.at(s, 1))
                gate_exp.inc(nc.scalar.activation(gd[:, 1, :], gd[:, 0, :], ACT.Exp))
                gelus(0)
                exps(GLOBAL_UNITS, 0, lambda i: J * P)
                turned_copy(1, y2T[:, :])
                square(1)
                gelus(1)
                exps(LOCAL_UNITS, 40, lambda i: J * LOCAL[LOCAL_UNITS[i][0]][1])
                gelus(2)

            with act.Fori(0, seqs) as s:
                act.wait_ge(l_turned.sem, l_turned.at(s, 1))
                l_turned_sb.inc(nc.scalar.activation(xnT[:, :], misc[:, :], ACT.Copy))
                act.wait_ge(l_gate_in.sem, l_gate_in.at(s, 1))
                l_gate_exp.inc(nc.scalar.activation(gd[:, 1, :], gd[:, 0, :], ACT.Exp))
                act.wait_ge(l_proj.sem, l_proj.at(s, 4))
                l_v1.inc(nc.scalar.activation(v1[:, :, :].rearrange("p t d -> p (t d)"), bank[4][:, :], ACT.Copy))
                for qt in range(T):
                    n = (qt + 1) * P
                    act.wait_ge(l_max.sem, l_max.at(s, qt + 1))
                    if qt >= 2:
                        act.wait_ge(l_prT.sem, l_prT.at(s, qt - 1))
                    l_exp.inc(nc.scalar.activation(pr1[:, qt % 2, 0:n], bank[qt % 2][:, 0:n], ACT.Exp, bias=top[:, 1, qt:qt + 1],
                                                   scale=L1_SCALE, accum_out=psums[:, 0, qt:qt + 1]))

            for e in range(E):
                act.wait_ge(e_hidden, e + 1)
                if e >= 2:
                    act.wait_ge(e_gated, e - 1)
                nc.scalar.activation(sig[:, e % 2, :, :].rearrange("p c n -> p (c n)"), bank[4 + e % 2][:, :], ACT.Sigmoid).then_inc(e_sig, 1)

        @block.vector
        def _(v):
            v.wait_ge(weights_in, WEIGHT_LOADS * 16)
            step = [0]

            def setup(ins):
                step[0] += 1
                ins.then_inc(setup_dve, 1)
                v.wait_ge(setup_dve, step[0])

            setup(nc.vector.tensor_copy(ident16[:, :], ident))
            setup(nc.vector.memset(Vg[:, :, :, HD:VD], 1.0))
            setup(nc.vector.memset(Vl[:, :, :, HD:VD], 1.0))
            setup(nc.vector.memset(cw[:, :, E:E + 1], 1.0))
            for dst, raw, nrm in ((wg, wg_raw, norm1), (wl, wl_raw, norm2)):
                setup(nc.vector.tensor_scalar(dst[:, 0:D].rearrange("p (j g d) -> p j g d", j=J, g=KVH),
                                              raw[:, 0:D].rearrange("p (g j d) -> p j g d", j=J, g=KVH),
                                              nrm[:, 0:1], None, ALU.mult))
            setup(nc.vector.tensor_scalar(wl[:, D:D + 64], wl_raw[:, D:D + 64], norm2[:, 0:1], None, ALU.mult))
            v.wait_ge(setup_pe, 1)
            setup(nc.vector.tensor_copy(kv_downT[:, :], bank[0][0:LAT, 0:P]))
            v.wait_ge(setup_pe, 2)
            setup(nc.vector.tensor_scalar(wg[:, D:D + 64], bank[1][:, 0:64], norm1[:, 0:1], None, ALU.mult))
            for i in range(2):
                src = bank[2 + i][:, 0:P]
                swapped = wqk1[:, 2 * i + 1, :].rearrange("p (n e) -> p n e", e=2)
                v.wait_ge(setup_pe, 3 + i)
                setup(nc.vector.tensor_copy(wqk1[:, 2 * i, :], src))
                for e in range(2):
                    setup(nc.vector.tensor_copy(swapped[:, :, e], src.rearrange("p (n e) -> p n e", e=2)[:, :, 1 - e]))
            v.wait_ge(setup_pe, 5)
            setup(nc.vector.tensor_copy(wv1[:, :], bank[4][:, 0:P]))
            setup(nc.vector.tensor_copy(tok[:, :], const("tok")))
            setup(nc.vector.memset(before_t[:, T, :], 0.0))
            nc.vector.memset(small[:, 9, :], 0.0).then_inc(xn1_stored.sem, 16)
            nc.vector.memset(small[:, 10, :], 0.0).then_inc(out_stored.sem, 16)
            nc.vector.memset(small[:, 11, :], 0.0).then_inc(xnew_stored.sem, 16)

            def top2(chained, src):
                wide = lambda z: z.unsqueeze(2).to_broadcast([P, T, E])
                iota = const("iota").unsqueeze(1).to_broadcast([P, T, E])
                for k in range(2):
                    chained(nc.vector.tensor_reduce(gm[:, k, :], src[:, :, :], AX.X, ALU.max))
                    chained(nc.vector.tensor_tensor(gk[:, :, :], src[:, :, :], wide(gm[:, k, :]), ALU.is_equal))
                    chained(nc.vector.scalar_tensor_tensor(gk[:, :, :], gk[:, :, :], -16.0, iota, ALU.mult, ALU.add))
                    chained(nc.vector.tensor_reduce(km[:, k, :], gk[:, :, :], AX.X, ALU.min))
                    chained(nc.vector.tensor_tensor(oh[:, k, :, :], gk[:, :, :], wide(km[:, k, :]), ALU.is_equal))
                    if k == 0:
                        chained(nc.vector.scalar_tensor_tensor(l2[:, :, :], oh[:, 0, :, :], -BIG, src[:, :, :], ALU.mult, ALU.add))
                        src = l2

            def moments(s, sig, src):
                def wait():
                    v.wait_ge(sig.sem, sig.at(s, sig.n))
                for t in range(T):
                    sig.inc(nc.vector.bn_stats(stats[:, t, :], src[:, t, :]))
                wait()
                m = small[:, 8:11, :]
                sig.inc(nc.vector.tensor_tensor(m[:, 0, :], stats[:, :, 1], stats[:, :, 4], ALU.add))
                sig.inc(nc.vector.tensor_tensor(m[:, 1, :], stats[:, :, 1], stats[:, :, 4], ALU.subtract))
                sig.inc(nc.vector.tensor_tensor(m[:, 2, :], stats[:, :, 2], stats[:, :, 5], ALU.add))
                wait()
                sig.inc(nc.vector.tensor_scalar(mv[:, :, 0], m[:, 0, :], 0.5, None, ALU.mult))
                sig.inc(nc.vector.tensor_tensor(m[:, 1, :], m[:, 1, :], m[:, 1, :], ALU.mult))
                sig.inc(nc.vector.tensor_scalar(m[:, 2, :], m[:, 2, :], 1.0 / D, None, ALU.mult))
                wait()
                sig.inc(nc.vector.scalar_tensor_tensor(mv[:, :, 1], m[:, 1, :], 0.25, m[:, 2, :], ALU.mult, ALU.add))
                wait()

            with v.Fori(0, seqs) as s:
                def chained(ins):
                    vec.inc(ins)
                    v.wait_ge(vec.sem, vec.at(s, vec.n))

                def powers(ins, after=None):
                    pow_in.inc(ins)
                    n = pow_in.n
                    if after:
                        after()
                    v.wait_ge(pow_out.sem, pow_out.at(s, n))

                v.wait_ge(x_loaded.sem, x_loaded.at(s, 16))
                moments(s, vec, x)
                powers(nc.vector.tensor_scalar(small[:, VE, :], mv[:, :, 1], 1e-5, None, ALU.add))
                for t in range(T):
                    normed.inc(nc.vector.tensor_scalar(xn[:, t, :], x[:, t, :], mv[:, t, 0:1], small[:, RSTD, t:t + 1],
                                                       ALU.subtract, ALU.mult))
                chained(nc.vector.tensor_tensor(small[:, SQ, :], small[:, RSTD, :], small[:, RSTD, :], ALU.mult))
                chained(nc.vector.tensor_tensor(small[:, SQ, :], small[:, SQ, :], mv[:, :, 1], ALU.mult))
                powers(nc.vector.tensor_scalar(small[:, E1, :], small[:, SQ, :], 1e-6, None, ALU.add))
                chained(nc.vector.tensor_scalar(small[:, EPS1, :], small[:, E1, :], 1e-6, None, ALU.mult))
                x_free.inc(nc.vector.tensor_tensor(x1[:, :, :], x[:, :, :], xn[:, :, :], ALU.add))

                def rope(i, n, eps, meanwhile):
                    cos = const("cos_" + n).rearrange("p (t d) -> p t d", t=T)
                    sin = const("sin_" + n).rearrange("p (t d) -> p t d", t=T)
                    nsin = const("nsin_" + n).rearrange("p (t d) -> p t d", t=T)
                    for h in range(2):
                        ts = slice(2 * h, 2 * h + 2)
                        src = qkv2(h, 0, QK)
                        pairs = src.rearrange("p t (n d e) -> p t n d e", d=HD // 2, e=2)
                        to = t2[:, ts, :].rearrange("p t (n d e) -> p t n d e", d=HD // 2, e=2)
                        vec.inc(nc.vector.tensor_tensor(
                            t1[:, ts, :].rearrange("p t (n d) -> p t n d", d=HD),
                            src.rearrange("p t (n d) -> p t n d", d=HD),
                            cos[:, ts, :].unsqueeze(2).to_broadcast([P, 2, H + KVH, HD]), ALU.mult))
                        for e, tab in ((0, nsin), (1, sin)):
                            vec.inc(nc.vector.tensor_tensor(
                                to[:, :, :, :, e], pairs[:, :, :, :, 1 - e],
                                tab[:, ts, :].unsqueeze(2).to_broadcast([P, 2, H + KVH, HD // 2]), ALU.mult))
                    v.wait_ge(vec.sem, vec.at(s, vec.n))
                    roped.inc(nc.vector.tensor_tensor(t1[:, :, :], t1[:, :, :], t2[:, :, :], ALU.add))
                    meanwhile()
                    v.wait_ge(squared.sem, squared.at(s, i + 1))
                    chained(nc.vector.tensor_reduce(msum[:, :], sq[:, :, :].rearrange("p t (n d) -> p (t n) d", d=HD), AX.X, ALU.add))
                    if eps is None:
                        ins = nc.vector.tensor_scalar(msum[:, :], msum[:, :], 1.0 / HD, 1e-6, ALU.mult, ALU.add)
                    else:
                        m3 = msum[:, :].rearrange("p (t n) -> p t n", t=T)
                        ins = nc.vector.scalar_tensor_tensor(m3, m3, 1.0 / HD, eps.unsqueeze(2).to_broadcast([P, T, H + KVH]),
                                                             ALU.mult, ALU.add)
                    return ins

                def halves(i):
                    as3 = lambda z: z.rearrange("p t (n d) -> p (t n) d", d=HD)
                    slots = stack[:, :, :, :, :].rearrange("p t n s d -> p (t n) s d")
                    v.wait_ge(vec.sem, vec.at(s, vec.n))
                    chained(nc.vector.tensor_tensor(as3(qn[:, :, :]), as3(t1[:, :, :]),
                                                    rq[:, :].unsqueeze(2).to_broadcast([P, T * (H + KVH), HD]), ALU.mult))
                    chained(nc.vector.tensor_copy(slots[:, :, 0, :], as3(qn[:, :, :])))
                    chained(nc.vector.tensor_tensor(slots[:, :, 3, :], as3(qn[:, :, :]), slots[:, :, 0, :], ALU.subtract))
                    for dst, src, lo, hi in ((1, 0, 0, H), (2, 3, 0, H), (2, 0, H, H + KVH), (1, 3, H, H + KVH)):
                        ins = nc.vector.tensor_copy(stack[:, :, lo:hi, dst, :], stack[:, :, lo:hi, src, :])
                    stacked.inc(ins)

                def head_copies():
                    for t in range(T):
                        v.wait_ge(stackT.sem, stackT.at(s, heads.n + 1))
                        heads.inc(nc.vector.tensor_copy(QKT[:, :, t * P:(t + 1) * P], as16(ring[t % 3])))

                def gating():
                    for h in range(2):
                        vec.inc(nc.vector.tensor_tensor(lg[:, 2 * h:2 * h + 2, :], qkv2(h, QK + 32, QK + 32 + E),
                                                        gate_b[:, :].unsqueeze(1).to_broadcast([P, 2, E]), ALU.add))
                    v.wait_ge(vec.sem, vec.at(s, vec.n))
                    top2(chained, lg)
                    gate_in.inc(nc.vector.tensor_tensor(gd[:, 0, :], gm[:, 1, :], gm[:, 0, :], ALU.subtract))

                def gate_weights():
                    v.wait_ge(gate_exp.sem, gate_exp.at(s, 1))
                    wide = lambda z: z.unsqueeze(2).to_broadcast([P, T, E])
                    chained(nc.vector.tensor_scalar(gw[:, 0, :], gd[:, 1, :], 1.0, None, ALU.add))
                    chained(nc.vector.reciprocal(gw[:, 0, :], gw[:, 0, :]))
                    chained(nc.vector.tensor_tensor(gw[:, 1, :], gw[:, 0, :], gd[:, 1, :], ALU.mult))
                    for k in range(2):
                        chained(nc.vector.tensor_tensor(oh[:, k, :, :], oh[:, k, :, :], wide(gw[:, k, :]), ALU.mult))
                    cw_ready.inc(nc.vector.tensor_tensor(cw[:, :, 0:E], oh[:, 0, :, :], oh[:, 1, :, :], ALU.add))
                    v.wait_ge(cw_ready.sem, cw_ready.at(s, 1))

                def combine(group):
                    for e in EXPERTS[group]:
                        n = yused.n
                        v.wait_ge(ypsum.sem, ypsum.at(s, n + 1))
                        if n:
                            v.wait_ge(yused.sem, yused.at(s, n))
                        y = obank[n % 2][:, :].rearrange("p (t d) -> p t d", t=T)
                        if e == E:
                            v.wait_ge(xnew_stored.sem, 16 * s + 16)
                            yused.inc(nc.vector.tensor_tensor(acc[:, :, :], y, x1[:, :, :], ALU.add))
                            continue
                        for t in range(T):
                            ins = nc.vector.scalar_tensor_tensor(acc[:, t, :], y[:, t, :], cw[:, t, e:e + 1], acc[:, t, :], ALU.mult, ALU.add)
                        yused.inc(ins)

                def mask(use, slot, table, nq, q_off):
                    v.wait_ge(evac.sem, evac.at(s, use + 1))
                    m = const(table)[:, q_off:q_off + nq].unsqueeze(1).to_broadcast([P, J, nq])
                    pr = probs[:, slot, 0:J * nq].rearrange("p (j q) -> p j q", j=J)
                    masked.inc(nc.vector.tensor_tensor(pr, pr, m, ALU.mult))

                def divide(blk, nq, last_unit):
                    r = blk % 2
                    v.wait_ge(pv.sem, pv.at(s, last_unit + 1))
                    o = obank[r][0:nq, 0:H * VD].rearrange("p (h d) -> p h d", d=VD)
                    chained(nc.vector.reciprocal(rden[0:nq, r, :], o[:, :, HD]))
                    otoks.inc(nc.vector.tensor_tensor(otok[0:nq, r, :, :], o[:, :, 0:HD],
                                                      rden[0:nq, r, :].unsqueeze(2).to_broadcast([nq, H, HD]), ALU.mult))

                def oT_copy(q0, nq):
                    v.wait_ge(oturn.sem, oturn.at(s, oT_sb.n + 1))
                    oT_sb.inc(nc.vector.tensor_copy(oT[:, q0:q0 + nq], misc[:, q0:q0 + nq]))

                b0 = bank[0][:, :].rearrange("p (t d) -> p t d", t=T)
                v.wait_ge(projected.sem, projected.at(s, 1))

                def global_values():
                    for h in range(2):
                        ts = slice(2 * h, 2 * h + 2)
                        ins = nc.vector.tensor_tensor(Vg[:, ts, :, 0:HD], qkv2(h, QK, QK + 32).rearrange("p t (g d) -> p t g d", g=KVH),
                                                      small[:, R1, ts].unsqueeze(2).unsqueeze(3).to_broadcast([P, 2, KVH, HD]), ALU.mult)
                    values.inc(ins)

                def local_values():
                    values.inc(nc.vector.tensor_copy(Vl[:, :, :, 0:HD], misc[:, 0:len(LOCAL) * 32].rearrange("p (b g d) -> p b g d", g=KVH, d=HD)))

                powers(rope(0, "g", small[:, EPS1, :], global_values), gating)
                halves(0)
                gate_weights()
                combine(0)
                head_copies()
                for i, (qt, g, kt) in enumerate(GLOBAL_UNITS):
                    if kt == qt:
                        mask(12 + i, i % 4, "causal", P, 0)
                        if qt and g == 0:
                            divide(qt - 1, P, 2 * qt * (qt + 1) - 1)
                        if qt and g == 1:
                            oT_copy((qt - 1) * P, P)
                divide(T - 1, P, 2 * T * (T + 1) - 1)
                oT_copy((T - 1) * P, P)
                v.wait_ge(attn.sem, attn.at(s, 1))
                v.wait_ge(yused.sem, yused.at(s, 3))
                vec.inc(nc.vector.tensor_tensor(x1[:, :, :], xn[:, :, :], b0, ALU.add))
                attn_used.inc(nc.vector.tensor_tensor(acc[:, :, :], acc[:, :, :], b0, ALU.add))
                v.wait_ge(attn_used.sem, attn_used.at(s, 1))
                moments(s, vec, x1)
                chained(nc.vector.tensor_tensor(small[:, SQ, :], mv[:, :, 0], mv[:, :, 0], ALU.mult))
                powers(nc.vector.scalar_tensor_tensor(small[:, MS2, :], small[:, SQ, :], 1e-6, mv[:, :, 1], ALU.add, ALU.add))
                for t in range(T):
                    normed.inc(nc.vector.tensor_scalar(y2[:, t, :], x1[:, t, :], small[:, R2, t:t + 1], None, ALU.mult))
                v.wait_ge(projected.sem, projected.at(s, 2))
                powers(rope(1, "l", None, local_values))
                halves(1)
                combine(1)
                head_copies()
                for i, (b, g) in enumerate(LOCAL_UNITS):
                    q0, nq, k0 = LOCAL[b]
                    mask(64 + i, i % 4, "band", nq, q0 - k0)
                    p0, pn, _ = LOCAL[b - 1]
                    if b and g == 1:
                        divide(b - 1, pn, 40 + 4 * b - 1)
                    if b and g == 3:
                        oT_copy(p0, pn)
                divide(len(LOCAL) - 1, LOCAL[-1][1], 63)
                oT_copy(LOCAL[-1][0], LOCAL[-1][1])
                v.wait_ge(attn.sem, attn.at(s, 2))
                v.wait_ge(yused.sem, yused.at(s, 6))
                attn_used.inc(nc.vector.tensor_tensor(acc[:, :, :], acc[:, :, :], b0, ALU.add))
                v.wait_ge(attn_used.sem, attn_used.at(s, 2))
                v.wait_ge(cw_turn.sem, cw_turn.at(s, 1))
                cwT_sb.inc(nc.vector.tensor_copy(cwT[:, :], misc[0:E + 1, :]))
                combine(2)
                v.wait_ge(bias2.sem, bias2.at(s, 1))
                v.wait_ge(yused.sem, yused.at(s, 9))
                xnew.inc(nc.vector.tensor_tensor(acc[:, :, :], acc[:, :, :], misc[:, :].rearrange("p (t d) -> p t d", t=T), ALU.add))
                assert vec.n == VEC_PER, vec.n

            with v.Fori(0, seqs) as s:
                def chained(ins):
                    l_vec.inc(ins)
                    v.wait_ge(l_vec.sem, l_vec.at(s, l_vec.n))
                wide = lambda z: z.unsqueeze(2).to_broadcast([P, T, E])
                v.wait_ge(l_loaded.sem, l_loaded.at(s, 16))
                moments(s, l_vec, x)
                l_pow_in.inc(nc.vector.tensor_scalar(small[:, VE, :], mv[:, :, 1], 1e-5, None, ALU.add))
                v.wait_ge(l_pow_out.sem, l_pow_out.at(s, 1))
                v.wait_ge(xn1_stored.sem, xn1_stored.at(s, 16))
                for t in range(T):
                    l_normed.inc(nc.vector.tensor_scalar(xn[:, t, :], x[:, t, :], mv[:, t, 0:1], small[:, RSTD, t:t + 1],
                                                         ALU.subtract, ALU.mult))
                v.wait_ge(l_proj.sem, l_proj.at(s, 1))
                chained(nc.vector.tensor_tensor(lg[:, :, :], bank[5][:, 0:T * E].rearrange("p (t e) -> p t e", e=E),
                                                router_b[:, :].unsqueeze(1).to_broadcast([P, T, E]), ALU.add))
                top2(chained, lg)
                l_gate_in.inc(nc.vector.tensor_tensor(gd[:, 0, :], gm[:, 1, :], gm[:, 0, :], ALU.subtract))
                chained(nc.vector.tensor_tensor(chosen[:, :, :], oh[:, 0, :, :], oh[:, 1, :, :], ALU.add))
                chained(nc.vector.tensor_copy(before_t[:, 0, :], before_t[:, T, :]))
                for t in range(T):
                    ins = nc.vector.tensor_tensor(before_t[:, t + 1, :], before_t[:, t, :], chosen[:, t, :], ALU.add)
                    (l_chosen.inc if t == T - 1 else chained)(ins)
                for i in range(2):
                    v.wait_ge(l_proj.sem, l_proj.at(s, 2 + i))
                    for h, tab in ((0, "cos1"), (1, "sin1")):
                        l_vec.inc(nc.vector.tensor_tensor(rot[:, i, h, :], bank[2 * i + h][:, :], const(tab), ALU.mult))
                    v.wait_ge(l_vec.sem, l_vec.at(s, l_vec.n))
                    l_rotated.inc(nc.vector.tensor_tensor(qk_turned[:, i, :], rot[:, i, 0, :], rot[:, i, 1, :], ALU.add))
                v.wait_ge(l_gate_exp.sem, l_gate_exp.at(s, 1))
                chained(nc.vector.tensor_scalar(gw[:, 0, :], gd[:, 1, :], 1.0, None, ALU.add))
                chained(nc.vector.reciprocal(gw[:, 0, :], gw[:, 0, :]))
                chained(nc.vector.tensor_tensor(gw[:, 1, :], gw[:, 0, :], gd[:, 1, :], ALU.mult))
                for k in range(2):
                    chained(nc.vector.tensor_copy(entry[:, k, :, 0], tok[:, :]))
                    chained(nc.vector.tensor_copy(entry[:, k, :, 1], gw[:, k, :]))
                v.wait_ge(l_rank.sem, l_rank.at(s, 1))
                chained(nc.vector.tensor_copy(rank[:, :, :], bank[6][:, 0:T * E].rearrange("p (t e) -> p t e", e=E)))
                for k in range(2):
                    vec_n = l_vec.n
                    l_vec.inc(nc.vector.tensor_tensor(rsel[:, k, 0, :, :], oh[:, k, :, :], rank[:, :, :], ALU.mult))
                    chained(nc.vector.tensor_tensor(rsel[:, k, 1, :, :], oh[:, k, :, :], const("base").unsqueeze(1).to_broadcast([P, T, E]), ALU.mult))
                chained(nc.vector.tensor_reduce(rk[:, :, :, :].rearrange("p a b t -> p (a b t)"),
                                                rsel[:, :, :, :, :].rearrange("p a b t e -> p (a b t) e"), AX.X, ALU.add))
                chained(nc.vector.tensor_tensor(rk[:, :, 1, :], rk[:, :, 1, :], rk[:, :, 0, :], ALU.add))
                chained(nc.vector.tensor_scalar(rk[:, :, 0, :], rk[:, :, 0, :], float(CAP), 1.0e6, ALU.is_ge, ALU.mult))
                l_entries.inc(nc.vector.tensor_tensor(slot[:, :, :], rk[:, :, 1, :], rk[:, :, 0, :], ALU.add))

                def peak(qt):
                    n = (qt + 1) * P
                    sc = bank[qt % 2]
                    v.wait_ge(l_scores.sem, l_scores.at(s, qt + 1))
                    chained(nc.vector.tensor_tensor(sc[:, n - P:n], sc[:, n - P:n], const("negmask"), ALU.add))
                    chained(nc.vector.tensor_reduce(top[:, 0, qt:qt + 1], sc[:, 0:n], AX.X, ALU.max))
                    l_max.inc(nc.vector.tensor_scalar(top[:, 1, qt:qt + 1], top[:, 0, qt:qt + 1], -L1_SCALE, None, ALU.mult))

                def probs_copy(qt):
                    v.wait_ge(l_prT.sem, l_prT.at(s, qt + 1))
                    n = (qt + 1) * P
                    l_prT_sb.inc(nc.vector.tensor_copy(prT[:, qt % 2, :, :].rearrange("p t n -> p (t n)")[:, 0:n], bank[2 + qt % 2][:, 0:n]))

                def finish(qt):
                    chained(nc.vector.reciprocal(psums[:, 1, qt:qt + 1], psums[:, 0, qt:qt + 1]))
                    v.wait_ge(l_pv.sem, l_pv.at(s, qt + 1))
                    if qt == 0:
                        v.wait_ge(out_stored.sem, out_stored.at(s, 16))
                    ins = nc.vector.scalar_tensor_tensor(acc[:, qt, :], bank[6 + qt % 2][:, 0:P], psums[:, 1, qt:qt + 1], x[:, qt, :], ALU.mult, ALU.add)
                    l_out.inc(ins)
                    if qt == T - 1:
                        l_free.inc(nc.vector.tensor_copy(small[:, 9, :], small[:, 9, :]))
                peak(0)
                peak(1)
                probs_copy(0)
                peak(2)
                finish(0)
                probs_copy(1)
                peak(3)
                finish(1)
                probs_copy(2)
                finish(2)
                probs_copy(3)
                finish(3)

            v.wait_ge(table_in, 16)
            nc.vector.tensor_scalar(tclip[:, :], table[:, :, 0], float(tokens - 1), None, ALU.min).then_inc(e_vec, 1)
            nc.vector.tensor_copy(add_at[:, :], table[:, :, 0]).then_inc(e_vec, 1)
            v.wait_ge(e_vec, 2)
            nc.vector.tensor_copy(gather_at[:, :], tclip[:, :]).then_inc(e_index, 1)
            def gate(e):
                v.wait_ge(e_turned, e + 1)
                if e >= 2:
                    v.wait_ge(e_hidden, e - 1)
                nc.vector.tensor_copy(xgT[:, e % 2, :], bank[e % 2][:, 0:CAP]).then_inc(e_turned_sb, 1)

            def product(e):
                v.wait_ge(e_sig, e + 1)
                flat = lambda z: z[:, e % 2, :, :].rearrange("p c n -> p (c n)")
                nc.vector.tensor_tensor(flat(sig), bank[4 + e % 2][:, :], flat(sig), ALU.mult).then_inc(e_vec, 1)
                v.wait_ge(e_vec, 3 + e)
                if e >= 2:
                    v.wait_ge(e_y, e - 1)
                nc.vector.tensor_tensor(flat(gT), bank[2 + e % 2][:, :], flat(sig), ALU.mult).then_inc(e_gated, 1)

            def weigh(e):
                v.wait_ge(e_y, e + 1)
                for c in range(CC):
                    ins = nc.vector.tensor_scalar(yo[:, CC * e + c, :], bank[6 + e % 2][:, c * P:(c + 1) * P], table[:, CC * e + c, 1:2], None, ALU.mult)
                ins.then_inc(e_yo, 1)
            gate(0)
            for e in range(E):
                if e + 1 < E:
                    gate(e + 1)
                product(e)
                weigh(e)

        @block.tensor
        def _(pe):
            pe.wait_ge(weights_in, WEIGHT_LOADS * 16)
            nc.tensor.transpose(bank[0][0:LAT, 0:P], kv_down[:, :], ident).then_inc(setup_pe, 1)
            pe.wait_ge(setup_dve, 8)
            nc.tensor.matmul(bank[1][:, 0:64], kv_downT[:, :], kv_up[:, :], start=True, stop=True).then_inc(setup_pe, 1)
            for i in range(3):
                nc.tensor.transpose(bank[2 + i][:, 0:P], l1_raw[:, i, :], ident).then_inc(setup_pe, 1)
            pe.wait_ge(setup_dve, 18)
            with pe.Fori(0, seqs) as s:
                def turn(i, src, dst_bank):
                    for t in range(T):
                        pe.wait_ge(normed.sem, normed.at(s, normed_n[0] + 1))
                        normed_n[0] += 1
                        ins = nc.tensor.transpose(dst_bank[:, t * P:(t + 1) * P], src[:, t, :], ident)
                    turned.inc(ins)
                normed_n = [0]

                def turn_heads(i):
                    pe.wait_ge(stacked.sem, stacked.at(s, i + 1))
                    for t in range(T):
                        if t == T - 1:
                            pe.wait_ge(heads.sem, heads.at(s, T * i + 1))
                        for b in range(J + 1):
                            ins = nc.tensor.transpose(as16(ring[t % 3])[:, b, :],
                                                      stack[:, t, b * KVH:(b + 1) * KVH, :, :].rearrange("p g s d -> p (g s d)"),
                                                      ident16[:, :])
                        stackT.inc(ins)
                    pe.wait_ge(heads.sem, heads.at(s, T * (i + 1)))
                    pe.wait_ge(values.sem, values.at(s, i + 1))

                def hidden(n, e):
                    for c in range(HC):
                        use = filled.n
                        if use >= 3:
                            pe.wait_ge(evac.sem, evac.at(s, use - 2))
                        filled.inc(nc.tensor.matmul(ring[use % 3][:, :], w1[:, e, c * P:(c + 1) * P], xnT[:, :], start=True, stop=True))
                    hidden_at[n] = filled.n
                hidden_at = {}

                def second(n, e):
                    pe.wait_ge(evac.sem, evac.at(s, hidden_at[n]))
                    if n >= 2:
                        pe.wait_ge(yused.sem, yused.at(s, n - 1))
                    for t in range(T):
                        for c in range(HC):
                            ins = nc.tensor.matmul(obank[n % 2][:, t * P:(t + 1) * P], hidT[:, n % 2, c, t * P:(t + 1) * P],
                                                   w2[:, e, c, :], start=(c == 0), stop=(c == HC - 1))
                    ypsum.inc(ins)

                def experts(group):
                    es = [(3 * group + k, e) for k, e in enumerate(EXPERTS[group])]
                    hidden(*es[0])
                    for k in range(1, len(es)):
                        hidden(*es[k])
                        second(*es[k - 1])
                    second(*es[-1])

                def scores(n_of, g, keys, k_off, q0, nq):
                    use = filled.n
                    if use >= 3:
                        pe.wait_ge(evac.sem, evac.at(s, use - 2))
                    r = slice(32 * g, 32 * g + 32)
                    filled.inc(nc.tensor.matmul(ring[use % 3][:, 0:J * nq], QKT[r, J, k_off:k_off + P],
                                                QKT[r, 0:J, q0:q0 + nq], start=True, stop=True))

                def values_product(unit, first_use, g, nq, V, blk, first, mask_n):
                    if mask_n is None:
                        pe.wait_ge(evac.sem, evac.at(s, first_use + 1))
                    else:
                        pe.wait_ge(masked.sem, masked.at(s, mask_n))
                    for j in range(J):
                        h = J * g + j
                        ins = nc.tensor.matmul(obank[blk % 2][0:nq, h * VD:(h + 1) * VD],
                                               probs[:, unit % 4, j * nq:(j + 1) * nq], V,
                                               start=(first and j == 0), stop=True, skip_group_check=True)
                    pv.inc(ins)

                def turn_out(blk, q0, nq):
                    pe.wait_ge(otoks.sem, otoks.at(s, oturn.n + 1))
                    o = otok[0:nq, blk % 2, :, :].rearrange("p h d -> p (h d)")
                    if nq > 32:
                        ins = nc.tensor.transpose(misc[:, q0:q0 + nq], o, ident[0:nq, 0:nq])
                    else:
                        ins = nc.tensor.matmul(misc[:, q0:q0 + nq], o, ident[0:nq, 0:nq], start=True, stop=True)
                    oturn.inc(ins)

                def project_out(t, w, upto):
                    pe.wait_ge(oT_sb.sem, oT_sb.at(s, upto))
                    return nc.tensor.matmul(bank[0][:, t * P:(t + 1) * P], oT[:, t * P:(t + 1) * P], w[:, :], start=True, stop=True)

                turn(0, xn, misc)
                pe.wait_ge(turned_sb.sem, turned_sb.at(s, 1))
                for t in range(T):
                    ins = nc.tensor.matmul(qkv(t, 0, QK + 32 + E), xnT[:, t * P:(t + 1) * P], wg[:, :], start=True, stop=True)
                projected.inc(ins)
                experts(0)
                turn_heads(0)
                pe.wait_ge(yused.sem, yused.at(s, 3))
                U = GLOBAL_UNITS
                masks = [0]
                for i in range(2):
                    scores(i, U[i][1], None, U[i][2] * P, U[i][0] * P, P)
                base = filled.n - 2
                since = {}
                for i, (qt, g, kt) in enumerate(U):
                    if i + 2 < len(U):
                        q2, g2, k2 = U[i + 2]
                        scores(i + 2, g2, None, k2 * P, q2 * P, P)
                    first = g == 0 and kt == 0
                    if first and qt >= 2:
                        pe.wait_ge(otoks.sem, otoks.at(s, qt - 1))
                    if kt == qt:
                        masks[0] += 1
                    values_product(i, base + i, g, P, Vg[:, kt, g, :], qt, first, masks[0] if kt == qt else None)
                    if qt and (g, kt) == (1, 0):
                        turn_out(qt - 1, (qt - 1) * P, P)
                    if qt and (g, kt) == (2, 1):
                        project_out(qt - 1, wo_g, qt)
                turn_out(T - 1, (T - 1) * P, P)
                attn.inc(project_out(T - 1, wo_g, T))

                turn(1, y2, misc)
                pe.wait_ge(turned_sb.sem, turned_sb.at(s, 2))
                pe.wait_ge(attn_used.sem, attn_used.at(s, 1))
                for t in range(T):
                    nc.tensor.matmul(qkv(t, 0, QK), y2T[:, t * P:(t + 1) * P], wl[:, 0:QK], start=True, stop=True)
                for b, (q0, nq, k0) in enumerate(LOCAL):
                    ins = nc.tensor.matmul(misc[:, b * 32:(b + 1) * 32], y2T[:, k0:k0 + P], wl[:, QK:QK + 32], start=True, stop=True)
                projected.inc(ins)
                experts(1)
                turn_heads(1)
                pe.wait_ge(yused.sem, yused.at(s, 6))
                U = LOCAL_UNITS
                for i in range(2):
                    q0, nq, k0 = LOCAL[U[i][0]]
                    scores(i, U[i][1], None, k0, q0, nq)
                base = filled.n - 2
                for i, (b, g) in enumerate(U):
                    if i + 2 < len(U):
                        q0, nq, k0 = LOCAL[U[i + 2][0]]
                        scores(i + 2, U[i + 2][1], None, k0, q0, nq)
                    q0, nq, k0 = LOCAL[b]
                    if g == 0 and b >= 2:
                        pe.wait_ge(otoks.sem, otoks.at(s, T + b - 1))
                    values_product(i, base + i, g, nq, Vl[:, b, g, :], b, g == 0, 4 * T + i + 1)
                    if b and g == 2:
                        p0, pn, _ = LOCAL[b - 1]
                        turn_out(b - 1, p0, pn)
                p0, pn, _ = LOCAL[-1]
                turn_out(len(LOCAL) - 1, p0, pn)
                for t in range(T):
                    ins = project_out(t, wo_l, T + len(LOCAL))
                attn.inc(ins)
                pe.wait_ge(cw_ready.sem, cw_ready.at(s, 1))
                for t in range(T):
                    ins = nc.tensor.matmul(misc[0:E + 1, t * P:(t + 1) * P], cw[:, t, :], ident, start=True, stop=True)
                cw_turn.inc(ins)
                experts(2)
                pe.wait_ge(cwT_sb.sem, cwT_sb.at(s, 1))
                for t in range(T):
                    ins = nc.tensor.matmul(misc[:, t * P:(t + 1) * P], cwT[:, t * P:(t + 1) * P], b2[:, :], start=True, stop=True)
                bias2.inc(ins)

            pe.wait_ge(xnew.sem, xnew.per * seqs)
            with pe.Fori(0, seqs) as s:
                for t in range(T):
                    pe.wait_ge(l_normed.sem, l_normed.at(s, t + 1))
                    ins = nc.tensor.transpose(misc[:, t * P:(t + 1) * P], xn[:, t, :], ident)
                l_turned.inc(ins)
                pe.wait_ge(l_turned_sb.sem, l_turned_sb.at(s, 1))
                for t in range(T):
                    ins = nc.tensor.matmul(bank[5][:, t * E:(t + 1) * E], xnT[:, t * P:(t + 1) * P], router[:, :], start=True, stop=True)
                l_proj.inc(ins)
                for i in range(2):
                    for h in range(2):
                        ins = nc.tensor.matmul(bank[2 * i + h][:, :], wqk1[:, 2 * i + h, :], xnT[:, :], start=True, stop=True)
                    l_proj.inc(ins)
                for t in range(T):
                    ins = nc.tensor.matmul(bank[4][:, t * P:(t + 1) * P], xnT[:, t * P:(t + 1) * P], wv1[:, :], start=True, stop=True)
                l_proj.inc(ins)
                pe.wait_ge(l_chosen.sem, l_chosen.at(s, 1))
                r = bank[6][:, 0:T * E]
                nc.tensor.matmul(r, const("before"), chosen[:, :, :].rearrange("p t e -> p (t e)"), start=True, stop=False)
                l_rank.inc(nc.tensor.matmul(r, const("ones"), before_t[:, 0:T, :].rearrange("p t e -> p (t e)"), start=False, stop=True))

                def scores1(qt):
                    n = (qt + 1) * P
                    if qt == 0:
                        pe.wait_ge(l_rotated.sem, l_rotated.at(s, 2))
                    if qt >= 2:
                        pe.wait_ge(l_exp.sem, l_exp.at(s, qt - 1))
                    l_scores.inc(nc.tensor.matmul(bank[qt % 2][:, 0:n], qk_turned[:, 0, qt * P:(qt + 1) * P], qk_turned[:, 1, 0:n], start=True, stop=True))

                def turn_probs(qt):
                    pe.wait_ge(l_exp.sem, l_exp.at(s, qt + 1))
                    if qt >= 2:
                        pe.wait_ge(l_prT_sb.sem, l_prT_sb.at(s, qt - 1))
                    for k in range(qt + 1):
                        ins = nc.tensor.transpose(bank[2 + qt % 2][:, k * P:(k + 1) * P], pr1[:, qt % 2, k * P:(k + 1) * P], ident)
                    l_prT.inc(ins)

                def pv1(qt):
                    if qt == 0:
                        pe.wait_ge(l_v1.sem, l_v1.at(s, 1))
                        pe.wait_ge(l_entries.sem, l_entries.at(s, 1))
                    if qt >= 2:
                        pe.wait_ge(l_out.sem, l_out.at(s, qt - 1))
                    pe.wait_ge(l_prT_sb.sem, l_prT_sb.at(s, qt + 1))
                    for k in range(qt + 1):
                        ins = nc.tensor.matmul(bank[6 + qt % 2][:, 0:P], prT[:, qt % 2, k, :], v1[:, k, :], start=(k == 0), stop=(k == qt))
                    l_pv.inc(ins)
                scores1(0)
                scores1(1)
                turn_probs(0)
                scores1(2)
                pv1(0)
                turn_probs(1)
                scores1(3)
                pv1(1)
                turn_probs(2)
                pv1(2)
                turn_probs(3)
                pv1(3)

            pe.wait_ge(l_out.sem, l_out.per * seqs)

            def turn_rows(e):
                if e >= 2:
                    pe.wait_ge(e_turned_sb, e - 1)
                pe.wait_ge(e_gathered[e], 16 * CC)
                for c in range(CC):
                    ins = nc.tensor.transpose(bank[e % 2][:, c * P:(c + 1) * P], xg[:, CC * e + c, :], ident)
                ins.then_inc(e_turned, 1)

            def hidden1(e):
                pe.wait_ge(e_turned_sb, e + 1)
                if e >= 2:
                    pe.wait_ge(e_gated, e - 1)
                for w, b in ((w_a, bank[2 + e % 2]), (w_b, bank[4 + e % 2])):
                    for c in range(HC1):
                        ins = nc.tensor.matmul(b[:, c * CAP:(c + 1) * CAP], w[:, e, c * P:(c + 1) * P], xgT[:, e % 2, :], start=True, stop=True)
                ins.then_inc(e_hidden, 1)

            def out1(e):
                pe.wait_ge(e_gated, e + 1)
                if e >= 2:
                    pe.wait_ge(e_yo, e - 1)
                for c in range(CC):
                    for k in range(HC1):
                        ins = nc.tensor.matmul(bank[6 + e % 2][:, c * P:(c + 1) * P], gT[:, e % 2, k, c * P:(c + 1) * P], w_o[:, e, k, :],
                                               start=(k == 0), stop=(k == HC1 - 1))
                ins.then_inc(e_y, 1)
            turn_rows(0)
            hidden1(0)
            for e in range(E):
                if e + 1 < E:
                    turn_rows(e + 1)
                    hidden1(e + 1)
                out1(e)

        for g in S.values():
            if g.n and g.n != g.per:
                print("SIGNAL", g.name, g.n, g.per)


_INS = ['L0_attn_norm1_w', 'L0_attn_norm2_w', 'L0_attn_g_wq', 'L0_attn_g_kv_down', 'L0_attn_g_k_up',
        'L0_attn_g_v_up', 'L0_attn_g_wo', 'L0_attn_l_wq', 'L0_attn_l_wk', 'L0_attn_l_wv', 'L0_attn_l_wo',
        'L0_ffn_gate_w', 'L0_ffn_gate_b', 'L0_ffn_w1', 'L0_ffn_b1', 'L0_ffn_w2', 'L0_ffn_b2', 'L0_ffn_ws1',
        'L0_ffn_bs1', 'L0_ffn_ws2', 'L0_ffn_bs2', 'L1_attn_w_q', 'L1_attn_w_k', 'L1_attn_w_v',
        'L1_ffn_router_w', 'L1_ffn_router_b', 'L1_ffn_W', 'L1_ffn_V', 'L1_ffn_W_out']


def kernel(**inputs):
    import numpy as _np
    import concourse.bacc as _bacc
    from concourse import mybir as _mybir
    from concourse.bass_utils import run_bass_kernel_spmd as _run

    nc = _bacc.Bacc("TRN2", target_bir_lowering=False, num_devices=1)
    arrays, aps = {}, {}

    def given(name, key, v):
        arrays[name] = v
        aps[key] = nc.dram_tensor(name, v.shape, _mybir.dt.from_np(v.dtype), kind="ExternalInput").ap()
    given("x_dram", "x", _np.ascontiguousarray(inputs["L0_attn_hidden"]))
    given("shape_constants_dram", "shape_constants", shape_constants())
    given("zero_rows_dram", "zero_rows", _np.zeros((SLOTS, D), _np.float32))
    for n in _INS:
        given(f"in_{n}_dram", n, _np.ascontiguousarray(inputs[n]))
    out = nc.dram_tensor("out_0_dram", [TOKENS + SLOTS, D], _mybir.dt.float32, kind="ExternalOutput").ap()
    program(nc, aps, out)
    r = _run(nc, [arrays], core_ids=[0])
    return r.results[0]["out_0_dram"][0:TOKENS].reshape(SEQS, LEN, D)
```

```python
import numpy as np
import concourse.bass as bass
from concourse import mybir
from contextlib import ExitStack

F32 = mybir.dt.float32
F16 = mybir.dt.float16
BF16 = mybir.dt.bfloat16
I32 = mybir.dt.int32
ALU = mybir.AluOpType
ACT = mybir.ActivationFunctionType
AX = mybir.AxisListType

P = 128
SEQS, LEN, D = 16, 512, 128
T = LEN // P
TOKENS = SEQS * LEN
H, KVH = 16, 4
HD = D // H
J = H // KVH
QK = (H + KVH) * HD
LAT, WIN = 32, 32
E, HID = 8, 512
HC = HID // P
TOPK = 2
CAP = 2 * (2 * 256) * TOPK // 8
HID1 = 256
HC1 = HID1 // P
CC = CAP // P
SLOTS = E * CAP
VD = HD + 1
ATT_SCALE = 1.0 / float(np.sqrt(np.float32(HD)))
L1_SCALE = 1.0 / float(np.sqrt(np.float32(D)))
BIG = 1.0e30
NEG = -30000.0
LIFT = 7.0
PARTS = 3

LOCAL = [(0, 96, 0), (96, 96, 64), (192, 96, 160), (288, 96, 256), (384, 96, 352), (480, 32, 384)]
GLOBAL_UNITS = [(qt, g, kt) for qt in range(T) for g in range(KVH) for kt in range(qt + 1)]
LOCAL_UNITS = [(b, g) for b in range(len(LOCAL)) for g in range(KVH)]
EXPERTS = [[E, 0, 1], [2, 3, 4], [5, 6, 7]]

CONST = {}
_at = 0
for _n, _w in [("ident", P), ("negmask", P), ("before", P), ("ones", P),
               ("cos_g", T * HD), ("sin_g", T * HD // 2), ("nsin_g", T * HD // 2),
               ("cos_l", T * HD), ("sin_l", T * HD // 2), ("nsin_l", T * HD // 2),
               ("negcausal", P), ("negband", P), ("cos1", LEN), ("sin1", LEN), ("iota", E), ("base", E), ("tok", T), ("len", T), ("half", T), ("dump", SLOTS // P * 2)]:
    CONST[_n] = (_at, _at + _w)
    _at += _w
NCONST = _at
WEIGHT_LOADS = 33


def shape_constants():
    f = np.float32
    c = np.zeros((P, NCONST), f)

    def put(name, x):
        a, b = CONST[name]
        c[:, a:b] = np.broadcast_to(np.asarray(x, f).reshape(-1, b - a), (P, b - a))

    i = np.arange(P)
    put("ident", np.eye(P))
    put("negcausal", np.where(i[:, None] <= i[None, :], 0.0, NEG))
    put("negband", np.where((i[None, :] - i[:, None] >= 0) & (i[None, :] - i[:, None] < WIN), 0.0, NEG))
    put("negmask", np.where(i[None, :] <= i[:, None], 0.0, -BIG))
    put("before", i[:, None] < i[None, :])
    put("ones", np.ones((P, P)))
    for n, base in (("g", 1000000.0), ("l", 10000.0)):
        inv = (f(1.0) / (f(base) ** (np.arange(0, HD, 2, dtype=f) / f(HD)))).astype(f)
        ang = (np.arange(LEN, dtype=f)[:, None] * inv[None, :]).astype(f).astype(np.float64)
        cos, sin = np.cos(ang), np.sin(ang)
        tiles = lambda x: x.reshape(T, P, -1).transpose(1, 0, 2).reshape(P, -1)
        put("cos_" + n, tiles(np.repeat(cos, 2, axis=1)))
        put("sin_" + n, tiles(sin))
        put("nsin_" + n, tiles(-sin))
    theta = np.power(f(10000.0), (f(-2.0) * (np.arange(D // 2, dtype=f) - f(1.0)) / f(D)).astype(f)).astype(f)
    ang = (np.arange(LEN, dtype=f)[:, None] * theta[None, :]).astype(f).astype(np.float64)
    put("cos1", np.repeat(np.cos(ang), 2, axis=1).T)
    put("sin1", (np.repeat(np.sin(ang), 2, axis=1) * np.tile([1.0, -1.0], D // 2)).T)
    put("iota", np.arange(E))
    put("base", np.arange(E) * CAP)
    put("tok", i[:, None] + P * np.arange(T)[None, :])
    put("len", np.full(T, LEN))
    put("half", np.full(T, -0.5))
    d = np.zeros((P, SLOTS // P, 2))
    d[:, :, 0] = TOKENS + i[:, None] + P * np.arange(SLOTS // P)[None, :]
    put("dump", d.reshape(P, -1))
    return c




RING_USES = 36 + len(GLOBAL_UNITS) + len(LOCAL_UNITS)
UNITS = len(GLOBAL_UNITS) + len(LOCAL_UNITS)
ENDS = [2 * (q + 1) * (q + 2) - 1 for q in range(T)]
SECOND_G = [4 + 3 * k for k in range(12)]
COMBINE_G = [i + 2 for i in SECOND_G]
SECOND_L = [2 * k + 1 for k in range(11)]
COMBINE_L = [i + 2 for i in SECOND_L]
LN_STEPS, VEC_STEPS, L_STEPS, SETUP_A, SETUP_B = 14, 114, 57, 11, 21


def program(nc, a, out, seqs=SEQS, dbg=None):
    ctx = ExitStack()
    with ctx, nc.allow_non_contiguous_dma("weights are laid out once"):
        def sb(name, shape, dt=F32):
            return ctx.enter_context(nc.sbuf_tensor(name, shape, dt))

        def sem(name):
            return ctx.enter_context(nc.semaphore(name))

        def scratch(name, shape):
            return nc.dram_tensor(name, shape, F32, kind="Internal").ap()

        tokens = seqs * LEN
        xn1_d = scratch("xn1_d", [tokens, D])
        slot_d = scratch("slot_d", [SLOTS, 2])

        consts = sb("consts", [P, NCONST])

        def const(name):
            return consts[:, CONST[name][0]:CONST[name][1]]
        ident = const("ident")
        ident16 = sb("ident16", [P, P], F16)
        masks16 = sb("masks16", [P, 2, P], F16)
        lift = sb("lift", [P, 1])
        w1 = sb("w1", [P, E + 1, HID])
        w2 = sb("w2", [P, E + 1, HC, D])
        b1 = sb("b1", [P, E + 1, HC])
        b2 = sb("b2", [E + 1, D])
        gate_b = sb("gate_b", [P, E])
        wg_raw = sb("wg_raw", [P, D])
        wl_raw = sb("wl_raw", [P, D + 64])
        norm1 = sb("norm1", [P, 1])
        norm2 = sb("norm2", [P, 1])
        kv_down = sb("kv_down", [P, LAT])
        kv_downT = sb("kv_downT", [LAT, P])
        kv_up = sb("kv_up", [LAT, 64])
        wg = sb("wg", [P, QK + 32 + E])
        wl = sb("wl", [P, QK + 32])
        wo_g = sb("wo_g", [P, D])
        wo_l = sb("wo_l", [P, D])
        l1_raw = sb("l1_raw", [P, 3, D])
        wqk1 = sb("wqk1", [P, 4, D])
        wv1 = sb("wv1", [P, D])
        router = sb("router", [P, E])
        router_b = sb("router_b", [P, E])
        w_a = sb("w_a", [P, E, HID1])
        w_b = sb("w_b", [P, E, HID1])
        w_o = sb("w_o", [P, E, HC1, D])

        x = sb("x", [P, T, D])
        xn = sb("xn", [P, T, D])
        x1 = sb("x1", [P, T, D])
        y2 = sb("y2", [P, T, D])
        acc = sb("acc", [P, T, D])
        xnT = sb("xnT", [P, LEN])
        y2T = sb("y2T", [P, LEN])
        stats = sb("stats", [P, T, 6])
        mv = sb("mv", [P, T, 2])
        small = sb("small", [P, 12, T])
        VE, RSTD, E1, R1, EPS1, MS2, R2, SQ = range(8)
        NH = T * (H + KVH)
        t1 = sb("t1", [P, T, QK])
        t2 = sb("t2", [P, T, QK])
        msum = sb("msum", [P, NH])
        rq = sb("rq", [P, NH])
        rt = sb("rt", [P, 2, NH])
        qn = sb("qn", [P, T, QK])
        stack = sb("stack", [P, T, H + KVH, 4, HD], F16)
        QKT = sb("QKT", [P, J + 1, LEN], F16)
        vf = sb("vf", [P, 2, len(LOCAL), KVH, HD])
        V3 = sb("V3", [P, len(LOCAL), KVH, PARTS, VD], BF16)
        probs = sb("probs", [P, 4, LEN])
        hi16 = sb("hi16", [P, 4, LEN], F16)
        lo16 = sb("lo16", [P, 4, LEN], F16)
        hidT = sb("hidT", [P, 3, HC, LEN])
        osum = sb("osum", [P, 2, H, VD])
        rden = sb("rden", [P, 2, H])
        otok = sb("otok", [P, 2, H, HD])
        oT = sb("oT", [P, LEN])
        lg = sb("lg", [P, T, E])
        gk = sb("gk", [P, T, E])
        l2 = sb("l2", [P, T, E])
        oh = sb("oh", [P, 2, T, E])
        km = sb("km", [P, 2, T])
        gm = sb("gm", [P, 2, T])
        gd = sb("gd", [P, 2, T])
        gw = sb("gw", [P, 2, T])
        cw = sb("cw", [P, T, E + 1])
        cwT = sb("cwT", [E + 1, LEN])
        xl = sb("xl", [P, T, D])
        xn1 = sb("xn1", [P, T, D])
        xn1T = sb("xn1T", [P, LEN])
        out_sb = sb("out_sb", [P, T, D])
        qk_turned = sb("qk_turned", [P, 2, LEN])
        rot = sb("rot", [P, 2, 2, LEN])
        v1 = sb("v1", [P, T, D])
        pr1 = sb("pr1", [P, 2, LEN])
        prT = sb("prT", [P, 2, T, P])
        top = sb("top", [P, 2, T])
        psums = sb("psums", [P, 2, T])
        oh1 = sb("oh1", [P, 2, T, E])
        gd1 = sb("gd1", [P, 2, T])
        chosen = sb("chosen", [P, T, E])
        before_t = sb("before_t", [P, T + 1, E])
        rank = sb("rank", [P, T, E])
        rsel = sb("rsel", [P, 2, 2, T, E])
        rk = sb("rk", [P, 2, 2, T])
        tok = sb("tok", [P, T])
        entry = sb("entry", [P, 2, T, 2])
        slot = sb("slot", [P, 2, T], I32)
        table = sb("table", [P, E * CC, 2])
        gather_at = sb("gather_at", [P, E * CC], I32)
        add_at = sb("add_at", [P, E * CC], I32)
        tclip = sb("tclip", [P, E * CC])
        xgT = sb("xgT", [P, 2, CAP])
        flat = lambda k: hidT[:, k, :, :].rearrange("p c n -> p (c n)")
        xg = flat(0).rearrange("p (c d) -> p c d", d=D)
        yo = flat(1).rearrange("p (c d) -> p c d", d=D)
        sig, gT = (flat(2)[:, h * 2 * HID1 * 2:(h + 1) * 2 * HID1 * 2].rearrange("p (i c n) -> p i c n", i=2, c=HC1) for h in range(2))

        small1 = sb("small1", [P, 2, T])

        bank = [ctx.enter_context(nc.psum_tensor(f"bank{i}", [P, 512], F32)) for i in range(8)]
        abank, ybank = bank[0], bank[1]
        ring = [bank[2], bank[3], bank[4]]
        obank = [bank[5], bank[6]]
        misc = bank[7]
        rot_banks = ((bank[5], bank[6]), (bank[0], bank[7]))

        def qkv(t, lo, hi):
            return bank[t // 2][:, (t % 2) * 256 + lo:(t % 2) * 256 + hi]

        def qkv2(half, lo, hi):
            return bank[half][:, :].rearrange("p (t n) -> p t n", t=2)[:, :, lo:hi]

        def as16(b):
            return b[:, 0:(J + 1) * P // 2].bitcast(F16).rearrange("p (b n) -> p b n", b=J + 1)

        def tiles(b):
            return b[:, :].rearrange("p (t d) -> p t d", t=T)

        S = []

        class Signal:
            def __init__(self, name, per):
                self.sem, self.per, self.name, self.n = sem(name), per, name, 0
                S.append(self)

            def inc(self, ins, by=1):
                self.n += by
                ins.then_inc(self.sem, by)

            def at(self, s, n):
                return s * self.per + n

        def count_anew():
            for g in S:
                assert g.n in (0, g.per), (g.name, g.n, g.per)
                g.n = 0

        weights_in = sem("weights_in")
        setup_dve = sem("setup_dve")
        setup_pe = sem("setup_pe")

        x_loaded = Signal("x_loaded", 16)
        x_free = Signal("x_free", 1)
        ln = Signal("ln", LN_STEPS)
        ln_pow_in = Signal("ln_pow_in", 2)
        ln_pow_out = Signal("ln_pow_out", 2)
        normed = Signal("normed", T)
        vec = Signal("vec", VEC_STEPS)
        pow_in = Signal("pow_in", 1)
        pow_out = Signal("pow_out", 1)
        normed2 = Signal("normed2", T)
        turned = Signal("turned", 2)
        turned_sb = Signal("turned_sb", 2)
        projected = Signal("projected", 2)
        stacked = Signal("stacked", 2)
        stackT = Signal("stackT", 2 * T)
        heads = Signal("heads", 2 * T)
        values = Signal("values", 2)
        filled = Signal("filled", RING_USES)
        evac = Signal("evac", RING_USES)
        lows = Signal("lows", UNITS)
        pv = Signal("pv", UNITS)
        otoks = Signal("otoks", T + 6)
        oturn = Signal("oturn", T + 6)
        oT_sb = Signal("oT_sb", T + 6)
        attn = Signal("attn", 2)
        attn_used = Signal("attn_used", 2)
        ypsum = Signal("ypsum", 9 * T)
        yused = Signal("yused", 9 * T)
        gate_in = Signal("gate_in", 1)
        gate_exp = Signal("gate_exp", 1)
        cw_ready = Signal("cw_ready", 1)
        cw_turn = Signal("cw_turn", 1)
        cwT_sb = Signal("cwT_sb", 1)
        xl_ready = Signal("xl_ready", 1)
        l_vec = Signal("l_vec", L_STEPS)
        l_pow_in = Signal("l_pow_in", 1)
        l_pow_out = Signal("l_pow_out", 1)
        l_normed = Signal("l_normed", T)
        l_turned = Signal("l_turned", 1)
        l_turned_sb = Signal("l_turned_sb", 1)
        l_proj = Signal("l_proj", 4)
        l_lg = Signal("l_lg", 1)
        l_v1 = Signal("l_v1", 1)
        l_rotated = Signal("l_rotated", 2)
        l_gate_in = Signal("l_gate_in", 1)
        l_gate_exp = Signal("l_gate_exp", 1)
        l_chosen = Signal("l_chosen", 1)
        l_rank = Signal("l_rank", 1)
        l_ranked = Signal("l_ranked", 1)
        l_entries = Signal("l_entries", 1)
        tok_next = Signal("tok_next", 1)
        l_scattered = Signal("l_scattered", 16 * 2 * T)
        l_scores = Signal("l_scores", T)
        l_max = Signal("l_max", T)
        l_exp = Signal("l_exp", T)
        l_prT = Signal("l_prT", T)
        l_prT_sb = Signal("l_prT_sb", T)
        l_pv = Signal("l_pv", T)
        l_out = Signal("l_out", T)
        xn1_stored = Signal("xn1_stored", 16)
        out_stored = Signal("out_stored", 16)
        table_in = sem("table_in")
        e_vec = sem("e_vec")
        e_index = sem("e_index")
        e_gathered = [sem(f"e_gathered{e}") for e in range(E)]
        e_turned = sem("e_turned")
        e_turned_sb = sem("e_turned_sb")
        e_hidden = sem("e_hidden")
        e_sig = sem("e_sig")
        e_gated = sem("e_gated")
        e_y = sem("e_y")
        e_yo = sem("e_yo")
        e_added = sem("e_added")

        block = ctx.enter_context(nc.Block())

        def sequences(eng, body):
            count_anew()
            body(0, True, False)
            count_anew()
            if seqs > 1:
                with eng.Fori(1, seqs) as s:
                    body(s, True, True)
                count_anew()
            body(seqs, False, True)
            count_anew()

        @block.sync
        def _(sp):
            n = [0]

            def load(dst, src):
                sp.dma_start(dst, src).then_inc(weights_in, 16)
                n[0] += 1
            x_by_seq = a["x"].rearrange("s (t p) d -> s p t d", p=P)
            sp.dma_start(x[:, :, :], x_by_seq[0]).then_inc(x_loaded.sem, 16)
            load(consts[:, :], a["shape_constants"])
            load(norm1[:, 0:1], a["L0_attn_norm1_w"].rearrange("(p o) -> p o", o=1))
            load(norm2[:, 0:1], a["L0_attn_norm2_w"].rearrange("(p o) -> p o", o=1))
            load(wg_raw[:, :], a["L0_attn_g_wq"])
            load(kv_down[:, :], a["L0_attn_g_kv_down"])
            load(kv_up[:, 0:32], a["L0_attn_g_k_up"])
            load(kv_up[:, 32:64], a["L0_attn_g_v_up"])
            load(wl_raw[:, 0:D], a["L0_attn_l_wq"])
            load(wl_raw[:, D:D + 32], a["L0_attn_l_wk"])
            load(wl_raw[:, D + 32:D + 64], a["L0_attn_l_wv"])
            load(wo_g[:, :], a["L0_attn_g_wo"])
            load(wo_l[:, :], a["L0_attn_l_wo"])
            load(wg[:, QK + 32:QK + 32 + E], a["L0_ffn_gate_w"])
            load(gate_b[:, :], a["L0_ffn_gate_b"].partition_broadcast(P))
            load(w1[:, 0:E, :], a["L0_ffn_w1"].rearrange("e d h -> d e h"))
            load(w1[:, E, :], a["L0_ffn_ws1"])
            load(w2[:, E, :, :], a["L0_ffn_ws2"].rearrange("(c p) d -> p c d", p=P))
            for e in range(0, E, 4):
                load(w2[:, e:e + 4, :, :].rearrange("p e c d -> p (e c) d"),
                     a["L0_ffn_w2"][e:e + 4].rearrange("e (c p) d -> p (e c) d", p=P))
            load(b1[:, 0:E, :].rearrange("p e c -> p (e c)"), a["L0_ffn_b1"].rearrange("e (c p) -> p (e c)", p=P))
            load(b1[:, E, :], a["L0_ffn_bs1"].rearrange("(c p) -> p c", p=P))
            load(b2[0:E, :], a["L0_ffn_b2"])
            load(b2[E:E + 1, :], a["L0_ffn_bs2"].rearrange("(o d) -> o d", o=1))
            load(slot_d.rearrange("(c p) w -> p c w", p=P), a["shape_constants"][:, CONST["dump"][0]:CONST["dump"][1]].rearrange("p (c w) -> p c w", w=2))
            load(l1_raw[:, 0, :], a["L1_attn_w_q"])
            load(l1_raw[:, 1, :], a["L1_attn_w_k"])
            load(l1_raw[:, 2, :], a["L1_attn_w_v"])
            load(router[:, :], a["L1_ffn_router_w"].rearrange("e d -> d e"))
            load(router_b[:, :], a["L1_ffn_router_b"].partition_broadcast(P))
            load(w_a[:, :, :], a["L1_ffn_W"].rearrange("e d h -> d e h"))
            load(w_b[:, :, :], a["L1_ffn_V"].rearrange("e d h -> d e h"))
            load(w_o[:, :, :, :].rearrange("p e c d -> p (e c) d"), a["L1_ffn_W_out"].rearrange("e (c p) d -> p (e c) d", p=P))
            load(out[TOKENS:TOKENS + SLOTS, :].rearrange("(r p) d -> p r d", p=P), a["zero_rows"].rearrange("(r p) d -> p r d", p=P))
            assert n[0] == WEIGHT_LOADS, n[0]
            xn1_by_seq = xn1_d.rearrange("(s t p) d -> s p t d", p=P, t=T)
            out_by_seq = out[0:tokens, :].rearrange("(s t p) d -> s p t d", p=P, t=T)

            def body(s, l0, l1):
                if l0:
                    sp.wait_ge(x_free.sem, s + 1)
                    sp.dma_start(x[:, :, :], x_by_seq[(s + 1) % seqs]).then_inc(x_loaded.sem, 16)
                if l1:
                    r = s - 1
                    sp.wait_ge(l_normed.sem, l_normed.at(r, T))
                    sp.dma_start(xn1_by_seq[r], xn1[:, :, :]).then_inc(xn1_stored.sem, 16)
                    sp.wait_ge(l_out.sem, l_out.at(r, T))
                    sp.dma_start(out_by_seq[r], out_sb[:, :, :]).then_inc(out_stored.sem, 16)
            sequences(sp, body)
            sp.wait_ge(l_scattered.sem, l_scattered.per * seqs)
            sp.dma_start(table[:, :, :], slot_d.rearrange("(c p) w -> p c w", p=P)).then_inc(table_in, 16)
            sp.wait_ge(x_loaded.sem, x_loaded.per * (seqs + 1))
            sp.wait_ge(xn1_stored.sem, 16 * (seqs + 1))
            sp.wait_ge(out_stored.sem, 16 * (seqs + 1))
            sp.wait_ge(e_added, 16 * E * CC)

        @block.gpsimd
        def _(pool):
            pool.wait_ge(weights_in, WEIGHT_LOADS * 16)

            def power(s, given, done, dst, src):
                pool.wait_ge(given.sem, given.at(s, done.n + 1))
                done.inc(nc.gpsimd.tensor_tensor(dst, src, const("half"), ALU.pow))

            def norm_powers(s):
                power(s, ln_pow_in, ln_pow_out, small[:, RSTD, :], small[:, VE, :])
                power(s, ln_pow_in, ln_pow_out, small[:, R1, :], small[:, E1, :])

            def body(s, l0, l1):
                if l1:
                    power(s - 1, l_pow_in, l_pow_out, small1[:, 1, :], small1[:, 0, :])
                if l0:
                    power(s, pow_in, pow_out, small[:, R2, :], small[:, MS2, :])
                    norm_powers(s + 1)
                if l1:
                    r = s - 1
                    pool.wait_ge(l_entries.sem, l_entries.at(r, 1))
                    tok_next.inc(nc.gpsimd.tensor_tensor(tok[:, :], tok[:, :], const("len"), ALU.add))
                    for k in range(2):
                        for t in range(T):
                            l_scattered.inc(nc.gpsimd.indirect_dma_start(
                                slot_d, bass.IndirectOffsetOnAxis(ap=slot[:, k, t:t + 1], axis=0), entry[:, k, t, :], None,
                                bounds_check=SLOTS - 1, oob_is_err=False), 16)
                    pool.wait_ge(l_scattered.sem, l_scattered.at(r, l_scattered.per))
            norm_powers(0)
            sequences(pool, body)

            pool.wait_ge(e_index, 1)
            pool.wait_ge(xn1_stored.sem, 16 * (seqs + 1))
            for c in range(E * CC):
                nc.gpsimd.indirect_dma_start(xg[:, c, :], None, xn1_d, bass.IndirectOffsetOnAxis(ap=gather_at[:, c:c + 1], axis=0),
                                             bounds_check=tokens - 1, oob_is_err=True).then_inc(e_gathered[c // CC], 16)
            pool.wait_ge(out_stored.sem, 16 * (seqs + 1))
            for e in range(E):
                pool.wait_ge(e_yo, e + 1)
                if e:
                    pool.wait_ge(e_added, 16 * CC * e)
                for c in range(CC * e, CC * e + CC):
                    nc.gpsimd.indirect_dma_start(out, bass.IndirectOffsetOnAxis(ap=add_at[:, c:c + 1], axis=0), yo[:, c, :], None,
                                                 bounds_check=TOKENS + SLOTS - 1, oob_is_err=True, compute_op=ALU.add).then_inc(e_added, 16)

        @block.scalar
        def _(act):
            act.wait_ge(weights_in, WEIGHT_LOADS * 16)

            def body(s, l0, l1):
                r = s - 1

                def turned_copy(i, dst):
                    act.wait_ge(turned.sem, turned.at(s, i + 1))
                    turned_sb.inc(nc.scalar.activation(dst, misc[:, :], ACT.Copy))

                def gelus(group):
                    if group or not (isinstance(s, int) and s == 0):
                        act.wait_ge(ypsum.sem, ypsum.at(s, 3 * T * group))
                    for k, e in enumerate(EXPERTS[group]):
                        for c in range(HC):
                            act.wait_ge(filled.sem, filled.at(s, evac.n + 1))
                            evac.inc(nc.scalar.activation(hidT[:, k, c, :], ring[evac.n % 3][:, :], ACT.Gelu, bias=b1[:, e, c:c + 1]))

                def exps(n_units, first, width):
                    for i in range(n_units):
                        if i >= 4:
                            act.wait_ge(pv.sem, pv.at(s, first + i - 3))
                        n = width(i)
                        b = ring[evac.n % 3]
                        act.wait_ge(filled.sem, filled.at(s, evac.n + 1))
                        nc.scalar.activation(probs[:, i % 4, 0:n], b[:, 0:n], ACT.Exp, bias=lift[:, 0:1], scale=ATT_SCALE)
                        evac.inc(nc.scalar.activation(hi16[:, i % 4, 0:n], b[:, 0:n], ACT.Exp, bias=lift[:, 0:1], scale=ATT_SCALE))

                if l0:
                    turned_copy(0, xnT[:, :])
                    gelus(0)
                    act.wait_ge(gate_in.sem, gate_in.at(s, 1))
                    gate_exp.inc(nc.scalar.activation(gd[:, 1, :], gd[:, 0, :], ACT.Exp))
                    exps(len(GLOBAL_UNITS), 0, lambda i: J * P)
                    turned_copy(1, y2T[:, :])
                    gelus(1)
                    exps(len(LOCAL_UNITS), len(GLOBAL_UNITS), lambda i: J * LOCAL[LOCAL_UNITS[i][0]][1])
                if l1:
                    act.wait_ge(l_turned.sem, l_turned.at(r, 1))
                    l_turned_sb.inc(nc.scalar.activation(xn1T[:, :], misc[:, :], ACT.Copy))
                if l0:
                    gelus(2)
                if l1:
                    act.wait_ge(l_proj.sem, l_proj.at(r, 2))
                    l_v1.inc(nc.scalar.activation(v1[:, :, :].rearrange("p t d -> p (t d)"), ybank[:, :], ACT.Copy))
                    act.wait_ge(l_gate_in.sem, l_gate_in.at(r, 1))
                    l_gate_exp.inc(nc.scalar.activation(gd1[:, 1, :], gd1[:, 0, :], ACT.Exp))
                    for qt in range(T):
                        n = (qt + 1) * P
                        act.wait_ge(l_max.sem, l_max.at(r, qt + 1))
                        if qt >= 2:
                            act.wait_ge(l_prT.sem, l_prT.at(r, qt - 1))
                        l_exp.inc(nc.scalar.activation(pr1[:, qt % 2, 0:n], obank[qt % 2][:, 0:n], ACT.Exp, bias=top[:, 1, qt:qt + 1],
                                                       scale=L1_SCALE, accum_out=psums[:, 0, qt:qt + 1]))
            sequences(act, body)

            for e in range(E):
                act.wait_ge(e_hidden, e + 1)
                if e >= 2:
                    act.wait_ge(e_gated, e - 1)
                nc.scalar.activation(sig[:, e % 2, :, :].rearrange("p c n -> p (c n)"), bank[4 + e % 2][:, :], ACT.Sigmoid).then_inc(e_sig, 1)

        @block.vector
        def _(v):
            v.wait_ge(weights_in, WEIGHT_LOADS * 16)
            step = [0]

            def setup(ins):
                step[0] += 1
                ins.then_inc(setup_dve, 1)
                v.wait_ge(setup_dve, step[0])

            setup(nc.vector.tensor_copy(ident16[:, :], ident))
            setup(nc.vector.tensor_copy(masks16[:, 0, :], const("negcausal")))
            setup(nc.vector.tensor_copy(masks16[:, 1, :], const("negband")))
            setup(nc.vector.memset(lift[:, :], LIFT))
            setup(nc.vector.memset(V3[:, :, :, 1:PARTS, HD:VD], 0.0))
            setup(nc.vector.memset(V3[:, :, :, 0, HD:VD], 1.0))
            setup(nc.vector.memset(cw[:, :, E:E + 1], 1.0))
            for dst, raw, nrm in ((wg, wg_raw, norm1), (wl, wl_raw, norm2)):
                setup(nc.vector.tensor_scalar(dst[:, 0:D].rearrange("p (j g d) -> p j g d", j=J, g=KVH),
                                              raw[:, 0:D].rearrange("p (g j d) -> p j g d", j=J, g=KVH),
                                              nrm[:, 0:1], None, ALU.mult))
            setup(nc.vector.tensor_scalar(wl[:, D:D + 64], wl_raw[:, D:D + 64], norm2[:, 0:1], None, ALU.mult))
            v.wait_ge(setup_pe, 1)
            setup(nc.vector.tensor_copy(kv_downT[:, :], bank[0][0:LAT, 0:P]))
            assert step[0] == SETUP_A
            v.wait_ge(setup_pe, 2)
            setup(nc.vector.tensor_scalar(wg[:, D:D + 64], bank[1][:, 0:64], norm1[:, 0:1], None, ALU.mult))
            for i in range(2):
                src = bank[2 + i][:, 0:P]
                swapped = wqk1[:, 2 * i + 1, :].rearrange("p (n e) -> p n e", e=2)
                v.wait_ge(setup_pe, 3 + i)
                setup(nc.vector.tensor_copy(wqk1[:, 2 * i, :], src))
                for e in range(2):
                    setup(nc.vector.tensor_copy(swapped[:, :, e], src.rearrange("p (n e) -> p n e", e=2)[:, :, 1 - e]))
            v.wait_ge(setup_pe, 5)
            setup(nc.vector.tensor_copy(wv1[:, :], bank[4][:, 0:P]))
            setup(nc.vector.tensor_copy(tok[:, :], const("tok")))
            setup(nc.vector.memset(before_t[:, T, :], 0.0))
            nc.vector.memset(small[:, 9, :], 0.0).then_inc(xn1_stored.sem, 16)
            nc.vector.memset(small[:, 10, :], 0.0).then_inc(out_stored.sem, 16)
            assert step[0] == SETUP_B

            def top2(chained, src, oh):
                wide = lambda z: z.unsqueeze(2).to_broadcast([P, T, E])
                iota = const("iota").unsqueeze(1).to_broadcast([P, T, E])
                for k in range(2):
                    chained(nc.vector.tensor_reduce(gm[:, k, :], src[:, :, :], AX.X, ALU.max))
                    chained(nc.vector.tensor_tensor(gk[:, :, :], src[:, :, :], wide(gm[:, k, :]), ALU.is_equal))
                    chained(nc.vector.scalar_tensor_tensor(gk[:, :, :], gk[:, :, :], -16.0, iota, ALU.mult, ALU.add))
                    chained(nc.vector.tensor_reduce(km[:, k, :], gk[:, :, :], AX.X, ALU.min))
                    chained(nc.vector.tensor_tensor(oh[:, k, :, :], gk[:, :, :], wide(km[:, k, :]), ALU.is_equal))
                    if k == 0:
                        chained(nc.vector.scalar_tensor_tensor(l2[:, :, :], oh[:, 0, :, :], -BIG, src[:, :, :], ALU.mult, ALU.add))
                        src = l2

            def moments(s, sig, src):
                def wait():
                    v.wait_ge(sig.sem, sig.at(s, sig.n))
                for t in range(T):
                    sig.inc(nc.vector.bn_stats(stats[:, t, :], src[:, t, :]))
                wait()
                m = small[:, 8:11, :]
                sig.inc(nc.vector.tensor_tensor(m[:, 0, :], stats[:, :, 1], stats[:, :, 4], ALU.add))
                sig.inc(nc.vector.tensor_tensor(m[:, 1, :], stats[:, :, 1], stats[:, :, 4], ALU.subtract))
                sig.inc(nc.vector.tensor_tensor(m[:, 2, :], stats[:, :, 2], stats[:, :, 5], ALU.add))
                wait()
                sig.inc(nc.vector.tensor_scalar(mv[:, :, 0], m[:, 0, :], 0.5, None, ALU.mult))
                sig.inc(nc.vector.tensor_tensor(m[:, 1, :], m[:, 1, :], m[:, 1, :], ALU.mult))
                sig.inc(nc.vector.tensor_scalar(m[:, 2, :], m[:, 2, :], 1.0 / D, None, ALU.mult))
                wait()
                sig.inc(nc.vector.scalar_tensor_tensor(mv[:, :, 1], m[:, 1, :], 0.25, m[:, 2, :], ALU.mult, ALU.add))
                wait()

            def layer_norm(s):
                def chained(ins):
                    ln.inc(ins)
                    v.wait_ge(ln.sem, ln.at(s, ln.n))
                v.wait_ge(x_loaded.sem, x_loaded.at(s, 16))
                moments(s, ln, x)
                ln_pow_in.inc(nc.vector.tensor_scalar(small[:, VE, :], mv[:, :, 1], 1e-5, None, ALU.add))
                v.wait_ge(ln_pow_out.sem, ln_pow_out.at(s, 1))
                for t in range(T):
                    normed.inc(nc.vector.tensor_scalar(xn[:, t, :], x[:, t, :], mv[:, t, 0:1], small[:, RSTD, t:t + 1],
                                                       ALU.subtract, ALU.mult))
                chained(nc.vector.tensor_tensor(small[:, SQ, :], small[:, RSTD, :], small[:, RSTD, :], ALU.mult))
                chained(nc.vector.tensor_tensor(small[:, SQ, :], small[:, SQ, :], mv[:, :, 1], ALU.mult))
                ln_pow_in.inc(nc.vector.tensor_scalar(small[:, E1, :], small[:, SQ, :], 1e-6, None, ALU.add))
                v.wait_ge(ln_pow_in.sem, ln_pow_in.at(s, 2))
                chained(nc.vector.tensor_scalar(small[:, EPS1, :], small[:, E1, :], 1e-6, None, ALU.mult))
                x_free.inc(nc.vector.tensor_tensor(x1[:, :, :], x[:, :, :], xn[:, :, :], ALU.add))

            def l1_norm(r):
                v.wait_ge(xn1_stored.sem, xn1_stored.at(r, 16))
                moments(r, l_vec, xl)
                l_pow_in.inc(nc.vector.tensor_scalar(small1[:, 0, :], mv[:, :, 1], 1e-5, None, ALU.add))
                v.wait_ge(l_pow_out.sem, l_pow_out.at(r, 1))
                for t in range(T):
                    l_normed.inc(nc.vector.tensor_scalar(xn1[:, t, :], xl[:, t, :], mv[:, t, 0:1], small1[:, 1, t:t + 1],
                                                         ALU.subtract, ALU.mult))

            def body(s, l0, l1):
                r = s - 1

                def chained(ins):
                    vec.inc(ins)
                    v.wait_ge(vec.sem, vec.at(s, vec.n))

                def chained1(ins):
                    l_vec.inc(ins)
                    v.wait_ge(l_vec.sem, l_vec.at(r, l_vec.n))

                def rope(i, n, eps, meanwhile):
                    cos = const("cos_" + n).rearrange("p (t d) -> p t d", t=T)
                    sin = const("sin_" + n).rearrange("p (t d) -> p t d", t=T)
                    nsin = const("nsin_" + n).rearrange("p (t d) -> p t d", t=T)
                    for h in range(2):
                        ts = slice(2 * h, 2 * h + 2)
                        src = qkv2(h, 0, QK)
                        pairs = src.rearrange("p t (n d e) -> p t n d e", d=HD // 2, e=2)
                        to = t2[:, ts, :].rearrange("p t (n d e) -> p t n d e", d=HD // 2, e=2)
                        vec.inc(nc.vector.tensor_tensor(
                            t1[:, ts, :].rearrange("p t (n d) -> p t n d", d=HD),
                            src.rearrange("p t (n d) -> p t n d", d=HD),
                            cos[:, ts, :].unsqueeze(2).to_broadcast([P, 2, H + KVH, HD]), ALU.mult))
                        for e, tab in ((0, nsin), (1, sin)):
                            vec.inc(nc.vector.tensor_tensor(
                                to[:, :, :, :, e], pairs[:, :, :, :, 1 - e],
                                tab[:, ts, :].unsqueeze(2).to_broadcast([P, 2, H + KVH, HD // 2]), ALU.mult))
                    v.wait_ge(vec.sem, vec.at(s, vec.n))
                    chained(nc.vector.tensor_tensor(t1[:, :, :], t1[:, :, :], t2[:, :, :], ALU.add))
                    chained(nc.vector.tensor_tensor(t2[:, :, :], t1[:, :, :], t1[:, :, :], ALU.mult))
                    chained(nc.vector.tensor_reduce(msum[:, :], t2[:, :, :].rearrange("p t (n d) -> p (t n) d", d=HD), AX.X, ALU.add))
                    if eps is None:
                        chained(nc.vector.tensor_scalar(msum[:, :], msum[:, :], 1.0 / HD, 1e-6, ALU.mult, ALU.add))
                    else:
                        m3 = msum[:, :].rearrange("p (t n) -> p t n", t=T)
                        chained(nc.vector.scalar_tensor_tensor(m3, m3, 1.0 / HD, eps.unsqueeze(2).to_broadcast([P, T, H + KVH]),
                                                               ALU.mult, ALU.add))
                    rsqrt()
                    as3 = lambda z: z.rearrange("p t (n d) -> p (t n) d", d=HD)
                    slots = stack[:, :, :, :, :].rearrange("p t n s d -> p (t n) s d")
                    chained(nc.vector.tensor_tensor(as3(qn[:, :, :]), as3(t1[:, :, :]),
                                                    rq[:, :].unsqueeze(2).to_broadcast([P, NH, HD]), ALU.mult))
                    chained(nc.vector.tensor_copy(slots[:, :, 0, :], as3(qn[:, :, :])))
                    chained(nc.vector.tensor_tensor(slots[:, :, 3, :], as3(qn[:, :, :]), slots[:, :, 0, :], ALU.subtract))
                    for dst, src, lo, hi in ((1, 0, 0, H), (2, 3, 0, H), (2, 0, H, H + KVH), (1, 3, H, H + KVH)):
                        ins = nc.vector.tensor_copy(stack[:, :, lo:hi, dst, :], stack[:, :, lo:hi, src, :])
                    stacked.inc(ins)
                    meanwhile()
                    for t in range(T):
                        v.wait_ge(stackT.sem, stackT.at(s, heads.n + 1))
                        heads.inc(nc.vector.tensor_copy(QKT[:, :, t * P:(t + 1) * P], as16(ring[t % 3])))

                def rsqrt():
                    chained(nc.vector.tensor_scalar(rt[:, 0, :].bitcast(I32), msum[:, :].bitcast(I32), 1, None, ALU.arith_shift_right))
                    chained(nc.vector.tensor_scalar(rq[:, :].bitcast(I32), rt[:, 0, :].bitcast(I32), -1.0, float(0x5F3759DF), ALU.mult, ALU.add))
                    for _ in range(4):
                        chained(nc.vector.scalar_tensor_tensor(rt[:, 0, :], rq[:, :], -0.5, rq[:, :], ALU.mult, ALU.mult))
                        chained(nc.vector.tensor_tensor(rt[:, 1, :], rt[:, 0, :], msum[:, :], ALU.mult))
                        chained(nc.vector.scalar_tensor_tensor(rq[:, :], rt[:, 1, :], 1.5, rq[:, :], ALU.add, ALU.mult))

                def split_values(n):
                    full, rest = vf[:, 0, 0:n, :, :], vf[:, 1, 0:n, :, :]
                    part = [V3[:, 0:n, :, k, 0:HD] for k in range(PARTS)]
                    chained(nc.vector.tensor_copy(part[0], full))
                    chained(nc.vector.tensor_tensor(rest, full, part[0], ALU.subtract))
                    chained(nc.vector.tensor_copy(part[1], rest))
                    values.inc(nc.vector.tensor_tensor(part[2], rest, part[1], ALU.subtract))

                def global_values():
                    v.wait_ge(ln_pow_out.sem, ln_pow_out.at(s, 2))
                    for h in range(2):
                        ts = slice(2 * h, 2 * h + 2)
                        vec.inc(nc.vector.tensor_tensor(vf[:, 0, ts, :, :], qkv2(h, QK, QK + 32).rearrange("p t (g d) -> p t g d", g=KVH),
                                                        small[:, R1, ts].unsqueeze(2).unsqueeze(3).to_broadcast([P, 2, KVH, HD]), ALU.mult))
                    v.wait_ge(vec.sem, vec.at(s, vec.n))
                    split_values(T)

                def local_values():
                    chained(nc.vector.tensor_copy(vf[:, 0, :, :, :], misc[:, 0:len(LOCAL) * 32].rearrange("p (b g d) -> p b g d", g=KVH, d=HD)))
                    split_values(len(LOCAL))

                def gating():
                    for h in range(2):
                        vec.inc(nc.vector.tensor_tensor(lg[:, 2 * h:2 * h + 2, :], qkv2(h, QK + 32, QK + 32 + E),
                                                        gate_b[:, :].unsqueeze(1).to_broadcast([P, 2, E]), ALU.add))
                    v.wait_ge(vec.sem, vec.at(s, vec.n))
                    top2(chained, lg, oh)
                    gate_in.inc(nc.vector.tensor_tensor(gd[:, 0, :], gm[:, 1, :], gm[:, 0, :], ALU.subtract))

                def gate_weights():
                    v.wait_ge(gate_exp.sem, gate_exp.at(s, 1))
                    wide = lambda z: z.unsqueeze(2).to_broadcast([P, T, E])
                    chained(nc.vector.tensor_scalar(gw[:, 0, :], gd[:, 1, :], 1.0, None, ALU.add))
                    chained(nc.vector.reciprocal(gw[:, 0, :], gw[:, 0, :]))
                    chained(nc.vector.tensor_tensor(gw[:, 1, :], gw[:, 0, :], gd[:, 1, :], ALU.mult))
                    for k in range(2):
                        chained(nc.vector.tensor_tensor(oh[:, k, :, :], oh[:, k, :, :], wide(gw[:, k, :]), ALU.mult))
                    cw_ready.inc(nc.vector.tensor_tensor(cw[:, :, 0:E], oh[:, 0, :, :], oh[:, 1, :, :], ALU.add))
                    v.wait_ge(cw_ready.sem, cw_ready.at(s, 1))

                def combine():
                    k = yused.n
                    t, e = k % T, sum(EXPERTS, [])[k // T]
                    v.wait_ge(ypsum.sem, ypsum.at(s, k + 1))
                    y = tiles(ybank)[:, t, :]
                    if e == E:
                        ins = nc.vector.tensor_tensor(acc[:, t, :], y, x1[:, t, :], ALU.add)
                    else:
                        v.wait_ge(yused.sem, yused.at(s, k - T + 1))
                        ins = nc.vector.scalar_tensor_tensor(acc[:, t, :], y, cw[:, t, e:e + 1], acc[:, t, :], ALU.mult, ALU.add)
                    yused.inc(ins)

                def low(use, slot, n):
                    v.wait_ge(evac.sem, evac.at(s, use + 1))
                    lows.inc(nc.vector.tensor_tensor(lo16[:, slot, 0:n], probs[:, slot, 0:n], hi16[:, slot, 0:n], ALU.subtract))

                def divide(blk, nq, last_unit):
                    k = blk % 2
                    v.wait_ge(pv.sem, pv.at(s, last_unit + 1))
                    o = obank[k][0:nq, 0:H * PARTS * VD].rearrange("p (h c d) -> p h d c", c=PARTS, d=VD)
                    chained(nc.vector.tensor_reduce(osum[0:nq, k, :, :], o, AX.X, ALU.add))
                    chained(nc.vector.reciprocal(rden[0:nq, k, :], osum[0:nq, k, :, HD]))
                    otoks.inc(nc.vector.tensor_tensor(otok[0:nq, k, :, :], osum[0:nq, k, :, 0:HD],
                                                      rden[0:nq, k, :].unsqueeze(2).to_broadcast([nq, H, HD]), ALU.mult))

                def oT_copy(q0, nq):
                    v.wait_ge(oturn.sem, oturn.at(s, oT_sb.n + 1))
                    oT_sb.inc(nc.vector.tensor_copy(oT[:, q0:q0 + nq], misc[:, q0:q0 + nq]))

                def l1_router():
                    v.wait_ge(l_proj.sem, l_proj.at(r, 1))
                    l_lg.inc(nc.vector.tensor_tensor(lg[:, :, :], abank[:, 0:T * E].rearrange("p (t e) -> p t e", e=E),
                                                     router_b[:, :].unsqueeze(1).to_broadcast([P, T, E]), ALU.add))
                    v.wait_ge(l_lg.sem, l_lg.at(r, 1))
                    top2(chained1, lg, oh1)
                    l_gate_in.inc(nc.vector.tensor_tensor(gd1[:, 0, :], gm[:, 1, :], gm[:, 0, :], ALU.subtract))
                    chained1(nc.vector.tensor_tensor(chosen[:, :, :], oh1[:, 0, :, :], oh1[:, 1, :, :], ALU.add))
                    chained1(nc.vector.tensor_copy(before_t[:, 0, :], before_t[:, T, :]))
                    for t in range(T):
                        ins = nc.vector.tensor_tensor(before_t[:, t + 1, :], before_t[:, t, :], chosen[:, t, :], ALU.add)
                        (l_chosen.inc if t == T - 1 else chained1)(ins)

                def l1_rotate(i):
                    v.wait_ge(l_proj.sem, l_proj.at(r, 3 + i))
                    for h, tab in ((0, "cos1"), (1, "sin1")):
                        l_vec.inc(nc.vector.tensor_tensor(rot[:, i, h, :], rot_banks[i][h][:, :], const(tab), ALU.mult))
                    v.wait_ge(l_vec.sem, l_vec.at(r, l_vec.n))
                    l_rotated.inc(nc.vector.tensor_tensor(qk_turned[:, i, :], rot[:, i, 0, :], rot[:, i, 1, :], ALU.add))

                def l1_slots():
                    v.wait_ge(l_gate_exp.sem, l_gate_exp.at(r, 1))
                    chained1(nc.vector.tensor_scalar(gw[:, 0, :], gd1[:, 1, :], 1.0, None, ALU.add))
                    chained1(nc.vector.reciprocal(gw[:, 0, :], gw[:, 0, :]))
                    chained1(nc.vector.tensor_tensor(gw[:, 1, :], gw[:, 0, :], gd1[:, 1, :], ALU.mult))
                    for k in range(2):
                        l_vec.inc(nc.vector.tensor_copy(entry[:, k, :, 0], tok[:, :]))
                        l_vec.inc(nc.vector.tensor_copy(entry[:, k, :, 1], gw[:, k, :]))
                    v.wait_ge(l_rank.sem, l_rank.at(r, 1))
                    l_ranked.inc(nc.vector.tensor_copy(rank[:, :, :], misc[:, 0:T * E].rearrange("p (t e) -> p t e", e=E)))
                    v.wait_ge(l_ranked.sem, l_ranked.at(r, 1))
                    for k in range(2):
                        l_vec.inc(nc.vector.tensor_tensor(rsel[:, k, 0, :, :], oh1[:, k, :, :], rank[:, :, :], ALU.mult))
                        l_vec.inc(nc.vector.tensor_tensor(rsel[:, k, 1, :, :], oh1[:, k, :, :], const("base").unsqueeze(1).to_broadcast([P, T, E]), ALU.mult))
                    v.wait_ge(l_vec.sem, l_vec.at(r, l_vec.n))
                    chained1(nc.vector.tensor_reduce(rk[:, :, :, :].rearrange("p a b t -> p (a b t)"),
                                                     rsel[:, :, :, :, :].rearrange("p a b t e -> p (a b t) e"), AX.X, ALU.add))
                    chained1(nc.vector.tensor_tensor(rk[:, :, 1, :], rk[:, :, 1, :], rk[:, :, 0, :], ALU.add))
                    chained1(nc.vector.tensor_scalar(rk[:, :, 0, :], rk[:, :, 0, :], float(CAP), 1.0e6, ALU.is_ge, ALU.mult))
                    l_entries.inc(nc.vector.tensor_tensor(slot[:, :, :], rk[:, :, 1, :], rk[:, :, 0, :], ALU.add))

                def peak(qt):
                    n = (qt + 1) * P
                    sc = obank[qt % 2]
                    v.wait_ge(l_scores.sem, l_scores.at(r, qt + 1))
                    chained1(nc.vector.tensor_tensor(sc[:, n - P:n], sc[:, n - P:n], const("negmask"), ALU.add))
                    chained1(nc.vector.tensor_reduce(top[:, 0, qt:qt + 1], sc[:, 0:n], AX.X, ALU.max))
                    l_max.inc(nc.vector.tensor_scalar(top[:, 1, qt:qt + 1], top[:, 0, qt:qt + 1], -L1_SCALE, None, ALU.mult))

                def probs_copy(qt):
                    n = (qt + 1) * P
                    v.wait_ge(l_prT.sem, l_prT.at(r, qt + 1))
                    l_prT_sb.inc(nc.vector.tensor_copy(prT[:, qt % 2, :, :].rearrange("p t n -> p (t n)")[:, 0:n], ring[qt % 2][:, 0:n]))

                def finish(qt):
                    if qt == 0:
                        v.wait_ge(out_stored.sem, out_stored.at(r, 16))
                    v.wait_ge(l_exp.sem, l_exp.at(r, qt + 1))
                    chained1(nc.vector.reciprocal(psums[:, 1, qt:qt + 1], psums[:, 0, qt:qt + 1]))
                    v.wait_ge(l_pv.sem, l_pv.at(r, qt + 1))
                    l_out.inc(nc.vector.scalar_tensor_tensor(out_sb[:, qt, :], tiles(abank)[:, qt, :], psums[:, 1, qt:qt + 1],
                                                             xl[:, qt, :], ALU.mult, ALU.add))

                if l1:
                    l1_norm(r)
                if l0:
                    v.wait_ge(projected.sem, projected.at(s, 1))

                    def beside_g():
                        global_values()
                        gating()
                    rope(0, "g", small[:, EPS1, :], beside_g)
                    gate_weights()
                    G, L = len(GLOBAL_UNITS), len(LOCAL_UNITS)
                    for i in range(G):
                        low(12 + i, i % 4, J * P)
                        if i == 2:
                            v.wait_ge(cw_turn.sem, cw_turn.at(s, 1))
                            cwT_sb.inc(nc.vector.tensor_copy(cwT[:, :], misc[0:E + 1, :]))
                        for q in range(T - 1):
                            if i == ENDS[q] + 2:
                                divide(q, P, ENDS[q])
                            if i == ENDS[q] + 5:
                                oT_copy(q * P, P)
                        if i in COMBINE_G:
                            combine()
                    while yused.n < 12:
                        combine()
                    divide(T - 1, P, G - 1)
                    oT_copy((T - 1) * P, P)
                    v.wait_ge(attn.sem, attn.at(s, 1))
                    v.wait_ge(yused.sem, yused.at(s, 12))
                    vec.inc(nc.vector.tensor_tensor(x1[:, :, :], xn[:, :, :], tiles(abank), ALU.add))
                    v.wait_ge(vec.sem, vec.at(s, vec.n))
                    attn_used.inc(nc.vector.tensor_tensor(acc[:, :, :], acc[:, :, :], tiles(abank), ALU.add))
                    moments(s, vec, x1)
                    chained(nc.vector.tensor_tensor(small[:, SQ, :], mv[:, :, 0], mv[:, :, 0], ALU.mult))
                    pow_in.inc(nc.vector.scalar_tensor_tensor(small[:, MS2, :], small[:, SQ, :], 1e-6, mv[:, :, 1], ALU.add, ALU.add))
                    v.wait_ge(pow_out.sem, pow_out.at(s, 1))
                    for t in range(T):
                        normed2.inc(nc.vector.tensor_scalar(y2[:, t, :], x1[:, t, :], small[:, R2, t:t + 1], None, ALU.mult))
                    v.wait_ge(projected.sem, projected.at(s, 2))
                    rope(1, "l", None, local_values)
                    for i, (b, g) in enumerate(LOCAL_UNITS):
                        q0, nq, k0 = LOCAL[b]
                        low(12 + G + 12 + i, i % 4, J * nq)
                        if b and g == 1:
                            divide(b - 1, LOCAL[b - 1][1], G + 4 * b - 1)
                        if b >= 2 and g == 0:
                            oT_copy(*LOCAL[b - 2][0:2])
                        if i in COMBINE_L:
                            combine()
                    while yused.n < 24:
                        combine()
                    oT_copy(*LOCAL[-2][0:2])
                    divide(len(LOCAL) - 1, LOCAL[-1][1], UNITS - 1)
                    oT_copy(*LOCAL[-1][0:2])
                    v.wait_ge(attn.sem, attn.at(s, 2))
                    v.wait_ge(yused.sem, yused.at(s, 24))
                    attn_used.inc(nc.vector.tensor_tensor(acc[:, :, :], acc[:, :, :], tiles(abank), ALU.add))
                    v.wait_ge(attn_used.sem, attn_used.at(s, 2))

                def some(k):
                    for _ in range(k if l0 else 0):
                        combine()
                if l1:
                    l1_router()
                if l0:
                    layer_norm(s + 1)
                if l1:
                    l1_rotate(0)
                    l1_rotate(1)
                    l1_slots()
                    peak(0)
                    peak(1)
                    some(2)
                    probs_copy(0)
                    peak(2)
                    some(2)
                    probs_copy(1)
                    finish(0)
                    peak(3)
                    some(2)
                    finish(1)
                    probs_copy(2)
                    some(2)
                    finish(2)
                    probs_copy(3)
                    some(2)
                    finish(3)
                if l0:
                    while yused.n < 36:
                        combine()
                    v.wait_ge(yused.sem, yused.at(s, 36))
                    if l1:
                        v.wait_ge(l_out.sem, l_out.at(r, T))
                    xl_ready.inc(nc.vector.tensor_copy(xl[:, :, :], acc[:, :, :]))
                    v.wait_ge(xl_ready.sem, xl_ready.at(s, 1))
                assert not l0 or vec.n == VEC_STEPS, vec.n
                assert not l1 or l_vec.n == L_STEPS, l_vec.n
            layer_norm(0)
            assert ln.n == LN_STEPS, ln.n
            sequences(v, body)

            v.wait_ge(table_in, 16)
            nc.vector.tensor_scalar(tclip[:, :], table[:, :, 0], float(tokens - 1), None, ALU.min).then_inc(e_vec, 1)
            nc.vector.tensor_copy(add_at[:, :], table[:, :, 0]).then_inc(e_vec, 1)
            v.wait_ge(e_vec, 2)
            nc.vector.tensor_copy(gather_at[:, :], tclip[:, :]).then_inc(e_index, 1)
            def gate(e):
                v.wait_ge(e_turned, e + 1)
                if e >= 2:
                    v.wait_ge(e_hidden, e - 1)
                nc.vector.tensor_copy(xgT[:, e % 2, :], bank[e % 2][:, 0:CAP]).then_inc(e_turned_sb, 1)

            def product(e):
                v.wait_ge(e_sig, e + 1)
                flat = lambda z: z[:, e % 2, :, :].rearrange("p c n -> p (c n)")
                nc.vector.tensor_tensor(flat(sig), bank[4 + e % 2][:, :], flat(sig), ALU.mult).then_inc(e_vec, 1)
                v.wait_ge(e_vec, 3 + e)
                if e >= 2:
                    v.wait_ge(e_y, e - 1)
                nc.vector.tensor_tensor(flat(gT), bank[2 + e % 2][:, :], flat(sig), ALU.mult).then_inc(e_gated, 1)

            def weigh(e):
                v.wait_ge(e_y, e + 1)
                for c in range(CC):
                    ins = nc.vector.tensor_scalar(yo[:, CC * e + c, :], bank[6 + e % 2][:, c * P:(c + 1) * P], table[:, CC * e + c, 1:2], None, ALU.mult)
                ins.then_inc(e_yo, 1)
            gate(0)
            for e in range(E):
                if e + 1 < E:
                    gate(e + 1)
                product(e)
                weigh(e)

        @block.tensor
        def _(pe):
            pe.wait_ge(weights_in, WEIGHT_LOADS * 16)
            nc.tensor.transpose(bank[0][0:LAT, 0:P], kv_down[:, :], ident).then_inc(setup_pe, 1)
            pe.wait_ge(setup_dve, SETUP_A)
            nc.tensor.matmul(bank[1][:, 0:64], kv_downT[:, :], kv_up[:, :], start=True, stop=True).then_inc(setup_pe, 1)
            for i in range(3):
                nc.tensor.transpose(bank[2 + i][:, 0:P], l1_raw[:, i, :], ident).then_inc(setup_pe, 1)
            pe.wait_ge(setup_dve, SETUP_B)

            def body(s, l0, l1):
                r = s - 1

                def turn(i, src, sig):
                    for t in range(T):
                        pe.wait_ge(sig.sem, sig.at(s, t + 1))
                        ins = nc.tensor.transpose(misc[:, t * P:(t + 1) * P], src[:, t, :], ident)
                    turned.inc(ins)
                    pe.wait_ge(turned_sb.sem, turned_sb.at(s, i + 1))

                def turn_heads(i, uses):
                    pe.wait_ge(evac.sem, evac.at(s, uses))
                    pe.wait_ge(stacked.sem, stacked.at(s, i + 1))
                    for t in range(T):
                        if t == T - 1:
                            pe.wait_ge(heads.sem, heads.at(s, T * i + 1))
                        for b in range(J + 1):
                            ins = nc.tensor.transpose(as16(ring[t % 3])[:, b, :],
                                                      stack[:, t, b * KVH:(b + 1) * KVH, :, :].rearrange("p g s d -> p (g s d)"),
                                                      ident16[:, :])
                        stackT.inc(ins)
                    pe.wait_ge(heads.sem, heads.at(s, T * (i + 1)))

                def hidden(k):
                    e = sum(EXPERTS, [])[k]
                    for c in range(HC):
                        use = filled.n
                        if use >= 3:
                            pe.wait_ge(evac.sem, evac.at(s, use - 2))
                        filled.inc(nc.tensor.matmul(ring[use % 3][:, :], w1[:, e, c * P:(c + 1) * P], xnT[:, :], start=True, stop=True))

                def second():
                    k = ypsum.n
                    t, n = k % T, k // T
                    e = sum(EXPERTS, [])[n]
                    if k:
                        pe.wait_ge(yused.sem, yused.at(s, k))
                    if k == 0:
                        pe.wait_ge(cwT_sb.sem, cwT_sb.at(s, 1))
                    y = ybank[:, t * P:(t + 1) * P]
                    for c in range(HC):
                        ins = nc.tensor.matmul(y, hidT[:, n % 3, c, t * P:(t + 1) * P], w2[:, e, c, :],
                                               start=(c == 0), stop=(c == HC - 1 and e != E))
                    if e == E:
                        ins = nc.tensor.matmul(y, cwT[:, t * P:(t + 1) * P], b2[:, :], start=False, stop=True)
                    ypsum.inc(ins)

                def scores(g, k_off, q0, nq, mask):
                    use = filled.n
                    pe.wait_ge(evac.sem, evac.at(s, use - 2))
                    dst = ring[use % 3][:, 0:J * nq]
                    if mask:
                        m, at = mask
                        nc.tensor.matmul(dst, ident16[:, :], masks16[:, m, at:at + nq].unsqueeze(1).to_broadcast([P, J, nq]),
                                         start=True, stop=False)
                    rows = slice(32 * g, 32 * g + 32)
                    filled.inc(nc.tensor.matmul(dst, QKT[rows, J, k_off:k_off + P], QKT[rows, 0:J, q0:q0 + nq],
                                                start=not mask, stop=True))

                def values_product(i, slot, g, nq, vblk, blk, first):
                    pe.wait_ge(lows.sem, lows.at(s, i + 1))
                    V = V3[:, vblk, g, :, :].rearrange("p c d -> p (c d)")
                    for j in range(J):
                        h = J * g + j
                        dst = obank[blk % 2][0:nq, h * PARTS * VD:(h + 1) * PARTS * VD]
                        for half in (hi16, lo16):
                            ins = nc.tensor.matmul(dst, half[:, slot, j * nq:(j + 1) * nq], V,
                                                   start=(first and j == 0 and half is hi16), stop=True, skip_group_check=True)
                    pv.inc(ins)

                def turn_out(blk, q0, nq):
                    if oturn.n:
                        pe.wait_ge(oT_sb.sem, oT_sb.at(s, oturn.n))
                    pe.wait_ge(otoks.sem, otoks.at(s, oturn.n + 1))
                    o = otok[0:nq, blk % 2, :, :].rearrange("p h d -> p (h d)")
                    if nq > 32:
                        ins = nc.tensor.transpose(misc[:, q0:q0 + nq], o, ident[0:nq, 0:nq])
                    else:
                        ins = nc.tensor.matmul(misc[:, q0:q0 + nq], o, ident[0:nq, 0:nq], start=True, stop=True)
                    oturn.inc(ins)

                def project_out(t, w, upto):
                    pe.wait_ge(oT_sb.sem, oT_sb.at(s, upto))
                    return nc.tensor.matmul(abank[:, t * P:(t + 1) * P], oT[:, t * P:(t + 1) * P], w[:, :], start=True, stop=True)

                def l1_turn():
                    for t in range(T):
                        pe.wait_ge(l_normed.sem, l_normed.at(r, t + 1))
                        ins = nc.tensor.transpose(misc[:, t * P:(t + 1) * P], xn1[:, t, :], ident)
                    l_turned.inc(ins)

                def l1_logits_values():
                    pe.wait_ge(l_turned_sb.sem, l_turned_sb.at(r, 1))
                    for t in range(T):
                        ins = nc.tensor.matmul(abank[:, t * E:(t + 1) * E], xn1T[:, t * P:(t + 1) * P], router[:, :], start=True, stop=True)
                    l_proj.inc(ins)
                    for t in range(T):
                        ins = nc.tensor.matmul(ybank[:, t * P:(t + 1) * P], xn1T[:, t * P:(t + 1) * P], wv1[:, :], start=True, stop=True)
                    l_proj.inc(ins)

                def l1_project(i):
                    if i == 1:
                        pe.wait_ge(l_lg.sem, l_lg.at(r, 1))
                    for h in range(2):
                        ins = nc.tensor.matmul(rot_banks[i][h][:, :], wqk1[:, 2 * i + h, :], xn1T[:, :], start=True, stop=True)
                    l_proj.inc(ins)

                def l1_ranks():
                    pe.wait_ge(l_chosen.sem, l_chosen.at(r, 1))
                    pe.wait_ge(l_rotated.sem, l_rotated.at(r, 2))
                    dst = misc[:, 0:T * E]
                    nc.tensor.matmul(dst, const("before"), chosen[:, :, :].rearrange("p t e -> p (t e)"), start=True, stop=False)
                    l_rank.inc(nc.tensor.matmul(dst, const("ones"), before_t[:, 0:T, :].rearrange("p t e -> p (t e)"), start=False, stop=True))

                def l1_scores(qt):
                    n = (qt + 1) * P
                    if qt >= 2:
                        pe.wait_ge(l_exp.sem, l_exp.at(r, qt - 1))
                    l_scores.inc(nc.tensor.matmul(obank[qt % 2][:, 0:n], qk_turned[:, 0, qt * P:(qt + 1) * P], qk_turned[:, 1, 0:n], start=True, stop=True))

                def l1_turn_probs(qt):
                    pe.wait_ge(l_exp.sem, l_exp.at(r, qt + 1))
                    if qt >= 2:
                        pe.wait_ge(l_prT_sb.sem, l_prT_sb.at(r, qt - 1))
                    for k in range(qt + 1):
                        ins = nc.tensor.transpose(ring[qt % 2][:, k * P:(k + 1) * P], pr1[:, qt % 2, k * P:(k + 1) * P], ident)
                    l_prT.inc(ins)

                def l1_pv(qt):
                    pe.wait_ge(l_prT_sb.sem, l_prT_sb.at(r, qt + 1))
                    if qt:
                        pe.wait_ge(l_out.sem, l_out.at(r, qt))
                    for k in range(qt + 1):
                        ins = nc.tensor.matmul(abank[:, qt * P:(qt + 1) * P], prT[:, qt % 2, k, :], v1[:, k, :], start=(k == 0), stop=(k == qt))
                    l_pv.inc(ins)

                if l0:
                    turn(0, xn, normed)
                    if not (isinstance(s, int) and s == 0):
                        pe.wait_ge(xl_ready.sem, xl_ready.at(s, 0))
                    for t in range(T):
                        ins = nc.tensor.matmul(qkv(t, 0, QK + 32 + E), xnT[:, t * P:(t + 1) * P], wg[:, :], start=True, stop=True)
                    projected.inc(ins)
                    for k in range(3):
                        hidden(k)
                    turn_heads(0, 12)
                    pe.wait_ge(values.sem, values.at(s, 1))
                    U = GLOBAL_UNITS

                    def scores_g(i):
                        qt, g, kt = U[i]
                        scores(g, kt * P, qt * P, P, (0, 0) if kt == qt else None)
                    scores_g(0)
                    scores_g(1)
                    for i, (qt, g, kt) in enumerate(U):
                        if i + 2 < len(U):
                            scores_g(i + 2)
                        first = g == 0 and kt == 0
                        if first and qt >= 2:
                            pe.wait_ge(otoks.sem, otoks.at(s, qt - 1))
                        values_product(i, i % 4, g, P, kt, qt, first)
                        if i == 1:
                            pe.wait_ge(cw_ready.sem, cw_ready.at(s, 1))
                            for t in range(T):
                                ins = nc.tensor.matmul(misc[0:E + 1, t * P:(t + 1) * P], cw[:, t, :], ident, start=True, stop=True)
                            cw_turn.inc(ins)
                        for q in range(T - 1):
                            if i == ENDS[q] + 3:
                                turn_out(q, q * P, P)
                            if i == ENDS[q] + 7:
                                project_out(q, wo_g, q + 1)
                        if i in SECOND_G:
                            second()
                    while ypsum.n < 12:
                        second()
                    turn_out(T - 1, (T - 1) * P, P)
                    attn.inc(project_out(T - 1, wo_g, T))

                    turn(1, y2, normed2)
                    pe.wait_ge(attn_used.sem, attn_used.at(s, 1))
                    pe.wait_ge(yused.sem, yused.at(s, 12))
                    for t in range(T):
                        nc.tensor.matmul(qkv(t, 0, QK), y2T[:, t * P:(t + 1) * P], wl[:, 0:QK], start=True, stop=True)
                    for b, (q0, nq, k0) in enumerate(LOCAL):
                        ins = nc.tensor.matmul(misc[:, b * 32:(b + 1) * 32], y2T[:, k0:k0 + P], wl[:, QK:QK + 32], start=True, stop=True)
                    projected.inc(ins)
                    for k in range(3, 6):
                        hidden(k)
                    turn_heads(1, 12 + len(U) + 12)
                    pe.wait_ge(values.sem, values.at(s, 2))
                    U = LOCAL_UNITS

                    def scores_l(i):
                        b, g = U[i]
                        q0, nq, k0 = LOCAL[b]
                        scores(g, k0, q0, nq, (1, q0 - k0))
                    scores_l(0)
                    scores_l(1)
                    for i, (b, g) in enumerate(U):
                        if i + 2 < len(U):
                            scores_l(i + 2)
                        q0, nq, k0 = LOCAL[b]
                        if g == 0:
                            pe.wait_ge(otoks.sem, otoks.at(s, T + b - 1))
                        values_product(len(GLOBAL_UNITS) + i, i % 4, g, nq, b, b, g == 0)
                        if b and g == 2:
                            turn_out(b - 1, *LOCAL[b - 1][0:2])
                        if i in SECOND_L:
                            second()
                    while ypsum.n < 24:
                        second()
                    turn_out(len(LOCAL) - 1, *LOCAL[-1][0:2])
                    for t in range(T):
                        ins = project_out(t, wo_l, T + len(LOCAL))
                    attn.inc(ins)

                def some(k):
                    for _ in range(k if l0 else 0):
                        second()
                if l1:
                    l1_turn()
                if l0:
                    hidden(6)
                if l1:
                    if l0:
                        pe.wait_ge(attn_used.sem, attn_used.at(s, 2))
                        pe.wait_ge(yused.sem, yused.at(s, 24))
                    l1_logits_values()
                    l1_project(0)
                if l0:
                    hidden(7)
                if l1:
                    l1_project(1)
                if l0:
                    hidden(8)
                if l1:
                    l1_ranks()
                    l1_scores(0)
                    l1_scores(1)
                    pe.wait_ge(l_v1.sem, l_v1.at(r, 1))
                    some(2)
                    if l0:
                        pe.wait_ge(evac.sem, evac.at(s, RING_USES))
                    l1_turn_probs(0)
                    l1_scores(2)
                    some(2)
                    l1_turn_probs(1)
                    l1_pv(0)
                    l1_scores(3)
                    some(2)
                    l1_pv(1)
                    l1_turn_probs(2)
                    some(2)
                    l1_pv(2)
                    l1_turn_probs(3)
                    some(2)
                    l1_pv(3)
                if l0:
                    if not l1:
                        pe.wait_ge(evac.sem, evac.at(s, RING_USES))
                    while ypsum.n < 36:
                        second()
            sequences(pe, body)

            pe.wait_ge(l_out.sem, l_out.per * seqs)
            def turn_rows(e):
                if e >= 2:
                    pe.wait_ge(e_turned_sb, e - 1)
                pe.wait_ge(e_gathered[e], 16 * CC)
                for c in range(CC):
                    ins = nc.tensor.transpose(bank[e % 2][:, c * P:(c + 1) * P], xg[:, CC * e + c, :], ident)
                ins.then_inc(e_turned, 1)

            def hidden1(e):
                pe.wait_ge(e_turned_sb, e + 1)
                if e >= 2:
                    pe.wait_ge(e_gated, e - 1)
                for w, b in ((w_a, bank[2 + e % 2]), (w_b, bank[4 + e % 2])):
                    for c in range(HC1):
                        ins = nc.tensor.matmul(b[:, c * CAP:(c + 1) * CAP], w[:, e, c * P:(c + 1) * P], xgT[:, e % 2, :], start=True, stop=True)
                ins.then_inc(e_hidden, 1)

            def out1(e):
                pe.wait_ge(e_gated, e + 1)
                if e >= 2:
                    pe.wait_ge(e_yo, e - 1)
                for c in range(CC):
                    for k in range(HC1):
                        ins = nc.tensor.matmul(bank[6 + e % 2][:, c * P:(c + 1) * P], gT[:, e % 2, k, c * P:(c + 1) * P], w_o[:, e, k, :],
                                               start=(k == 0), stop=(k == HC1 - 1))
                ins.then_inc(e_y, 1)
            turn_rows(0)
            hidden1(0)
            for e in range(E):
                if e + 1 < E:
                    turn_rows(e + 1)
                    hidden1(e + 1)
                out1(e)



_INS = ['L0_attn_norm1_w', 'L0_attn_norm2_w', 'L0_attn_g_wq', 'L0_attn_g_kv_down', 'L0_attn_g_k_up',
        'L0_attn_g_v_up', 'L0_attn_g_wo', 'L0_attn_l_wq', 'L0_attn_l_wk', 'L0_attn_l_wv', 'L0_attn_l_wo',
        'L0_ffn_gate_w', 'L0_ffn_gate_b', 'L0_ffn_w1', 'L0_ffn_b1', 'L0_ffn_w2', 'L0_ffn_b2', 'L0_ffn_ws1',
        'L0_ffn_bs1', 'L0_ffn_ws2', 'L0_ffn_bs2', 'L1_attn_w_q', 'L1_attn_w_k', 'L1_attn_w_v',
        'L1_ffn_router_w', 'L1_ffn_router_b', 'L1_ffn_W', 'L1_ffn_V', 'L1_ffn_W_out']


def kernel(**inputs):
    import numpy as _np
    import concourse.bacc as _bacc
    from concourse import mybir as _mybir
    from concourse.bass_utils import run_bass_kernel_spmd as _run

    nc = _bacc.Bacc("TRN2", target_bir_lowering=False, num_devices=1)
    arrays, aps = {}, {}

    def given(name, key, v):
        arrays[name] = v
        aps[key] = nc.dram_tensor(name, v.shape, _mybir.dt.from_np(v.dtype), kind="ExternalInput").ap()
    given("x_dram", "x", _np.ascontiguousarray(inputs["L0_attn_hidden"]))
    given("shape_constants_dram", "shape_constants", shape_constants())
    given("zero_rows_dram", "zero_rows", _np.zeros((SLOTS, D), _np.float32))
    for n in _INS:
        given(f"in_{n}_dram", n, _np.ascontiguousarray(inputs[n]))
    out = nc.dram_tensor("out_0_dram", [TOKENS + SLOTS, D], _mybir.dt.float32, kind="ExternalOutput").ap()
    program(nc, aps, out)
    r = _run(nc, [arrays], core_ids=[0])
    return r.results[0]["out_0_dram"][0:TOKENS].reshape(SEQS, LEN, D)
```

```python
import numpy as np
import concourse.bass as bass
from concourse import mybir
from contextlib import ExitStack

F32 = mybir.dt.float32
F16 = mybir.dt.float16
BF16 = mybir.dt.bfloat16
I32 = mybir.dt.int32
ALU = mybir.AluOpType
ACT = mybir.ActivationFunctionType
AX = mybir.AxisListType

P = 128
SEQS, LEN, D = 16, 512, 128
T = LEN // P
TOKENS = SEQS * LEN
H, KVH = 16, 4
HD = D // H
J = H // KVH
QK = (H + KVH) * HD
LAT, WIN = 32, 32
E, HID = 8, 512
HC = HID // P
TOPK = 2
CAP = 2 * (2 * 256) * TOPK // 8
HID1 = 256
HC1 = HID1 // P
CC = CAP // P
SLOTS = E * CAP
VD = HD + 1
ATT_SCALE = 1.0 / float(np.sqrt(np.float32(HD)))
L1_SCALE = 1.0 / float(np.sqrt(np.float32(D)))
BIG = 1.0e30
NEG = -30000.0
LIFT = 7.0
W1_SCALE = 64.0
PARTS = 3
VROWS = 32

LOCAL = [(0, 96, 0), (96, 96, 64), (192, 96, 160), (288, 96, 256), (384, 96, 352), (480, 32, 384)]
GLOBAL_UNITS = [(qt, g, kt) for qt in range(T) for g in range(KVH) for kt in range(qt + 1)]
LOCAL_UNITS = [(b, g) for b in range(len(LOCAL)) for g in range(KVH)]
EXPERTS = [[0, 1, E], [2, 3, 4], [5, 6, 7]]
EARLY = T

CONST = {}
_at = 0
for _n, _w in [("ident", P), ("negmask", P), ("before", P), ("ones", P),
               ("cos_g", T * HD), ("sin_g", T * HD // 2), ("nsin_g", T * HD // 2),
               ("cos_l", T * HD), ("sin_l", T * HD // 2), ("nsin_l", T * HD // 2),
               ("negcausal", P), ("negband", P), ("cos1", LEN), ("sin1", LEN), ("iota", E), ("base", E), ("tok", T), ("len", T), ("half", T), ("dump", SLOTS // P * 2),
               ("sum_parts", KVH * VD)]:
    CONST[_n] = (_at, _at + _w)
    _at += _w
NCONST = _at
FIRST_LOADS, SECOND_LOADS, EXPERT_LOADS = 26, 3, 4


def shape_constants():
    f = np.float32
    c = np.zeros((P, NCONST), f)

    def put(name, x):
        a, b = CONST[name]
        c[:, a:b] = np.broadcast_to(np.asarray(x, f).reshape(-1, b - a), (P, b - a))

    i = np.arange(P)
    put("ident", np.eye(P))
    put("negcausal", np.where(i[:, None] <= i[None, :], 0.0, NEG))
    put("negband", np.where((i[None, :] - i[:, None] >= 0) & (i[None, :] - i[:, None] < WIN), 0.0, NEG))
    put("negmask", np.where(i[None, :] <= i[:, None], 0.0, -BIG))
    put("before", i[:, None] < i[None, :])
    put("ones", np.ones((P, P)))
    for n, base in (("g", 1000000.0), ("l", 10000.0)):
        inv = (f(1.0) / (f(base) ** (np.arange(0, HD, 2, dtype=f) / f(HD)))).astype(f)
        ang = (np.arange(LEN, dtype=f)[:, None] * inv[None, :]).astype(f).astype(np.float64)
        cos, sin = np.cos(ang), np.sin(ang)
        tiles = lambda x: x.reshape(T, P, -1).transpose(1, 0, 2).reshape(P, -1)
        put("cos_" + n, tiles(np.repeat(cos, 2, axis=1)))
        put("sin_" + n, tiles(sin))
        put("nsin_" + n, tiles(-sin))
    theta = np.power(f(10000.0), (f(-2.0) * (np.arange(D // 2, dtype=f) - f(1.0)) / f(D)).astype(f)).astype(f)
    ang = (np.arange(LEN, dtype=f)[:, None] * theta[None, :]).astype(f).astype(np.float64)
    put("cos1", np.repeat(np.cos(ang), 2, axis=1).T)
    put("sin1", (np.repeat(np.sin(ang), 2, axis=1) * np.tile([1.0, -1.0], D // 2)).T)
    put("iota", np.arange(E))
    put("base", np.arange(E) * CAP)
    put("tok", i[:, None] + P * np.arange(T)[None, :])
    put("len", np.full(T, LEN))
    put("half", np.full(T, -0.5))
    d = np.zeros((P, SLOTS // P, 2))
    d[:, :, 0] = TOKENS + i[:, None] + P * np.arange(SLOTS // P)[None, :]
    put("dump", d.reshape(P, -1))
    m = np.zeros((KVH, VROWS, KVH, VD))
    for g in range(KVH):
        for part in range(PARTS):
            m[g, part * VD:(part + 1) * VD, g, :] = np.eye(VD)
    put("sum_parts", m.reshape(P, -1))
    return c




RING_USES = 36 + len(GLOBAL_UNITS) + len(LOCAL_UNITS)
UNITS = len(GLOBAL_UNITS) + len(LOCAL_UNITS)
ENDS = [2 * (q + 1) * (q + 2) - 1 for q in range(T)]
SECOND_G = [7 + 4 * k + 2 * h for k in range(3 * T - EARLY) for h in range(2)]
COMBINE_G = [2, 3, 5, 6] + [10 + 4 * k for k in range(3 * T - EARLY)]
SECOND_L = [4 + 2 * k + h for k in range(3 * T - EARLY) for h in range(2)]
COMBINE_L = [6 + 2 * k for k in range(3 * T - EARLY)]
DVE_HIGHS = [i for i in range(6, len(GLOBAL_UNITS)) if i % 2 == 1]
POOL_LOWS = [i for i in range(UNITS) if i % 4 == 2]
LN_STEPS, VEC_STEPS, L_STEPS, SETUP_A, SETUP_B = 14, 98, 57, 11, 22


def program(nc, a, out, seqs=SEQS, dbg=None):
    ctx = ExitStack()
    with ctx, nc.allow_non_contiguous_dma("weights are laid out once"):
        def sb(name, shape, dt=F32):
            return ctx.enter_context(nc.sbuf_tensor(name, shape, dt))

        def sem(name):
            return ctx.enter_context(nc.semaphore(name))

        def scratch(name, shape):
            return nc.dram_tensor(name, shape, F32, kind="Internal").ap()

        tokens = seqs * LEN
        xn1_d = scratch("xn1_d", [tokens, D])
        slot_d = scratch("slot_d", [SLOTS, 2])

        consts = sb("consts", [P, NCONST])

        def const(name):
            return consts[:, CONST[name][0]:CONST[name][1]]
        ident = const("ident")
        ident16 = sb("ident16", [P, P], F16)
        masks16 = sb("masks16", [P, 2, P], F16)
        lift = sb("lift", [P, 1])
        w1_hi = sb("w1_hi", [P, E + 1, HID], F16)
        w1_lo = sb("w1_lo", [P, E + 1, HID], F16)
        w2 = sb("w2", [P, E + 1, HC, D])
        b1 = sb("b1", [P, E + 1, HC])
        b2 = sb("b2", [E + 1, D])
        gate_b = sb("gate_b", [P, E])
        wg_raw = sb("wg_raw", [P, D])
        wl_raw = sb("wl_raw", [P, D + 64])
        norm1 = sb("norm1", [P, 1])
        norm2 = sb("norm2", [P, 1])
        kv_down = sb("kv_down", [P, LAT])
        kv_downT = sb("kv_downT", [LAT, P])
        kv_up = sb("kv_up", [LAT, 64])
        wg = sb("wg", [P, QK + 32 + E])
        wl = sb("wl", [P, QK + 32])
        wo_g = sb("wo_g", [P, D])
        wo_l = sb("wo_l", [P, D])
        l1_raw = sb("l1_raw", [P, 3, D])
        wqk1 = sb("wqk1", [P, 4, D])
        wv1 = sb("wv1", [P, D])
        router = sb("router", [P, E])
        router_b = sb("router_b", [P, E])
        w_a = sb("w_a", [P, E, HID1])
        w_b = sb("w_b", [P, E, HID1])
        w_o = sb("w_o", [P, E, HC1, D])

        x = sb("x", [P, T, D])
        xn = sb("xn", [P, T, D])
        x1 = sb("x1", [P, T, D])
        y2 = sb("y2", [P, T, D])
        acc = sb("acc", [P, T, D])
        xnT = sb("xnT", [P, LEN])
        xnT_hi = sb("xnT_hi", [P, LEN], F16)
        xnT_lo = sb("xnT_lo", [P, LEN], F16)
        y2T = sb("y2T", [P, LEN])
        stats = sb("stats", [P, T, 6])
        mv = sb("mv", [P, T, 2])
        small = sb("small", [P, 12, T])
        VE, RSTD, E1, R1, EPS1, MS2, R2, SQ = range(8)
        NH = T * (H + KVH)
        t1 = sb("t1", [P, T, QK])
        t2 = sb("t2", [P, T, QK])
        msum = sb("msum", [P, NH])
        rq = sb("rq", [P, NH])
        rt = sb("rt", [P, 2, NH])
        qn = sb("qn", [P, T, QK])
        stack = sb("stack", [P, T, H + KVH, 4, HD], F16)
        QKT = sb("QKT", [P, J + 1, LEN], F16)
        vf = sb("vf", [P, 2, len(LOCAL), KVH, HD])
        V3 = sb("V3", [P, len(LOCAL), KVH, VROWS], BF16)
        probs = sb("probs", [P, 4, LEN])
        hi16 = sb("hi16", [P, 4, LEN], F16)
        lo16 = sb("lo16", [P, 4, LEN], F16)
        hidT = sb("hidT", [P, 3, HC, LEN])
        w1 = hidT[:, :, :, :].rearrange("p k c n -> p (k c n)")[:, 0:(E + 1) * HID].rearrange("p (e h) -> p e h", h=HID)
        oparts = sb("oparts", [P, 2, LEN])
        rden = sb("rden", [P, 2, J, KVH])
        otok = sb("otok", [P, 2, H, HD])
        oT = sb("oT", [P, LEN])
        lg = sb("lg", [P, T, E])
        gk = sb("gk", [P, T, E])
        l2 = sb("l2", [P, T, E])
        oh = sb("oh", [P, 2, T, E])
        km = sb("km", [P, 2, T])
        gm = sb("gm", [P, 2, T])
        gd = sb("gd", [P, 2, T])
        gw = sb("gw", [P, 2, T])
        cw = sb("cw", [P, T, E + 1])
        cwT = sb("cwT", [E + 1, LEN])
        xl = sb("xl", [P, T, D])
        xn1 = sb("xn1", [P, T, D])
        xn1T = sb("xn1T", [P, LEN])
        out_sb = sb("out_sb", [P, T, D])
        qk_turned = sb("qk_turned", [P, 2, LEN])
        rot = sb("rot", [P, 2, 2, LEN])
        v1 = sb("v1", [P, T, D])
        pr1 = sb("pr1", [P, 2, LEN])
        prT = sb("prT", [P, 2, T, P])
        top = sb("top", [P, 2, T])
        psums = sb("psums", [P, 2, T])
        oh1 = sb("oh1", [P, 2, T, E])
        gd1 = sb("gd1", [P, 2, T])
        chosen = sb("chosen", [P, T, E])
        before_t = sb("before_t", [P, T + 1, E])
        rank = sb("rank", [P, T, E])
        rsel = sb("rsel", [P, 2, 2, T, E])
        rk = sb("rk", [P, 2, 2, T])
        tok = sb("tok", [P, T])
        entry = sb("entry", [P, 2, T, 2])
        slot = sb("slot", [P, 2, T], I32)
        table = sb("table", [P, E * CC, 2])
        gather_at = sb("gather_at", [P, E * CC], I32)
        add_at = sb("add_at", [P, E * CC], I32)
        tclip = sb("tclip", [P, E * CC])
        xgT = sb("xgT", [P, 2, CAP])
        flat = lambda k: hidT[:, k, :, :].rearrange("p c n -> p (c n)")
        xg = flat(0).rearrange("p (c d) -> p c d", d=D)
        yo = flat(1).rearrange("p (c d) -> p c d", d=D)
        sig, gT = (flat(2)[:, h * 2 * HID1 * 2:(h + 1) * 2 * HID1 * 2].rearrange("p (i c n) -> p i c n", i=2, c=HC1) for h in range(2))

        small1 = sb("small1", [P, 2, T])

        bank = [ctx.enter_context(nc.psum_tensor(f"bank{i}", [P, 512], F32)) for i in range(8)]
        abank, ybank = bank[0], bank[1]
        ring = [bank[2], bank[3], bank[4]]

        def yslot(k):
            return (ring[2] if k >= 6 * T and k % 2 else ybank)[:, k % T * P:(k % T + 1) * P]

        obank = [bank[5], bank[6]]
        misc = bank[7]
        rot_banks = ((bank[5], bank[6]), (bank[0], bank[7]))

        def qkv(t, lo, hi):
            return bank[t // 2][:, (t % 2) * 256 + lo:(t % 2) * 256 + hi]

        def qkv2(half, lo, hi):
            return bank[half][:, :].rearrange("p (t n) -> p t n", t=2)[:, :, lo:hi]

        def as16(b):
            return b[:, 0:(J + 1) * P // 2].bitcast(F16).rearrange("p (b n) -> p b n", b=J + 1)

        def tiles(b):
            return b[:, :].rearrange("p (t d) -> p t d", t=T)

        S = []

        class Signal:
            def __init__(self, name, per):
                self.sem, self.per, self.name, self.n = sem(name), per, name, 0
                S.append(self)

            def inc(self, ins, by=1):
                self.n += by
                ins.then_inc(self.sem, by)

            def at(self, s, n):
                return s * self.per + n

        def count_anew():
            for g in S:
                assert g.n in (0, g.per), (g.name, g.n, g.per)
                g.n = 0

        weights_in = sem("weights_in")
        w2_in = sem("w2_in")
        experts_in = sem("experts_in")
        setup_dve = sem("setup_dve")
        setup_pe = sem("setup_pe")
        setup_act = sem("setup_act")

        x_loaded = Signal("x_loaded", 16)
        x_free = Signal("x_free", 1)
        ln = Signal("ln", LN_STEPS)
        ln_pow_in = Signal("ln_pow_in", 2)
        ln_pow_out = Signal("ln_pow_out", 2)
        normed = Signal("normed", T)
        vec = Signal("vec", VEC_STEPS)
        pow_in = Signal("pow_in", 1)
        pow_out = Signal("pow_out", 1)
        normed2 = Signal("normed2", T)
        turned = Signal("turned", 2)
        turned_sb = Signal("turned_sb", 2)
        xn_hi = Signal("xn_hi", 1)
        xn_lo = Signal("xn_lo", 1)
        projected = Signal("projected", 2)
        stacked = Signal("stacked", 4)
        stackT = Signal("stackT", 2 * T)
        heads = Signal("heads", 2 * T)
        qkv_read = Signal("qkv_read", 4)
        squared = Signal("squared", 4)
        values = Signal("values", 2)
        filled = Signal("filled", RING_USES)
        evac = Signal("evac", RING_USES)
        lows = Signal("lows", UNITS - len(POOL_LOWS))
        pool_lows = Signal("pool_lows", len(POOL_LOWS))
        highs = Signal("highs", len(DVE_HIGHS))
        pv = Signal("pv", UNITS)
        oparts_sb = Signal("oparts_sb", T + 6)
        osummed = Signal("osummed", T + 6)
        otoks = Signal("otoks", T + 6)
        oturn = Signal("oturn", T + 6)
        oT_sb = Signal("oT_sb", T + 6)
        attn = Signal("attn", 2)
        attn_used = Signal("attn_used", 2)
        ypsum = Signal("ypsum", 9 * T)
        yused = Signal("yused", 9 * T)
        gate_in = Signal("gate_in", 1)
        gate_exp = Signal("gate_exp", 1)
        cw_ready = Signal("cw_ready", 1)
        cw_turn = Signal("cw_turn", 1)
        cwT_sb = Signal("cwT_sb", 1)
        xl_ready = Signal("xl_ready", 1)
        l_vec = Signal("l_vec", L_STEPS)
        l_pow_in = Signal("l_pow_in", 1)
        l_pow_out = Signal("l_pow_out", 1)
        l_normed = Signal("l_normed", T)
        l_turned = Signal("l_turned", 1)
        l_turned_sb = Signal("l_turned_sb", 1)
        l_proj = Signal("l_proj", 4)
        l_lg = Signal("l_lg", 1)
        l_v1 = Signal("l_v1", 1)
        l_rotated = Signal("l_rotated", 2)
        l_gate_in = Signal("l_gate_in", 1)
        l_gate_exp = Signal("l_gate_exp", 1)
        l_chosen = Signal("l_chosen", 1)
        l_rank = Signal("l_rank", 1)
        l_ranked = Signal("l_ranked", 1)
        l_entries = Signal("l_entries", 1)
        tok_next = Signal("tok_next", 1)
        l_scattered = Signal("l_scattered", 16 * 2 * T)
        l_scores = Signal("l_scores", T)
        l_max = Signal("l_max", T)
        l_exp = Signal("l_exp", T)
        l_prT = Signal("l_prT", T)
        l_prT_sb = Signal("l_prT_sb", T)
        l_pv = Signal("l_pv", T)
        l_out = Signal("l_out", T)
        xn1_stored = Signal("xn1_stored", 16)
        out_stored = Signal("out_stored", 16)
        table_in = sem("table_in")
        e_vec = sem("e_vec")
        e_index = sem("e_index")
        e_gathered = [sem(f"e_gathered{e}") for e in range(E)]
        e_turned = sem("e_turned")
        e_turned_sb = sem("e_turned_sb")
        e_hidden = sem("e_hidden")
        e_sig = sem("e_sig")
        e_gated = sem("e_gated")
        e_y = sem("e_y")
        e_yo = sem("e_yo")
        e_added = sem("e_added")

        block = ctx.enter_context(nc.Block())

        def sequences(eng, body):
            count_anew()
            body(0, True, False)
            count_anew()
            if seqs > 1:
                with eng.Fori(1, seqs) as s:
                    body(s, True, True)
                count_anew()
            body(seqs, False, True)
            count_anew()

        @block.sync
        def _(sp):
            def load(dst, src, done=weights_in):
                sp.dma_start(dst, src).then_inc(done, 16)
            x_by_seq = a["x"].rearrange("s (t p) d -> s p t d", p=P)
            sp.dma_start(x[:, :, :], x_by_seq[0]).then_inc(x_loaded.sem, 16)
            load(consts[:, :], a["shape_constants"])
            load(norm1[:, 0:1], a["L0_attn_norm1_w"].rearrange("(p o) -> p o", o=1))
            load(norm2[:, 0:1], a["L0_attn_norm2_w"].rearrange("(p o) -> p o", o=1))
            load(wg_raw[:, :], a["L0_attn_g_wq"])
            load(kv_down[:, :], a["L0_attn_g_kv_down"])
            load(kv_up[:, 0:32], a["L0_attn_g_k_up"])
            load(kv_up[:, 32:64], a["L0_attn_g_v_up"])
            load(wl_raw[:, 0:D], a["L0_attn_l_wq"])
            load(wl_raw[:, D:D + 32], a["L0_attn_l_wk"])
            load(wl_raw[:, D + 32:D + 64], a["L0_attn_l_wv"])
            load(wo_g[:, :], a["L0_attn_g_wo"])
            load(wo_l[:, :], a["L0_attn_l_wo"])
            load(wg[:, QK + 32:QK + 32 + E], a["L0_ffn_gate_w"])
            load(gate_b[:, :], a["L0_ffn_gate_b"].partition_broadcast(P))
            load(w1[:, 0:E, :], a["L0_ffn_w1"].rearrange("e d h -> d e h"))
            load(w1[:, E, :], a["L0_ffn_ws1"])
            load(b1[:, 0:E, :].rearrange("p e c -> p (e c)"), a["L0_ffn_b1"].rearrange("e (c p) -> p (e c)", p=P))
            load(b1[:, E, :], a["L0_ffn_bs1"].rearrange("(c p) -> p c", p=P))
            load(b2[0:E, :], a["L0_ffn_b2"])
            load(b2[E:E + 1, :], a["L0_ffn_bs2"].rearrange("(o d) -> o d", o=1))
            load(slot_d.rearrange("(c p) w -> p c w", p=P), a["shape_constants"][:, CONST["dump"][0]:CONST["dump"][1]].rearrange("p (c w) -> p c w", w=2))
            load(l1_raw[:, 0, :], a["L1_attn_w_q"])
            load(l1_raw[:, 1, :], a["L1_attn_w_k"])
            load(l1_raw[:, 2, :], a["L1_attn_w_v"])
            load(router[:, :], a["L1_ffn_router_w"].rearrange("e d -> d e"))
            load(router_b[:, :], a["L1_ffn_router_b"].partition_broadcast(P))
            load(w2[:, E, :, :], a["L0_ffn_ws2"].rearrange("(c p) d -> p c d", p=P), w2_in)
            for e in range(0, E, 4):
                load(w2[:, e:e + 4, :, :].rearrange("p e c d -> p (e c) d"),
                     a["L0_ffn_w2"][e:e + 4].rearrange("e (c p) d -> p (e c) d", p=P), w2_in)
            load(w_a[:, :, :], a["L1_ffn_W"].rearrange("e d h -> d e h"), experts_in)
            load(w_b[:, :, :], a["L1_ffn_V"].rearrange("e d h -> d e h"), experts_in)
            load(w_o[:, :, :, :].rearrange("p e c d -> p (e c) d"), a["L1_ffn_W_out"].rearrange("e (c p) d -> p (e c) d", p=P), experts_in)
            load(out[TOKENS:TOKENS + SLOTS, :].rearrange("(r p) d -> p r d", p=P), a["zero_rows"].rearrange("(r p) d -> p r d", p=P), experts_in)
            xn1_by_seq = xn1_d.rearrange("(s t p) d -> s p t d", p=P, t=T)
            out_by_seq = out[0:tokens, :].rearrange("(s t p) d -> s p t d", p=P, t=T)

            def body(s, l0, l1):
                if l0:
                    sp.wait_ge(x_free.sem, s + 1)
                    sp.dma_start(x[:, :, :], x_by_seq[(s + 1) % seqs]).then_inc(x_loaded.sem, 16)
                if l1:
                    r = s - 1
                    sp.wait_ge(l_normed.sem, l_normed.at(r, T))
                    sp.dma_start(xn1_by_seq[r], xn1[:, :, :]).then_inc(xn1_stored.sem, 16)
                    sp.wait_ge(l_out.sem, l_out.at(r, T))
                    sp.dma_start(out_by_seq[r], out_sb[:, :, :]).then_inc(out_stored.sem, 16)
            sequences(sp, body)
            sp.wait_ge(l_scattered.sem, l_scattered.per * seqs)
            sp.dma_start(table[:, :, :], slot_d.rearrange("(c p) w -> p c w", p=P)).then_inc(table_in, 16)
            sp.wait_ge(x_loaded.sem, x_loaded.per * (seqs + 1))
            sp.wait_ge(xn1_stored.sem, 16 * (seqs + 1))
            sp.wait_ge(out_stored.sem, 16 * (seqs + 1))
            sp.wait_ge(e_added, 16 * E * CC)

        @block.gpsimd
        def _(pool):
            pool.wait_ge(weights_in, FIRST_LOADS * 16)

            def power(s, given, done, dst, src):
                pool.wait_ge(given.sem, given.at(s, done.n + 1))
                done.inc(nc.gpsimd.tensor_tensor(dst, src, const("half"), ALU.pow))

            def norm_powers(s):
                power(s, ln_pow_in, ln_pow_out, small[:, RSTD, :], small[:, VE, :])
                power(s, ln_pow_in, ln_pow_out, small[:, R1, :], small[:, E1, :])

            def body(s, l0, l1):
                if l0:
                    pool.wait_ge(xn_hi.sem, xn_hi.at(s, 1))
                    xn_lo.inc(nc.gpsimd.tensor_tensor(xnT_lo[:, :], xnT[:, :], xnT_hi[:, :], ALU.subtract))
                if l1:
                    power(s - 1, l_pow_in, l_pow_out, small1[:, 1, :], small1[:, 0, :])
                def lows_of(first, units, before, n):
                    for i in units:
                        pool.wait_ge(evac.sem, evac.at(s, before + i - first + 1))
                        w = n(i - first)
                        slot = (i - first) % 4
                        pool_lows.inc(nc.gpsimd.tensor_tensor(lo16[:, slot, 0:w], probs[:, slot, 0:w], hi16[:, slot, 0:w], ALU.subtract))
                if l0:
                    G = len(GLOBAL_UNITS)
                    lows_of(0, [i for i in POOL_LOWS if i < G], 12, lambda i: J * P)
                    power(s, pow_in, pow_out, small[:, R2, :], small[:, MS2, :])
                    lows_of(G, [i for i in POOL_LOWS if i >= G], 12 + G + 12, lambda i: J * LOCAL[LOCAL_UNITS[i][0]][1])
                    norm_powers(s + 1)
                if l1:
                    r = s - 1
                    pool.wait_ge(l_entries.sem, l_entries.at(r, 1))
                    tok_next.inc(nc.gpsimd.tensor_tensor(tok[:, :], tok[:, :], const("len"), ALU.add))
                    for k in range(2):
                        for t in range(T):
                            l_scattered.inc(nc.gpsimd.indirect_dma_start(
                                slot_d, bass.IndirectOffsetOnAxis(ap=slot[:, k, t:t + 1], axis=0), entry[:, k, t, :], None,
                                bounds_check=SLOTS - 1, oob_is_err=False), 16)
                    pool.wait_ge(l_scattered.sem, l_scattered.at(r, l_scattered.per))
            norm_powers(0)
            sequences(pool, body)

            pool.wait_ge(experts_in, EXPERT_LOADS * 16)
            pool.wait_ge(e_index, 1)
            pool.wait_ge(xn1_stored.sem, 16 * (seqs + 1))
            for c in range(E * CC):
                nc.gpsimd.indirect_dma_start(xg[:, c, :], None, xn1_d, bass.IndirectOffsetOnAxis(ap=gather_at[:, c:c + 1], axis=0),
                                             bounds_check=tokens - 1, oob_is_err=True).then_inc(e_gathered[c // CC], 16)
            pool.wait_ge(out_stored.sem, 16 * (seqs + 1))
            for e in range(E):
                pool.wait_ge(e_yo, e + 1)
                if e:
                    pool.wait_ge(e_added, 16 * CC * e)
                for c in range(CC * e, CC * e + CC):
                    nc.gpsimd.indirect_dma_start(out, bass.IndirectOffsetOnAxis(ap=add_at[:, c:c + 1], axis=0), yo[:, c, :], None,
                                                 bounds_check=TOKENS + SLOTS - 1, oob_is_err=True, compute_op=ALU.add).then_inc(e_added, 16)

        @block.scalar
        def _(act):
            act.wait_ge(weights_in, FIRST_LOADS * 16)
            nc.scalar.activation(w1_hi[:, :, :], w1, ACT.Copy, scale=W1_SCALE).then_inc(setup_act, 1)

            def body(s, l0, l1):
                r = s - 1

                def turned_copy(i, dst):
                    act.wait_ge(turned.sem, turned.at(s, i + 1))
                    turned_sb.inc(nc.scalar.activation(dst, misc[:, :], ACT.Copy))

                gelus_done = [0]

                def gelus(n):
                    for _ in range(n):
                        k, c = gelus_done[0] // HC, gelus_done[0] % HC
                        gelus_done[0] += 1
                        if c == 0 and k % 3 == 0 and (k or not (isinstance(s, int) and s == 0)):
                            act.wait_ge(ypsum.sem, ypsum.at(s, T * k))
                        e = sum(EXPERTS, [])[k]
                        act.wait_ge(filled.sem, filled.at(s, evac.n + 1))
                        evac.inc(nc.scalar.activation(hidT[:, k % 3, c, :], ring[evac.n % 3][:, :], ACT.Gelu, bias=b1[:, e, c:c + 1],
                                                       scale=1.0 / W1_SCALE))

                def squares(i, h):
                    act.wait_ge(qkv_read.sem, qkv_read.at(s, 2 * i + h + 1))
                    squared.inc(nc.scalar.activation(qn[:, 2 * h:2 * h + 2, :], qkv2(h, 0, QK), ACT.Square))

                def heads_copies():
                    for t in range(T):
                        act.wait_ge(stackT.sem, stackT.at(s, heads.n + 1))
                        heads.inc(nc.scalar.activation(QKT[:, :, t * P:(t + 1) * P], as16(ring[t % 3]), ACT.Copy))

                def exps(i, first, n):
                    if i >= 4:
                        act.wait_ge(pv.sem, pv.at(s, first + i - 3))
                    b = ring[evac.n % 3]
                    act.wait_ge(filled.sem, filled.at(s, evac.n + 1))
                    ins = nc.scalar.activation(probs[:, i % 4, 0:n], b[:, 0:n], ACT.Exp, bias=lift[:, 0:1], scale=ATT_SCALE)
                    if first + i in DVE_HIGHS:
                        evac.inc(ins)
                    else:
                        evac.inc(nc.scalar.activation(hi16[:, i % 4, 0:n], b[:, 0:n], ACT.Exp, bias=lift[:, 0:1], scale=ATT_SCALE))

                def oparts_copy(blk, nq, last_unit):
                    if oparts_sb.n >= 2:
                        act.wait_ge(osummed.sem, osummed.at(s, oparts_sb.n - 1))
                    act.wait_ge(pv.sem, pv.at(s, last_unit + 1))
                    oparts_sb.inc(nc.scalar.activation(oparts[:, blk % 2, 0:J * nq], obank[blk % 2][:, 0:J * nq], ACT.Copy))

                def l1_stream_copy():
                    act.wait_ge(l_turned.sem, l_turned.at(r, 1))
                    l_turned_sb.inc(nc.scalar.activation(xn1T[:, :], abank[:, :], ACT.Copy))

                def l1_values_copy():
                    act.wait_ge(l_proj.sem, l_proj.at(r, 2))
                    l_v1.inc(nc.scalar.activation(v1[:, :, :].rearrange("p t d -> p (t d)"), abank[:, :], ACT.Copy))

                def l1_gate():
                    act.wait_ge(l_gate_in.sem, l_gate_in.at(r, 1))
                    l_gate_exp.inc(nc.scalar.activation(gd1[:, 1, :], gd1[:, 0, :], ACT.Exp))

                if l0:
                    turned_copy(0, xnT[:, :])
                    xn_hi.inc(nc.scalar.activation(xnT_hi[:, :], misc[:, :], ACT.Copy))
                    gelus(1)
                    squares(0, 0)
                    gelus(1)
                    squares(0, 1)
                    gelus(3 * HC - 2)
                    heads_copies()
                    for i in range(len(GLOBAL_UNITS)):
                        if i == 1:
                            act.wait_ge(gate_in.sem, gate_in.at(s, 1))
                            gate_exp.inc(nc.scalar.activation(gd[:, 1, :], gd[:, 0, :], ACT.Exp))
                        exps(i, 0, J * P)
                        for q in range(T - 1):
                            if i == ENDS[q] + 2:
                                oparts_copy(q, P, ENDS[q])
                    oparts_copy(T - 1, P, ENDS[T - 1])
                    gelus(HC)
                    turned_copy(1, y2T[:, :])
                    gelus(1)
                    squares(1, 0)
                    gelus(1)
                    squares(1, 1)
                    gelus(2 * HC - 2)
                    heads_copies()
                    for i, (b, g) in enumerate(LOCAL_UNITS):
                        exps(i, len(GLOBAL_UNITS), J * LOCAL[b][1])
                        if b and g == 1:
                            oparts_copy(b - 1, LOCAL[b - 1][1], len(GLOBAL_UNITS) + 4 * b - 1)
                        if l1 and i == 4:
                            l1_stream_copy()
                        if l1 and i == 11:
                            l1_values_copy()
                        if l1 and i == 20:
                            l1_gate()
                    oparts_copy(len(LOCAL) - 1, LOCAL[-1][1], UNITS - 1)
                    gelus(3 * HC)
                else:
                    l1_stream_copy()
                    l1_values_copy()
                    l1_gate()
                if l1:
                    for qt in range(T):
                        n = (qt + 1) * P
                        act.wait_ge(l_max.sem, l_max.at(r, qt + 1))
                        if qt >= 2:
                            act.wait_ge(l_prT.sem, l_prT.at(r, qt - 1))
                        l_exp.inc(nc.scalar.activation(pr1[:, qt % 2, 0:n], obank[qt % 2][:, 0:n], ACT.Exp, bias=top[:, 1, qt:qt + 1],
                                                       scale=L1_SCALE, accum_out=psums[:, 0, qt:qt + 1]))
            sequences(act, body)

            for e in range(E):
                act.wait_ge(e_hidden, e + 1)
                if e >= 2:
                    act.wait_ge(e_gated, e - 1)
                nc.scalar.activation(sig[:, e % 2, :, :].rearrange("p c n -> p (c n)"), bank[4 + e % 2][:, :], ACT.Sigmoid).then_inc(e_sig, 1)

        @block.vector
        def _(v):
            v.wait_ge(weights_in, FIRST_LOADS * 16)
            step = [0]

            def setup(ins):
                step[0] += 1
                ins.then_inc(setup_dve, 1)
                v.wait_ge(setup_dve, step[0])

            setup(nc.vector.tensor_copy(ident16[:, :], ident))
            setup(nc.vector.tensor_copy(masks16[:, 0, :], const("negcausal")))
            setup(nc.vector.tensor_copy(masks16[:, 1, :], const("negband")))
            setup(nc.vector.memset(lift[:, :], LIFT))
            setup(nc.vector.memset(V3[:, :, :, :], 0.0))
            setup(nc.vector.memset(V3[:, :, :, HD:VD], 1.0))
            setup(nc.vector.memset(cw[:, :, E:E + 1], 1.0))
            for dst, raw, nrm in ((wg, wg_raw, norm1), (wl, wl_raw, norm2)):
                setup(nc.vector.tensor_scalar(dst[:, 0:D].rearrange("p (j g d) -> p j g d", j=J, g=KVH),
                                              raw[:, 0:D].rearrange("p (g j d) -> p j g d", j=J, g=KVH),
                                              nrm[:, 0:1], None, ALU.mult))
            setup(nc.vector.tensor_scalar(wl[:, D:D + 64], wl_raw[:, D:D + 64], norm2[:, 0:1], None, ALU.mult))
            v.wait_ge(setup_pe, 1)
            setup(nc.vector.tensor_copy(kv_downT[:, :], bank[0][0:LAT, 0:P]))
            assert step[0] == SETUP_A
            v.wait_ge(setup_pe, 2)
            setup(nc.vector.tensor_scalar(wg[:, D:D + 64], bank[1][:, 0:64], norm1[:, 0:1], None, ALU.mult))
            for i in range(2):
                src = bank[2 + i][:, 0:P]
                swapped = wqk1[:, 2 * i + 1, :].rearrange("p (n e) -> p n e", e=2)
                v.wait_ge(setup_pe, 3 + i)
                setup(nc.vector.tensor_copy(wqk1[:, 2 * i, :], src))
                for e in range(2):
                    setup(nc.vector.tensor_copy(swapped[:, :, e], src.rearrange("p (n e) -> p n e", e=2)[:, :, 1 - e]))
            v.wait_ge(setup_pe, 5)
            setup(nc.vector.tensor_copy(wv1[:, :], bank[4][:, 0:P]))
            v.wait_ge(setup_act, 1)
            setup(nc.vector.scalar_tensor_tensor(w1_lo[:, :, :], w1, W1_SCALE, w1_hi[:, :, :], ALU.mult, ALU.subtract))
            setup(nc.vector.tensor_copy(tok[:, :], const("tok")))
            setup(nc.vector.memset(before_t[:, T, :], 0.0))
            nc.vector.memset(small[:, 9, :], 0.0).then_inc(xn1_stored.sem, 16)
            nc.vector.memset(small[:, 10, :], 0.0).then_inc(out_stored.sem, 16)
            assert step[0] == SETUP_B

            def pick(chained, k, oh):
                wide = lambda z: z.unsqueeze(2).to_broadcast([P, T, E])
                iota = const("iota").unsqueeze(1).to_broadcast([P, T, E])
                src = l2 if k else lg
                chained(nc.vector.tensor_reduce(gm[:, k, :], src[:, :, :], AX.X, ALU.max))
                chained(nc.vector.tensor_tensor(gk[:, :, :], src[:, :, :], wide(gm[:, k, :]), ALU.is_equal))
                chained(nc.vector.scalar_tensor_tensor(gk[:, :, :], gk[:, :, :], -16.0, iota, ALU.mult, ALU.add))
                chained(nc.vector.tensor_reduce(km[:, k, :], gk[:, :, :], AX.X, ALU.min))
                chained(nc.vector.tensor_tensor(oh[:, k, :, :], gk[:, :, :], wide(km[:, k, :]), ALU.is_equal))
                if k == 0:
                    chained(nc.vector.scalar_tensor_tensor(l2[:, :, :], oh[:, 0, :, :], -BIG, src[:, :, :], ALU.mult, ALU.add))

            def moments(s, sig, src):
                def wait():
                    v.wait_ge(sig.sem, sig.at(s, sig.n))
                for t in range(T):
                    sig.inc(nc.vector.bn_stats(stats[:, t, :], src[:, t, :]))
                wait()
                m = small[:, 8:11, :]
                sig.inc(nc.vector.tensor_tensor(m[:, 0, :], stats[:, :, 1], stats[:, :, 4], ALU.add))
                sig.inc(nc.vector.tensor_tensor(m[:, 1, :], stats[:, :, 1], stats[:, :, 4], ALU.subtract))
                sig.inc(nc.vector.tensor_tensor(m[:, 2, :], stats[:, :, 2], stats[:, :, 5], ALU.add))
                wait()
                sig.inc(nc.vector.tensor_scalar(mv[:, :, 0], m[:, 0, :], 0.5, None, ALU.mult))
                sig.inc(nc.vector.tensor_tensor(m[:, 1, :], m[:, 1, :], m[:, 1, :], ALU.mult))
                sig.inc(nc.vector.tensor_scalar(m[:, 2, :], m[:, 2, :], 1.0 / D, None, ALU.mult))
                wait()
                sig.inc(nc.vector.scalar_tensor_tensor(mv[:, :, 1], m[:, 1, :], 0.25, m[:, 2, :], ALU.mult, ALU.add))
                wait()

            def layer_moments(s):
                v.wait_ge(x_loaded.sem, x_loaded.at(s, 16))
                moments(s, ln, x)
                ln_pow_in.inc(nc.vector.tensor_scalar(small[:, VE, :], mv[:, :, 1], 1e-5, None, ALU.add))

            def layer_norm(s):
                def chained(ins):
                    ln.inc(ins)
                    v.wait_ge(ln.sem, ln.at(s, ln.n))
                v.wait_ge(ln_pow_out.sem, ln_pow_out.at(s, 1))
                for t in range(T):
                    normed.inc(nc.vector.tensor_scalar(xn[:, t, :], x[:, t, :], mv[:, t, 0:1], small[:, RSTD, t:t + 1],
                                                       ALU.subtract, ALU.mult))
                chained(nc.vector.tensor_tensor(small[:, SQ, :], small[:, RSTD, :], small[:, RSTD, :], ALU.mult))
                chained(nc.vector.tensor_tensor(small[:, SQ, :], small[:, SQ, :], mv[:, :, 1], ALU.mult))
                ln_pow_in.inc(nc.vector.tensor_scalar(small[:, E1, :], small[:, SQ, :], 1e-6, None, ALU.add))
                v.wait_ge(ln_pow_in.sem, ln_pow_in.at(s, 2))
                chained(nc.vector.tensor_scalar(small[:, EPS1, :], small[:, E1, :], 1e-6, None, ALU.mult))
                x_free.inc(nc.vector.tensor_tensor(x1[:, :, :], x[:, :, :], xn[:, :, :], ALU.add))

            def l1_moments(r):
                v.wait_ge(xn1_stored.sem, xn1_stored.at(r, 16))
                moments(r, l_vec, xl)
                l_pow_in.inc(nc.vector.tensor_scalar(small1[:, 0, :], mv[:, :, 1], 1e-5, None, ALU.add))

            def l1_norm(r, ts):
                if ts[0] == 0:
                    v.wait_ge(l_pow_out.sem, l_pow_out.at(r, 1))
                for t in ts:
                    l_normed.inc(nc.vector.tensor_scalar(xn1[:, t, :], xl[:, t, :], mv[:, t, 0:1], small1[:, 1, t:t + 1],
                                                         ALU.subtract, ALU.mult))

            def body(s, l0, l1):
                r = s - 1

                def chained(ins):
                    vec.inc(ins)
                    v.wait_ge(vec.sem, vec.at(s, vec.n))

                def chained1(ins):
                    l_vec.inc(ins)
                    v.wait_ge(l_vec.sem, l_vec.at(r, l_vec.n))

                def rope(i, n, eps, read):
                    cos = const("cos_" + n).rearrange("p (t d) -> p t d", t=T)
                    sin = const("sin_" + n).rearrange("p (t d) -> p t d", t=T)
                    nsin = const("nsin_" + n).rearrange("p (t d) -> p t d", t=T)
                    for h in range(2):
                        ts = slice(2 * h, 2 * h + 2)
                        src = qkv2(h, 0, QK)
                        pairs = src.rearrange("p t (n d e) -> p t n d e", d=HD // 2, e=2)
                        to = t2[:, ts, :].rearrange("p t (n d e) -> p t n d e", d=HD // 2, e=2)
                        read(h)
                        vec.inc(nc.vector.tensor_tensor(
                            t1[:, ts, :].rearrange("p t (n d) -> p t n d", d=HD),
                            src.rearrange("p t (n d) -> p t n d", d=HD),
                            cos[:, ts, :].unsqueeze(2).to_broadcast([P, 2, H + KVH, HD]), ALU.mult))
                        for e, tab in ((0, nsin), (1, sin)):
                            (qkv_read if e else vec).inc(nc.vector.tensor_tensor(
                                to[:, :, :, :, e], pairs[:, :, :, :, 1 - e],
                                tab[:, ts, :].unsqueeze(2).to_broadcast([P, 2, H + KVH, HD // 2]), ALU.mult))
                    v.wait_ge(qkv_read.sem, qkv_read.at(s, 2 * i + 2))
                    chained(nc.vector.tensor_tensor(t1[:, :, :], t1[:, :, :], t2[:, :, :], ALU.add))
                    v.wait_ge(squared.sem, squared.at(s, 2 * i + 2))
                    chained(nc.vector.tensor_reduce(msum[:, :], qn[:, :, :].rearrange("p t (n d) -> p (t n) d", d=HD), AX.X, ALU.add))
                    if eps is None:
                        chained(nc.vector.tensor_scalar(msum[:, :], msum[:, :], 1.0 / HD, 1e-6, ALU.mult, ALU.add))
                    else:
                        m3 = msum[:, :].rearrange("p (t n) -> p t n", t=T)
                        chained(nc.vector.scalar_tensor_tensor(m3, m3, 1.0 / HD, eps.unsqueeze(2).to_broadcast([P, T, H + KVH]),
                                                               ALU.mult, ALU.add))
                    rsqrt()
                    for h in range(2):
                        ts = slice(2 * h, 2 * h + 2)
                        as3 = lambda z: z[:, ts, :].rearrange("p t (n d) -> p (t n) d", d=HD)
                        slots = stack[:, ts, :, :, :].rearrange("p t n s d -> p (t n) s d")
                        chained(nc.vector.tensor_tensor(as3(qn), as3(t1), rq[:, h * NH // 2:(h + 1) * NH // 2].unsqueeze(2).to_broadcast([P, NH // 2, HD]), ALU.mult))
                        chained(nc.vector.tensor_copy(slots[:, :, 0, :], as3(qn)))
                        chained(nc.vector.tensor_tensor(slots[:, :, 3, :], as3(qn), slots[:, :, 0, :], ALU.subtract))
                        for dst, src, lo, hi in ((1, 0, 0, H), (2, 3, 0, H), (2, 0, H, H + KVH), (1, 3, H, H + KVH)):
                            ins = nc.vector.tensor_copy(stack[:, ts, lo:hi, dst, :], stack[:, ts, lo:hi, src, :])
                        stacked.inc(ins)

                def rsqrt():
                    chained(nc.vector.tensor_scalar(rt[:, 0, :].bitcast(I32), msum[:, :].bitcast(I32), 1, None, ALU.arith_shift_right))
                    chained(nc.vector.tensor_scalar(rq[:, :].bitcast(I32), rt[:, 0, :].bitcast(I32), -1.0, float(0x5F3759DF), ALU.mult, ALU.add))
                    for _ in range(3):
                        chained(nc.vector.scalar_tensor_tensor(rt[:, 0, :], rq[:, :], -0.5, rq[:, :], ALU.mult, ALU.mult))
                        chained(nc.vector.tensor_tensor(rt[:, 1, :], rt[:, 0, :], msum[:, :], ALU.mult))
                        chained(nc.vector.scalar_tensor_tensor(rq[:, :], rt[:, 1, :], 1.5, rq[:, :], ALU.add, ALU.mult))

                def split_values(n):
                    full, rest = vf[:, 0, 0:n, :, :], vf[:, 1, 0:n, :, :]
                    part = [V3[:, 0:n, :, k * VD:k * VD + HD] for k in range(PARTS)]
                    chained(nc.vector.tensor_copy(part[0], full))
                    chained(nc.vector.tensor_tensor(rest, full, part[0], ALU.subtract))
                    chained(nc.vector.tensor_copy(part[1], rest))
                    values.inc(nc.vector.tensor_tensor(part[2], rest, part[1], ALU.subtract))

                def read_g(h):
                    if h == 0:
                        v.wait_ge(ln_pow_out.sem, ln_pow_out.at(s, 2))
                    ts = slice(2 * h, 2 * h + 2)
                    vec.inc(nc.vector.tensor_tensor(vf[:, 0, ts, :, :], qkv2(h, QK, QK + 32).rearrange("p t (g d) -> p t g d", g=KVH),
                                                    small[:, R1, ts].unsqueeze(2).unsqueeze(3).to_broadcast([P, 2, KVH, HD]), ALU.mult))
                    vec.inc(nc.vector.tensor_tensor(lg[:, ts, :], qkv2(h, QK + 32, QK + 32 + E),
                                                    gate_b[:, :].unsqueeze(1).to_broadcast([P, 2, E]), ALU.add))

                def read_l(h):
                    if h == 0:
                        vec.inc(nc.vector.tensor_copy(vf[:, 0, :, :, :], misc[:, 0:len(LOCAL) * 32].rearrange("p (b g d) -> p b g d", g=KVH, d=HD)))

                def gate_difference():
                    gate_in.inc(nc.vector.tensor_tensor(gd[:, 0, :], gm[:, 1, :], gm[:, 0, :], ALU.subtract))

                def gate_weights():
                    v.wait_ge(gate_exp.sem, gate_exp.at(s, 1))
                    wide = lambda z: z.unsqueeze(2).to_broadcast([P, T, E])
                    chained(nc.vector.tensor_scalar(gw[:, 0, :], gd[:, 1, :], 1.0, None, ALU.add))
                    chained(nc.vector.reciprocal(gw[:, 0, :], gw[:, 0, :]))
                    chained(nc.vector.tensor_tensor(gw[:, 1, :], gw[:, 0, :], gd[:, 1, :], ALU.mult))
                    for k in range(2):
                        chained(nc.vector.tensor_tensor(oh[:, k, :, :], oh[:, k, :, :], wide(gw[:, k, :]), ALU.mult))
                    cw_ready.inc(nc.vector.tensor_tensor(cw[:, :, 0:E], oh[:, 0, :, :], oh[:, 1, :, :], ALU.add))
                    v.wait_ge(cw_ready.sem, cw_ready.at(s, 1))

                def combine():
                    k = yused.n
                    t, e = k % T, sum(EXPERTS, [])[k // T]
                    v.wait_ge(ypsum.sem, ypsum.at(s, k - k % (3 * T) + EARLY if k % (3 * T) < EARLY and k < 6 * T else k + 1))
                    if k >= T:
                        v.wait_ge(yused.sem, yused.at(s, k - T + 1))
                    yused.inc(nc.vector.scalar_tensor_tensor(acc[:, t, :], yslot(k), cw[:, t, e:e + 1],
                                                             (acc if k >= T else x1)[:, t, :], ALU.mult, ALU.add))

                def low(i, use, slot, n, high=False):
                    if high or i not in POOL_LOWS:
                        v.wait_ge(evac.sem, evac.at(s, use + 1))
                    if high:
                        highs.inc(nc.vector.tensor_copy(hi16[:, slot, 0:n], probs[:, slot, 0:n]))
                        v.wait_ge(highs.sem, highs.at(s, highs.n))
                    if i not in POOL_LOWS:
                        lows.inc(nc.vector.tensor_tensor(lo16[:, slot, 0:n], probs[:, slot, 0:n], hi16[:, slot, 0:n], ALU.subtract))

                def divide(blk, nq):
                    k = blk % 2
                    v.wait_ge(osummed.sem, osummed.at(s, otoks.n + 1))
                    o = misc[0:nq, 0:H * VD].rearrange("p (j g d) -> p j g d", g=KVH, d=VD)
                    chained(nc.vector.reciprocal(rden[0:nq, k, :, :], o[:, :, :, HD]))
                    otoks.inc(nc.vector.tensor_tensor(otok[0:nq, k, :, :].rearrange("p (g j) d -> p j g d", g=KVH), o[:, :, :, 0:HD],
                                                      rden[0:nq, k, :, :].unsqueeze(3).to_broadcast([nq, J, KVH, HD]), ALU.mult))

                def oT_copy(q0, nq):
                    v.wait_ge(oturn.sem, oturn.at(s, oT_sb.n + 1))
                    oT_sb.inc(nc.vector.tensor_copy(oT[:, q0:q0 + nq], misc[:, q0:q0 + nq]))

                def l1_logits():
                    v.wait_ge(l_proj.sem, l_proj.at(r, 1))
                    l_lg.inc(nc.vector.tensor_tensor(lg[:, :, :], abank[:, 0:T * E].rearrange("p (t e) -> p t e", e=E),
                                                     router_b[:, :].unsqueeze(1).to_broadcast([P, T, E]), ALU.add))
                    v.wait_ge(l_lg.sem, l_lg.at(r, 1))

                def l1_counts():
                    l_gate_in.inc(nc.vector.tensor_tensor(gd1[:, 0, :], gm[:, 1, :], gm[:, 0, :], ALU.subtract))
                    chained1(nc.vector.tensor_tensor(chosen[:, :, :], oh1[:, 0, :, :], oh1[:, 1, :, :], ALU.add))
                    chained1(nc.vector.tensor_copy(before_t[:, 0, :], before_t[:, T, :]))
                    for t in range(T):
                        ins = nc.vector.tensor_tensor(before_t[:, t + 1, :], before_t[:, t, :], chosen[:, t, :], ALU.add)
                        (l_chosen.inc if t == T - 1 else chained1)(ins)

                def l1_rotate(i):
                    v.wait_ge(l_proj.sem, l_proj.at(r, 3 + i))
                    for h, tab in ((0, "cos1"), (1, "sin1")):
                        l_vec.inc(nc.vector.tensor_tensor(rot[:, i, h, :], rot_banks[i][h][:, :], const(tab), ALU.mult))
                    v.wait_ge(l_vec.sem, l_vec.at(r, l_vec.n))
                    l_rotated.inc(nc.vector.tensor_tensor(qk_turned[:, i, :], rot[:, i, 0, :], rot[:, i, 1, :], ALU.add))

                def l1_rank_copy():
                    v.wait_ge(l_rank.sem, l_rank.at(r, 1))
                    l_ranked.inc(nc.vector.tensor_copy(rank[:, :, :], misc[:, 0:T * E].rearrange("p (t e) -> p t e", e=E)))
                    v.wait_ge(l_ranked.sem, l_ranked.at(r, 1))

                def l1_slots():
                    v.wait_ge(l_gate_exp.sem, l_gate_exp.at(r, 1))
                    chained1(nc.vector.tensor_scalar(gw[:, 0, :], gd1[:, 1, :], 1.0, None, ALU.add))
                    chained1(nc.vector.reciprocal(gw[:, 0, :], gw[:, 0, :]))
                    chained1(nc.vector.tensor_tensor(gw[:, 1, :], gw[:, 0, :], gd1[:, 1, :], ALU.mult))
                    for k in range(2):
                        l_vec.inc(nc.vector.tensor_copy(entry[:, k, :, 0], tok[:, :]))
                        l_vec.inc(nc.vector.tensor_copy(entry[:, k, :, 1], gw[:, k, :]))
                    for k in range(2):
                        l_vec.inc(nc.vector.tensor_tensor(rsel[:, k, 0, :, :], oh1[:, k, :, :], rank[:, :, :], ALU.mult))
                        l_vec.inc(nc.vector.tensor_tensor(rsel[:, k, 1, :, :], oh1[:, k, :, :], const("base").unsqueeze(1).to_broadcast([P, T, E]), ALU.mult))
                    v.wait_ge(l_vec.sem, l_vec.at(r, l_vec.n))
                    chained1(nc.vector.tensor_reduce(rk[:, :, :, :].rearrange("p a b t -> p (a b t)"),
                                                     rsel[:, :, :, :, :].rearrange("p a b t e -> p (a b t) e"), AX.X, ALU.add))
                    chained1(nc.vector.tensor_tensor(rk[:, :, 1, :], rk[:, :, 1, :], rk[:, :, 0, :], ALU.add))
                    chained1(nc.vector.tensor_scalar(rk[:, :, 0, :], rk[:, :, 0, :], float(CAP), 1.0e6, ALU.is_ge, ALU.mult))
                    l_entries.inc(nc.vector.tensor_tensor(slot[:, :, :], rk[:, :, 1, :], rk[:, :, 0, :], ALU.add))

                def peak(qt):
                    n = (qt + 1) * P
                    sc = obank[qt % 2]
                    v.wait_ge(l_scores.sem, l_scores.at(r, qt + 1))
                    chained1(nc.vector.tensor_tensor(sc[:, n - P:n], sc[:, n - P:n], const("negmask"), ALU.add))
                    chained1(nc.vector.tensor_reduce(top[:, 0, qt:qt + 1], sc[:, 0:n], AX.X, ALU.max))
                    l_max.inc(nc.vector.tensor_scalar(top[:, 1, qt:qt + 1], top[:, 0, qt:qt + 1], -L1_SCALE, None, ALU.mult))

                def probs_copy(qt):
                    n = (qt + 1) * P
                    v.wait_ge(l_prT.sem, l_prT.at(r, qt + 1))
                    l_prT_sb.inc(nc.vector.tensor_copy(prT[:, qt % 2, :, :].rearrange("p t n -> p (t n)")[:, 0:n], ring[qt % 2][:, 0:n]))

                def finish(qt):
                    if qt == 0:
                        v.wait_ge(out_stored.sem, out_stored.at(r, 16))
                    v.wait_ge(l_exp.sem, l_exp.at(r, qt + 1))
                    chained1(nc.vector.reciprocal(psums[:, 1, qt:qt + 1], psums[:, 0, qt:qt + 1]))
                    v.wait_ge(l_pv.sem, l_pv.at(r, qt + 1))
                    l_out.inc(nc.vector.scalar_tensor_tensor(out_sb[:, qt, :], tiles(abank)[:, qt, :], psums[:, 1, qt:qt + 1],
                                                             xl[:, qt, :], ALU.mult, ALU.add))

                if l1 and not l0:
                    l1_moments(r)
                if l0:
                    v.wait_ge(projected.sem, projected.at(s, 1))
                    rope(0, "g", small[:, EPS1, :], read_g)
                    split_values(T)
                    pick(chained, 0, oh)
                    pick(chained, 1, oh)
                    gate_difference()
                    if l1:
                        l1_moments(r)
                    G, L = len(GLOBAL_UNITS), len(LOCAL_UNITS)
                    for i in range(G):
                        low(i, 12 + i, i % 4, J * P, i in DVE_HIGHS)
                        if i == 1:
                            gate_weights()
                        if i == 4:
                            v.wait_ge(cw_turn.sem, cw_turn.at(s, 1))
                            cwT_sb.inc(nc.vector.tensor_copy(cwT[:, :], misc[0:E + 1, :]))
                        if l1 and 16 <= i < 16 + T:
                            l1_norm(r, [i - 16])
                        for q in range(T - 1):
                            if i == ENDS[q] + 4:
                                divide(q, P)
                            if i == ENDS[q] + 7:
                                oT_copy(q * P, P)
                        if i in COMBINE_G:
                            combine()
                    while yused.n < 12:
                        combine()
                    divide(T - 1, P)
                    oT_copy((T - 1) * P, P)
                    v.wait_ge(attn.sem, attn.at(s, 1))
                    v.wait_ge(yused.sem, yused.at(s, 12))
                    vec.inc(nc.vector.tensor_tensor(x1[:, :, :], xn[:, :, :], tiles(abank), ALU.add))
                    v.wait_ge(vec.sem, vec.at(s, vec.n))
                    attn_used.inc(nc.vector.tensor_tensor(acc[:, :, :], acc[:, :, :], tiles(abank), ALU.add))
                    moments(s, vec, x1)
                    chained(nc.vector.tensor_tensor(small[:, SQ, :], mv[:, :, 0], mv[:, :, 0], ALU.mult))
                    pow_in.inc(nc.vector.scalar_tensor_tensor(small[:, MS2, :], small[:, SQ, :], 1e-6, mv[:, :, 1], ALU.add, ALU.add))
                    v.wait_ge(pow_out.sem, pow_out.at(s, 1))
                    for t in range(T):
                        normed2.inc(nc.vector.tensor_scalar(y2[:, t, :], x1[:, t, :], small[:, R2, t:t + 1], None, ALU.mult))
                    v.wait_ge(projected.sem, projected.at(s, 2))
                    rope(1, "l", None, read_l)
                    split_values(len(LOCAL))
                    for _ in range(EARLY):
                        combine()
                    for i, (b, g) in enumerate(LOCAL_UNITS):
                        q0, nq, k0 = LOCAL[b]
                        low(G + i, 12 + G + 12 + i, i % 4, J * nq, G + i in DVE_HIGHS)
                        if b and g == 3:
                            divide(b - 1, LOCAL[b - 1][1])
                        if b >= 2 and g == 1:
                            oT_copy(*LOCAL[b - 2][0:2])
                        if i in COMBINE_L:
                            combine()
                        if l1 and i == 8:
                            l1_logits()
                        if l1 and i == 12:
                            pick(chained1, 0, oh1)
                        if l1 and i == 14:
                            pick(chained1, 1, oh1)
                        if l1 and i == 16:
                            l1_counts()
                    while yused.n < 24:
                        combine()
                    oT_copy(*LOCAL[-2][0:2])
                    divide(len(LOCAL) - 1, LOCAL[-1][1])
                    oT_copy(*LOCAL[-1][0:2])
                    if l1:
                        l1_rotate(0)
                    v.wait_ge(attn.sem, attn.at(s, 2))
                    v.wait_ge(yused.sem, yused.at(s, 24))
                    attn_used.inc(nc.vector.tensor_tensor(acc[:, :, :], acc[:, :, :], tiles(abank), ALU.add))
                    v.wait_ge(attn_used.sem, attn_used.at(s, 2))

                def some(k):
                    for _ in range(k if l0 else 0):
                        combine()
                if l1 and not l0:
                    l1_norm(r, range(T))
                    l1_logits()
                    pick(chained1, 0, oh1)
                    pick(chained1, 1, oh1)
                    l1_counts()
                    l1_rotate(0)
                if l1:
                    l1_rank_copy()
                if l0:
                    layer_moments(s + 1)
                if l1:
                    l1_rotate(1)
                    peak(0)
                    peak(1)
                if l0:
                    layer_norm(s + 1)
                if l1:
                    some(1)
                    probs_copy(0)
                    peak(2)
                    some(1)
                    probs_copy(1)
                    finish(0)
                    peak(3)
                    l1_slots()
                    some(2)
                    finish(1)
                    probs_copy(2)
                    some(2)
                    finish(2)
                    probs_copy(3)
                    some(2)
                    finish(3)
                if l0:
                    while yused.n < 36:
                        combine()
                    v.wait_ge(yused.sem, yused.at(s, 36))
                    if l1:
                        v.wait_ge(l_out.sem, l_out.at(r, T))
                    xl_ready.inc(nc.vector.tensor_copy(xl[:, :, :], acc[:, :, :]))
                    v.wait_ge(xl_ready.sem, xl_ready.at(s, 1))
                assert not l0 or vec.n == VEC_STEPS, vec.n
                assert not l1 or l_vec.n == L_STEPS, l_vec.n
            layer_moments(0)
            layer_norm(0)
            assert ln.n == LN_STEPS, ln.n
            sequences(v, body)

            v.wait_ge(table_in, 16)
            nc.vector.tensor_scalar(tclip[:, :], table[:, :, 0], float(tokens - 1), None, ALU.min).then_inc(e_vec, 1)
            nc.vector.tensor_copy(add_at[:, :], table[:, :, 0]).then_inc(e_vec, 1)
            v.wait_ge(e_vec, 2)
            nc.vector.tensor_copy(gather_at[:, :], tclip[:, :]).then_inc(e_index, 1)
            def gate(e):
                v.wait_ge(e_turned, e + 1)
                if e >= 2:
                    v.wait_ge(e_hidden, e - 1)
                nc.vector.tensor_copy(xgT[:, e % 2, :], bank[e % 2][:, 0:CAP]).then_inc(e_turned_sb, 1)

            def product(e):
                v.wait_ge(e_sig, e + 1)
                flat = lambda z: z[:, e % 2, :, :].rearrange("p c n -> p (c n)")
                nc.vector.tensor_tensor(flat(sig), bank[4 + e % 2][:, :], flat(sig), ALU.mult).then_inc(e_vec, 1)
                v.wait_ge(e_vec, 3 + e)
                if e >= 2:
                    v.wait_ge(e_y, e - 1)
                nc.vector.tensor_tensor(flat(gT), bank[2 + e % 2][:, :], flat(sig), ALU.mult).then_inc(e_gated, 1)

            def weigh(e):
                v.wait_ge(e_y, e + 1)
                for c in range(CC):
                    ins = nc.vector.tensor_scalar(yo[:, CC * e + c, :], bank[6 + e % 2][:, c * P:(c + 1) * P], table[:, CC * e + c, 1:2], None, ALU.mult)
                ins.then_inc(e_yo, 1)
            gate(0)
            for e in range(E):
                if e + 1 < E:
                    gate(e + 1)
                product(e)
                weigh(e)

        @block.tensor
        def _(pe):
            pe.wait_ge(weights_in, FIRST_LOADS * 16)
            nc.tensor.transpose(bank[0][0:LAT, 0:P], kv_down[:, :], ident).then_inc(setup_pe, 1)
            pe.wait_ge(setup_dve, SETUP_A)
            nc.tensor.matmul(bank[1][:, 0:64], kv_downT[:, :], kv_up[:, :], start=True, stop=True).then_inc(setup_pe, 1)
            for i in range(3):
                nc.tensor.transpose(bank[2 + i][:, 0:P], l1_raw[:, i, :], ident).then_inc(setup_pe, 1)
            pe.wait_ge(setup_dve, SETUP_B)

            def body(s, l0, l1):
                r = s - 1

                def turn(i, src, sig):
                    for t in range(T):
                        pe.wait_ge(sig.sem, sig.at(s, t + 1))
                        ins = nc.tensor.transpose(misc[:, t * P:(t + 1) * P], src[:, t, :], ident)
                    turned.inc(ins)
                    pe.wait_ge(turned_sb.sem, turned_sb.at(s, i + 1))

                def turn_heads(i, uses):
                    pe.wait_ge(evac.sem, evac.at(s, uses))
                    for t in range(T):
                        if t % 2 == 0:
                            pe.wait_ge(stacked.sem, stacked.at(s, 2 * i + t // 2 + 1))
                        if t == T - 1:
                            pe.wait_ge(heads.sem, heads.at(s, T * i + 1))
                        for b in range(J + 1):
                            ins = nc.tensor.transpose(as16(ring[t % 3])[:, b, :],
                                                      stack[:, t, b * KVH:(b + 1) * KVH, :, :].rearrange("p g s d -> p (g s d)"),
                                                      ident16[:, :])
                        stackT.inc(ins)
                    pe.wait_ge(heads.sem, heads.at(s, T * (i + 1)))

                hidden_at = []
                chunks = [0]

                def hidden(n):
                    for _ in range(n):
                        k, c = chunks[0] // HC, chunks[0] % HC
                        chunks[0] += 1
                        use = filled.n
                        if use >= 3:
                            pe.wait_ge(evac.sem, evac.at(s, use - 2))
                        e = sum(EXPERTS, [])[k]
                        if chunks[0] == 1:
                            pe.wait_ge(xn_lo.sem, xn_lo.at(s, 1))
                        for w, xh in ((w1_hi, xnT_hi), (w1_lo, xnT_hi), (w1_hi, xnT_lo)):
                            ins = nc.tensor.matmul(ring[use % 3][:, :], w[:, e, c * P:(c + 1) * P], xh[:, :], start=(w is w1_hi and xh is xnT_hi), stop=(xh is xnT_lo))
                        filled.inc(ins)
                        if c == HC - 1:
                            hidden_at.append(filled.n)

                def second_half(h, early=False):
                    k = ypsum.n
                    t, n = k % T, k // T
                    e = sum(EXPERTS, [])[n]
                    if early and t == 0 and h == 0:
                        pe.wait_ge(squared.sem, squared.at(s, 2 * (k // (3 * T)) + 2))
                    if k == 0 and h == 0 and isinstance(s, int):
                        pe.wait_ge(w2_in, SECOND_LOADS * 16)
                    if t == 0 and h == 0:
                        pe.wait_ge(evac.sem, evac.at(s, hidden_at[n]))
                    if h == 0 and k and not (early and t):
                        pe.wait_ge(yused.sem, yused.at(s, k - 1 if k > 6 * T + 1 else k))
                    if e == E and t == 0 and h == 0:
                        pe.wait_ge(cwT_sb.sem, cwT_sb.at(s, 1))
                    y = yslot(k)
                    for c in (0, 1) if h == 0 else (2, 3):
                        ins = nc.tensor.matmul(y, hidT[:, n % 3, c, t * P:(t + 1) * P], w2[:, e, c, :],
                                               start=(c == 0), stop=(c == HC - 1 and e != E))
                    if h:
                        if e == E:
                            ins = nc.tensor.matmul(y, cwT[:, t * P:(t + 1) * P], b2[:, :], start=False, stop=True)
                        ypsum.inc(ins)

                def second(early=False):
                    second_half(0, early)
                    second_half(1, early)

                def keep_warm(n, b=misc):
                    for _ in range(n):
                        nc.tensor.matmul(b[:, :], ident16[:, :], masks16[:, 0, :].unsqueeze(1).to_broadcast([P, J, P]), start=True, stop=True)

                def scores(g, k_off, q0, nq, mask):
                    use = filled.n
                    pe.wait_ge(evac.sem, evac.at(s, use - 2))
                    dst = ring[use % 3][:, 0:J * nq]
                    if mask:
                        m, at = mask
                        nc.tensor.matmul(dst, ident16[:, :], masks16[:, m, at:at + nq].unsqueeze(1).to_broadcast([P, J, nq]),
                                         start=True, stop=False)
                    rows = slice(32 * g, 32 * g + 32)
                    filled.inc(nc.tensor.matmul(dst, QKT[rows, J, k_off:k_off + P], QKT[rows, 0:J, q0:q0 + nq],
                                                start=not mask, stop=True))

                def values_product(i, slot, g, nq, vblk, blk, first, last):
                    if i in POOL_LOWS:
                        pe.wait_ge(pool_lows.sem, pool_lows.at(s, POOL_LOWS.index(i) + 1))
                    else:
                        pe.wait_ge(lows.sem, lows.at(s, i + 1 - len([k for k in POOL_LOWS if k < i])))
                    dst = obank[blk % 2][VROWS * g:VROWS * (g + 1), 0:J * nq]
                    nc.tensor.matmul(dst, V3[:, vblk, g, :], hi16[:, slot, 0:J * nq], start=first, stop=False)
                    pv.inc(nc.tensor.matmul(dst, V3[:, vblk, g, :], lo16[:, slot, 0:J * nq], start=False, stop=last))

                def sum_parts(blk, nq):
                    if oT_sb.n < osummed.n and osummed.n:
                        pe.wait_ge(oT_sb.sem, oT_sb.at(s, osummed.n))
                    pe.wait_ge(oparts_sb.sem, oparts_sb.at(s, osummed.n + 1))
                    for j in range(J):
                        ins = nc.tensor.matmul(misc[0:nq, j * KVH * VD:(j + 1) * KVH * VD], oparts[:, blk % 2, j * nq:(j + 1) * nq],
                                               const("sum_parts"), start=True, stop=True)
                    osummed.inc(ins)

                def turn_out(blk, q0, nq):
                    pe.wait_ge(otoks.sem, otoks.at(s, oturn.n + 1))
                    o = otok[0:nq, blk % 2, :, :].rearrange("p h d -> p (h d)")
                    if nq > 32:
                        ins = nc.tensor.transpose(misc[:, q0:q0 + nq], o, ident[0:nq, 0:nq])
                    else:
                        ins = nc.tensor.matmul(misc[:, q0:q0 + nq], o, ident[0:nq, 0:nq], start=True, stop=True)
                    oturn.inc(ins)

                def project_out(t, w, upto):
                    pe.wait_ge(oT_sb.sem, oT_sb.at(s, upto))
                    return nc.tensor.matmul(abank[:, t * P:(t + 1) * P], oT[:, t * P:(t + 1) * P], w[:, :], start=True, stop=True)

                def l1_turn():
                    for t in range(T):
                        pe.wait_ge(l_normed.sem, l_normed.at(r, t + 1))
                        ins = nc.tensor.transpose(abank[:, t * P:(t + 1) * P], xn1[:, t, :], ident)
                    l_turned.inc(ins)

                def l1_logits():
                    pe.wait_ge(l_turned_sb.sem, l_turned_sb.at(r, 1))
                    for t in range(T):
                        ins = nc.tensor.matmul(abank[:, t * E:(t + 1) * E], xn1T[:, t * P:(t + 1) * P], router[:, :], start=True, stop=True)
                    l_proj.inc(ins)

                def l1_values():
                    pe.wait_ge(l_lg.sem, l_lg.at(r, 1))
                    for t in range(T):
                        ins = nc.tensor.matmul(abank[:, t * P:(t + 1) * P], xn1T[:, t * P:(t + 1) * P], wv1[:, :], start=True, stop=True)
                    l_proj.inc(ins)

                def l1_project(i):
                    if i == 1:
                        pe.wait_ge(l_ranked.sem, l_ranked.at(r, 1))
                    for h in range(2):
                        ins = nc.tensor.matmul(rot_banks[i][h][:, :], wqk1[:, 2 * i + h, :], xn1T[:, :], start=True, stop=True)
                    l_proj.inc(ins)

                def l1_ranks():
                    pe.wait_ge(l_chosen.sem, l_chosen.at(r, 1))
                    dst = misc[:, 0:T * E]
                    nc.tensor.matmul(dst, const("before"), chosen[:, :, :].rearrange("p t e -> p (t e)"), start=True, stop=False)
                    l_rank.inc(nc.tensor.matmul(dst, const("ones"), before_t[:, 0:T, :].rearrange("p t e -> p (t e)"), start=False, stop=True))

                def l1_scores(qt):
                    n = (qt + 1) * P
                    if qt >= 2:
                        pe.wait_ge(l_exp.sem, l_exp.at(r, qt - 1))
                    l_scores.inc(nc.tensor.matmul(obank[qt % 2][:, 0:n], qk_turned[:, 0, qt * P:(qt + 1) * P], qk_turned[:, 1, 0:n], start=True, stop=True))

                def l1_turn_probs(qt):
                    pe.wait_ge(l_exp.sem, l_exp.at(r, qt + 1))
                    if qt >= 2:
                        pe.wait_ge(l_prT_sb.sem, l_prT_sb.at(r, qt - 1))
                    for k in range(qt + 1):
                        ins = nc.tensor.transpose(ring[qt % 2][:, k * P:(k + 1) * P], pr1[:, qt % 2, k * P:(k + 1) * P], ident)
                    l_prT.inc(ins)

                def l1_pv(qt):
                    pe.wait_ge(l_prT_sb.sem, l_prT_sb.at(r, qt + 1))
                    if qt:
                        pe.wait_ge(l_out.sem, l_out.at(r, qt))
                    for k in range(qt + 1):
                        ins = nc.tensor.matmul(abank[:, qt * P:(qt + 1) * P], prT[:, qt % 2, k, :], v1[:, k, :], start=(k == 0), stop=(k == qt))
                    l_pv.inc(ins)

                if l0:
                    turn(0, xn, normed)
                    if not (isinstance(s, int) and s == 0):
                        pe.wait_ge(xl_ready.sem, xl_ready.at(s, 0))
                    for t in range(T):
                        ins = nc.tensor.matmul(qkv(t, 0, QK + 32 + E), xnT[:, t * P:(t + 1) * P], wg[:, :], start=True, stop=True)
                    projected.inc(ins)
                    hidden(3 * HC)
                    for _ in range(EARLY):
                        second(early=True)
                    turn_heads(0, 12)
                    keep_warm(4)
                    pe.wait_ge(values.sem, values.at(s, 1))
                    U = GLOBAL_UNITS

                    def scores_g(i):
                        qt, g, kt = U[i]
                        scores(g, kt * P, qt * P, P, (0, 0) if kt == qt else None)
                    scores_g(0)
                    scores_g(1)
                    for i, (qt, g, kt) in enumerate(U):
                        if i + 2 < len(U):
                            scores_g(i + 2)
                        if i in SECOND_G:
                            second_half(SECOND_G.index(i) % 2)
                        if i >= 5 and (qt == 0 or i > ENDS[qt - 1] + 3):
                            keep_warm(1, obank[(qt + 1) % 2])
                        first = g == 0 and kt == 0
                        if first and qt >= 2:
                            pe.wait_ge(oparts_sb.sem, oparts_sb.at(s, qt - 1))
                        values_product(i, i % 4, g, P, kt, qt, kt == 0, kt == qt)
                        if i == 3:
                            pe.wait_ge(cw_ready.sem, cw_ready.at(s, 1))
                            for t in range(T):
                                ins = nc.tensor.matmul(misc[0:E + 1, t * P:(t + 1) * P], cw[:, t, :], ident, start=True, stop=True)
                            cw_turn.inc(ins)
                        for q in range(T - 1):
                            if i == ENDS[q] + 3:
                                sum_parts(q, P)
                            if i == ENDS[q] + 6:
                                turn_out(q, q * P, P)
                            if i == ENDS[q] + 9:
                                project_out(q, wo_g, q + 1)
                    while ypsum.n < 12:
                        second()
                    sum_parts(T - 1, P)
                    turn_out(T - 1, (T - 1) * P, P)
                    attn.inc(project_out(T - 1, wo_g, T))
                    hidden(HC)
                    keep_warm(4)
                    turn(1, y2, normed2)
                    pe.wait_ge(attn_used.sem, attn_used.at(s, 1))
                    pe.wait_ge(yused.sem, yused.at(s, 12))
                    for t in range(T):
                        nc.tensor.matmul(qkv(t, 0, QK), y2T[:, t * P:(t + 1) * P], wl[:, 0:QK], start=True, stop=True)
                    for b, (q0, nq, k0) in enumerate(LOCAL):
                        ins = nc.tensor.matmul(misc[:, b * 32:(b + 1) * 32], y2T[:, k0:k0 + P], wl[:, QK:QK + 32], start=True, stop=True)
                    projected.inc(ins)
                    hidden(2 * HC)
                    for _ in range(EARLY):
                        second(early=True)
                    turn_heads(1, 12 + len(U) + 12)
                    keep_warm(4)
                    pe.wait_ge(values.sem, values.at(s, 2))
                    U = LOCAL_UNITS

                    def scores_l(i):
                        b, g = U[i]
                        q0, nq, k0 = LOCAL[b]
                        scores(g, k0, q0, nq, (1, q0 - k0))
                    scores_l(0)
                    scores_l(1)
                    for i, (b, g) in enumerate(U):
                        if i + 2 < len(U):
                            scores_l(i + 2)
                        if i in SECOND_L:
                            second_half(SECOND_L.index(i) % 2)
                        if i < 4:
                            keep_warm(2)
                        q0, nq, k0 = LOCAL[b]
                        if g == 0:
                            pe.wait_ge(oparts_sb.sem, oparts_sb.at(s, T + b - 1))
                        values_product(len(GLOBAL_UNITS) + i, i % 4, g, nq, b, b, True, True)
                        if b and g == 2:
                            sum_parts(b - 1, LOCAL[b - 1][1])
                        if b >= 2 and g == 0:
                            turn_out(b - 2, *LOCAL[b - 2][0:2])
                        if l1 and i == 2:
                            l1_turn()
                        if l1 and i == 6:
                            l1_logits()
                        if l1 and i == 9:
                            l1_values()
                    while ypsum.n < 24:
                        second()
                    turn_out(len(LOCAL) - 2, *LOCAL[-2][0:2])
                    hidden(2)
                    sum_parts(len(LOCAL) - 1, LOCAL[-1][1])
                    if l1:
                        l1_project(0)
                    turn_out(len(LOCAL) - 1, *LOCAL[-1][0:2])
                    if l1:
                        pe.wait_ge(l_v1.sem, l_v1.at(r, 1))
                    for t in range(T):
                        ins = project_out(t, wo_l, T + len(LOCAL))
                    attn.inc(ins)

                def some(k):
                    for _ in range(k if l0 else 0):
                        second()
                if l1 and not l0:
                    l1_turn()
                    l1_logits()
                    l1_values()
                    l1_project(0)
                    pe.wait_ge(l_v1.sem, l_v1.at(r, 1))
                if l1:
                    l1_ranks()
                if l0:
                    hidden(2)
                if l1:
                    if l0:
                        pe.wait_ge(attn_used.sem, attn_used.at(s, 2))
                    l1_project(1)
                if l0:
                    hidden(5)
                if l1:
                    pe.wait_ge(l_rotated.sem, l_rotated.at(r, 2))
                    l1_scores(0)
                    l1_scores(1)
                if l0:
                    hidden(3)
                if l1:
                    some(1)
                    if l0:
                        pe.wait_ge(evac.sem, evac.at(s, RING_USES))
                    l1_turn_probs(0)
                    l1_scores(2)
                    some(1)
                    l1_turn_probs(1)
                    l1_pv(0)
                    l1_scores(3)
                    some(2)
                    l1_pv(1)
                    l1_turn_probs(2)
                    some(2)
                    l1_pv(2)
                    l1_turn_probs(3)
                    some(2)
                    l1_pv(3)
                if l0:
                    if not l1:
                        pe.wait_ge(evac.sem, evac.at(s, RING_USES))
                    while ypsum.n < 36:
                        second()
            sequences(pe, body)

            pe.wait_ge(experts_in, EXPERT_LOADS * 16)
            pe.wait_ge(l_out.sem, l_out.per * seqs)
            def turn_rows(e):
                if e >= 2:
                    pe.wait_ge(e_turned_sb, e - 1)
                pe.wait_ge(e_gathered[e], 16 * CC)
                for c in range(CC):
                    ins = nc.tensor.transpose(bank[e % 2][:, c * P:(c + 1) * P], xg[:, CC * e + c, :], ident)
                ins.then_inc(e_turned, 1)

            def hidden1(e):
                pe.wait_ge(e_turned_sb, e + 1)
                if e >= 2:
                    pe.wait_ge(e_gated, e - 1)
                for w, b in ((w_a, bank[2 + e % 2]), (w_b, bank[4 + e % 2])):
                    for c in range(HC1):
                        ins = nc.tensor.matmul(b[:, c * CAP:(c + 1) * CAP], w[:, e, c * P:(c + 1) * P], xgT[:, e % 2, :], start=True, stop=True)
                ins.then_inc(e_hidden, 1)

            def out1(e):
                pe.wait_ge(e_gated, e + 1)
                if e >= 2:
                    pe.wait_ge(e_yo, e - 1)
                for c in range(CC):
                    for k in range(HC1):
                        ins = nc.tensor.matmul(bank[6 + e % 2][:, c * P:(c + 1) * P], gT[:, e % 2, k, c * P:(c + 1) * P], w_o[:, e, k, :],
                                               start=(k == 0), stop=(k == HC1 - 1))
                ins.then_inc(e_y, 1)
            turn_rows(0)
            hidden1(0)
            for e in range(E):
                if e + 1 < E:
                    turn_rows(e + 1)
                    hidden1(e + 1)
                out1(e)



_INS = ['L0_attn_norm1_w', 'L0_attn_norm2_w', 'L0_attn_g_wq', 'L0_attn_g_kv_down', 'L0_attn_g_k_up',
        'L0_attn_g_v_up', 'L0_attn_g_wo', 'L0_attn_l_wq', 'L0_attn_l_wk', 'L0_attn_l_wv', 'L0_attn_l_wo',
        'L0_ffn_gate_w', 'L0_ffn_gate_b', 'L0_ffn_w1', 'L0_ffn_b1', 'L0_ffn_w2', 'L0_ffn_b2', 'L0_ffn_ws1',
        'L0_ffn_bs1', 'L0_ffn_ws2', 'L0_ffn_bs2', 'L1_attn_w_q', 'L1_attn_w_k', 'L1_attn_w_v',
        'L1_ffn_router_w', 'L1_ffn_router_b', 'L1_ffn_W', 'L1_ffn_V', 'L1_ffn_W_out']


def kernel(**inputs):
    import numpy as _np
    import concourse.bacc as _bacc
    from concourse import mybir as _mybir
    from concourse.bass_utils import run_bass_kernel_spmd as _run

    nc = _bacc.Bacc("TRN2", target_bir_lowering=False, num_devices=1)
    arrays, aps = {}, {}

    def given(name, key, v):
        arrays[name] = v
        aps[key] = nc.dram_tensor(name, v.shape, _mybir.dt.from_np(v.dtype), kind="ExternalInput").ap()
    given("x_dram", "x", _np.ascontiguousarray(inputs["L0_attn_hidden"]))
    given("shape_constants_dram", "shape_constants", shape_constants())
    given("zero_rows_dram", "zero_rows", _np.zeros((SLOTS, D), _np.float32))
    for n in _INS:
        given(f"in_{n}_dram", n, _np.ascontiguousarray(inputs[n]))
    out = nc.dram_tensor("out_0_dram", [TOKENS + SLOTS, D], _mybir.dt.float32, kind="ExternalOutput").ap()
    program(nc, aps, out)
    r = _run(nc, [arrays], core_ids=[0])
    return r.results[0]["out_0_dram"][0:TOKENS].reshape(SEQS, LEN, D)
```
